# Optimizing a Trainium2 kernel written in Bass

```python
import numpy as np
import jax
import jax.numpy as jnp

def _softmax(x, axis=-1):
    return jax.nn.softmax(x, axis=axis)

def _gelu(x):
    return jax.nn.gelu(x, approximate=True)

def _silu(x):
    return jax.nn.silu(x)

def _sigmoid(x):
    return jax.nn.sigmoid(x)

def _layernorm(x, axis=-1, eps=1e-05):
    m = jnp.mean(x, axis=axis, keepdims=True)
    v = jnp.var(x, axis=axis, keepdims=True)
    return (x - m) / jnp.sqrt(v + eps)

def _scatter_add(tgt, idx, src, axis=0):
    return tgt.at[idx].add(src)

def _segment_sum(src, seg, n):
    return jax.ops.segment_sum(src, seg, n)
kernel_name = 'mk_gnn_resnorm_d4_gnn_r8_69deca'

def setup_inputs(seed: int=0):
    np.random.seed(seed)
    _w = jnp.asarray

    def _rec_inputs():
        import jax
        import jax.numpy as jnp
        _gk = jax.random.key(seed)
        x = -0.0001006 + 1 * jax.random.normal(jax.random.fold_in(_gk, 1), (6250, 96), jnp.float32)
        src = jax.random.randint(jax.random.fold_in(_gk, 2), (100000,), 0, 6250, jnp.int32)
        dst = jnp.minimum((6250 * jax.random.uniform(jax.random.fold_in(_gk, 3), (100000,)) ** 2.0).astype(jnp.int32), 49999)
        _o = jnp.argsort(dst, stable=True)
        src = src[_o]
        dst = dst[_o]
        edge_attr_4 = 0.000714719 + 1.00021 * jax.random.normal(jax.random.fold_in(_gk, 12), (100000, 4), jnp.float32)
        return (x, src, dst, edge_attr_4)
    x, src, dst, edge_attr_4 = _rec_inputs()

    def _L0_gnn_setup():
        import jax, jax.numpy as jnp
        import numpy as np
        EPS = 1e-07
        BETA = 1.0
        key = jax.random.key(seed)
        k1, k2, k3, k4 = jax.random.split(key, 4)
        N, E, D_IN, D_OUT = (6250, 100000, 96, 96)
        feat = jax.random.normal(k1, (N, D_IN), dtype=jnp.float32)
        src = jax.random.randint(k2, (E,), 0, N, dtype=jnp.int32)
        dst = jax.random.randint(k3, (E,), 0, N, dtype=jnp.int32)
        W = jax.random.normal(k4, (D_IN, D_OUT), dtype=jnp.float32) / np.sqrt(D_IN)
        b = jnp.zeros((D_OUT,), dtype=jnp.float32)
        return {'feat': feat, 'src': src, 'dst': dst, 'W': W, 'b': b}
    _L0_gnn_all = _L0_gnn_setup()
    _L0_gnn_in = {k: v for k, v in _L0_gnn_all.items() if k in ('W', 'b')}
    del _L0_gnn_all

    def _L1_gnn_setup():
        import jax, jax.numpy as jnp
        import numpy as np
        EPS = 1e-05

        def _mlp(h, W, b, gamma, beta):
            h = jax.nn.relu(h @ W + b)
            mu = jnp.mean(h, axis=0)
            var = jnp.mean(jnp.square(h - mu), axis=0)
            return gamma * (h - mu) * jax.lax.rsqrt(var + EPS) + beta
        key = jax.random.key(seed)
        ks = jax.random.split(key, 10)
        N, E, C_in, C_out, E_dim = (6250, 100000, 96, 96, 4)
        x = jax.random.normal(ks[0], (N, C_in), dtype=jnp.float32)
        edge_index = jax.random.randint(ks[1], (2, E), 0, N, dtype=jnp.int64)
        edge_attr = jax.random.normal(ks[2], (E, E_dim), dtype=jnp.float32)
        s = lambda fan_in: 1.0 / np.sqrt(fan_in)
        W_node = jax.random.uniform(ks[3], (C_in, C_out), jnp.float32, -s(C_in), s(C_in))
        b_node = jnp.zeros((C_out,), jnp.float32)
        g_node = jnp.ones((C_out,), jnp.float32)
        beta_node = jnp.zeros((C_out,), jnp.float32)
        W_edge = jax.random.uniform(ks[4], (E_dim, C_out), jnp.float32, -s(E_dim), s(E_dim))
        b_edge = jnp.zeros((C_out,), jnp.float32)
        g_edge = jnp.ones((C_out,), jnp.float32)
        beta_edge = jnp.zeros((C_out,), jnp.float32)
        M_in = 2 * C_in + C_out
        W_msg = jax.random.uniform(ks[5], (M_in, C_out), jnp.float32, -s(M_in), s(M_in))
        b_msg = jnp.zeros((C_out,), jnp.float32)
        g_msg = jnp.ones((C_out,), jnp.float32)
        beta_msg = jnp.zeros((C_out,), jnp.float32)
        return dict(x=x, edge_index=edge_index, edge_attr=edge_attr, W_node=W_node, b_node=b_node, g_node=g_node, beta_node=beta_node, W_edge=W_edge, b_edge=b_edge, g_edge=g_edge, beta_edge=beta_edge, W_msg=W_msg, b_msg=b_msg, g_msg=g_msg, beta_msg=beta_msg)
    _L1_gnn_all = _L1_gnn_setup()
    _L1_gnn_in = {k: v for k, v in _L1_gnn_all.items() if k in ('W_node', 'b_node', 'g_node', 'beta_node', 'W_edge', 'b_edge', 'g_edge', 'beta_edge', 'W_msg', 'b_msg', 'g_msg', 'beta_msg')}
    del _L1_gnn_all

    def _L2_gnn_setup():
        import jax, jax.numpy as jnp
        import numpy as np
        N = 6250
        E = 100000
        D = 96

        def _mean_aggr(h, src, dst, num_nodes):
            msgs = h[src]
            summed = jax.ops.segment_sum(msgs, dst, num_segments=num_nodes)
            deg = jax.ops.segment_sum(jnp.ones((src.shape[0],), h.dtype), dst, num_segments=num_nodes)
            return summed / jnp.maximum(deg, 1.0)[:, None]

        def _sage_conv(h, src, dst, Wl, bl, Wr, num_nodes):
            agg = _mean_aggr(h, src, dst, num_nodes)
            return agg @ Wl.T + bl + h @ Wr.T
        key = jax.random.key(seed)
        ks = jax.random.split(key, 8)
        s = 1.0 / np.sqrt(D)
        return {'x': jax.random.normal(ks[0], (N, D), dtype=jnp.float32), 'edge_index': jax.random.randint(ks[1], (2, E), 0, N, dtype=jnp.int64), 'Wl1': jax.random.normal(ks[2], (D, D), dtype=jnp.float32) * s, 'bl1': jnp.zeros((D,), dtype=jnp.float32), 'Wr1': jax.random.normal(ks[3], (D, D), dtype=jnp.float32) * s, 'Wl2': jax.random.normal(ks[4], (D, D), dtype=jnp.float32) * s, 'bl2': jnp.zeros((D,), dtype=jnp.float32), 'Wr2': jax.random.normal(ks[5], (D, D), dtype=jnp.float32) * s}
    _L2_gnn_all = _L2_gnn_setup()
    _L2_gnn_in = {k: v for k, v in _L2_gnn_all.items() if k in ('Wl1', 'bl1', 'Wr1', 'Wl2', 'bl2', 'Wr2')}
    del _L2_gnn_all

    def _L3_gnn_setup():
        import jax, jax.numpy as jnp
        import numpy as np
        N_NODES = 6250
        N_EDGES = 100000
        D_IN = 96
        D_HID = 96

        def _sage_conv(x, src, dst, Wl, b, Wr, n_nodes):
            msg = x[src]
            agg = jax.ops.segment_sum(msg, dst, num_segments=n_nodes)
            cnt = jax.ops.segment_sum(jnp.ones((src.shape[0],), x.dtype), dst, num_segments=n_nodes)
            agg = agg / jnp.maximum(cnt, 1.0)[:, None]
            return agg @ Wl.T + b + x @ Wr.T
        key = jax.random.key(seed)
        ks = jax.random.split(key, 8)
        x = jax.random.normal(ks[0], (N_NODES, D_IN), dtype=jnp.float32)
        edge_index = jax.random.randint(ks[1], (2, N_EDGES), 0, N_NODES, dtype=jnp.int64)
        s1 = 1.0 / np.sqrt(D_IN)
        s2 = 1.0 / np.sqrt(D_HID)
        W1l = jax.random.uniform(ks[2], (D_HID, D_IN), jnp.float32, -s1, s1)
        b1 = jax.random.uniform(ks[3], (D_HID,), jnp.float32, -s1, s1)
        W1r = jax.random.uniform(ks[4], (D_HID, D_IN), jnp.float32, -s1, s1)
        W2l = jax.random.uniform(ks[5], (D_HID, D_HID), jnp.float32, -s2, s2)
        b2 = jax.random.uniform(ks[6], (D_HID,), jnp.float32, -s2, s2)
        W2r = jax.random.uniform(ks[7], (D_HID, D_HID), jnp.float32, -s2, s2)
        return {'x': x, 'edge_index': edge_index, 'W1l': W1l, 'b1': b1, 'W1r': W1r, 'W2l': W2l, 'b2': b2, 'W2r': W2r}
    _L3_gnn_all = _L3_gnn_setup()
    _L3_gnn_in = {k: v for k, v in _L3_gnn_all.items() if k in ('W1l', 'b1', 'W1r', 'W2l', 'b2', 'W2r')}
    del _L3_gnn_all
    return {'x': x, 'src': src, 'dst': dst, 'edge_attr_4': edge_attr_4, 'L0_gnn_W': _L0_gnn_in['W'], 'L0_gnn_b': _L0_gnn_in['b'], 'L1_gnn_W_node': _L1_gnn_in['W_node'], 'L1_gnn_b_node': _L1_gnn_in['b_node'], 'L1_gnn_g_node': _L1_gnn_in['g_node'], 'L1_gnn_beta_node': _L1_gnn_in['beta_node'], 'L1_gnn_W_edge': _L1_gnn_in['W_edge'], 'L1_gnn_b_edge': _L1_gnn_in['b_edge'], 'L1_gnn_g_edge': _L1_gnn_in['g_edge'], 'L1_gnn_beta_edge': _L1_gnn_in['beta_edge'], 'L1_gnn_W_msg': _L1_gnn_in['W_msg'], 'L1_gnn_b_msg': _L1_gnn_in['b_msg'], 'L1_gnn_g_msg': _L1_gnn_in['g_msg'], 'L1_gnn_beta_msg': _L1_gnn_in['beta_msg'], 'L2_gnn_Wl1': _L2_gnn_in['Wl1'], 'L2_gnn_bl1': _L2_gnn_in['bl1'], 'L2_gnn_Wr1': _L2_gnn_in['Wr1'], 'L2_gnn_Wl2': _L2_gnn_in['Wl2'], 'L2_gnn_bl2': _L2_gnn_in['bl2'], 'L2_gnn_Wr2': _L2_gnn_in['Wr2'], 'L3_gnn_W1l': _L3_gnn_in['W1l'], 'L3_gnn_b1': _L3_gnn_in['b1'], 'L3_gnn_W1r': _L3_gnn_in['W1r'], 'L3_gnn_W2l': _L3_gnn_in['W2l'], 'L3_gnn_b2': _L3_gnn_in['b2'], 'L3_gnn_W2r': _L3_gnn_in['W2r']}

def reference(x, src, dst, edge_attr_4, L0_gnn_W, L0_gnn_b, L1_gnn_W_node, L1_gnn_b_node, L1_gnn_g_node, L1_gnn_beta_node, L1_gnn_W_edge, L1_gnn_b_edge, L1_gnn_g_edge, L1_gnn_beta_edge, L1_gnn_W_msg, L1_gnn_b_msg, L1_gnn_g_msg, L1_gnn_beta_msg, L2_gnn_Wl1, L2_gnn_bl1, L2_gnn_Wr1, L2_gnn_Wl2, L2_gnn_bl2, L2_gnn_Wr2, L3_gnn_W1l, L3_gnn_b1, L3_gnn_W1r, L3_gnn_W2l, L3_gnn_b2, L3_gnn_W2r):
    import jax
    import jax.numpy as jnp

    def _L0_gnn_ref(feat, src, dst, W, b):
        import jax, jax.numpy as jnp
        import numpy as np
        EPS = 1e-07
        BETA = 1.0
        N = feat.shape[0]
        m = jax.nn.relu(feat[src]) + EPS
        logits = BETA * m
        seg_max = jax.ops.segment_max(logits, dst, num_segments=N)
        ex = jnp.exp(logits - seg_max[dst])
        denom = jax.ops.segment_sum(ex, dst, num_segments=N)
        a = ex / denom[dst]
        msg = jax.ops.segment_sum(a * m, dst, num_segments=N)
        feats = feat + msg
        return feats @ W + b

    def _L1_gnn_ref(x, edge_index, edge_attr, W_node, b_node, g_node, beta_node, W_edge, b_edge, g_edge, beta_edge, W_msg, b_msg, g_msg, beta_msg):
        import jax, jax.numpy as jnp
        import numpy as np
        EPS = 1e-05

        def _mlp(h, W, b, gamma, beta):
            h = jax.nn.relu(h @ W + b)
            mu = jnp.mean(h, axis=0)
            var = jnp.mean(jnp.square(h - mu), axis=0)
            return gamma * (h - mu) * jax.lax.rsqrt(var + EPS) + beta
        node_feat = _mlp(x, W_node, b_node, g_node, beta_node)
        edge_feat = _mlp(edge_attr, W_edge, b_edge, g_edge, beta_edge)
        row, col = (edge_index[0], edge_index[1])
        message = jnp.concatenate([x[row], x[col], edge_feat], axis=1)
        message = _mlp(message, W_msg, b_msg, g_msg, beta_msg)
        agg = jax.ops.segment_sum(message, col, num_segments=node_feat.shape[0])
        return agg + node_feat

    def _L2_gnn_ref(x, edge_index, Wl1, bl1, Wr1, Wl2, bl2, Wr2):
        import jax, jax.numpy as jnp
        import numpy as np
        N = 6250
        E = 100000
        D = 96

        def _mean_aggr(h, src, dst, num_nodes):
            msgs = h[src]
            summed = jax.ops.segment_sum(msgs, dst, num_segments=num_nodes)
            deg = jax.ops.segment_sum(jnp.ones((src.shape[0],), h.dtype), dst, num_segments=num_nodes)
            return summed / jnp.maximum(deg, 1.0)[:, None]

        def _sage_conv(h, src, dst, Wl, bl, Wr, num_nodes):
            agg = _mean_aggr(h, src, dst, num_nodes)
            return agg @ Wl.T + bl + h @ Wr.T
        src, dst = (edge_index[0], edge_index[1])
        n = x.shape[0]
        h = _sage_conv(x, src, dst, Wl1, bl1, Wr1, n)
        h = jax.nn.relu(h)
        h = _sage_conv(h, src, dst, Wl2, bl2, Wr2, n)
        return h

    def _L3_gnn_ref(x, edge_index, W1l, b1, W1r, W2l, b2, W2r):
        import jax, jax.numpy as jnp
        import numpy as np
        N_NODES = 6250
        N_EDGES = 100000
        D_IN = 96
        D_HID = 96

        def _sage_conv(x, src, dst, Wl, b, Wr, n_nodes):
            msg = x[src]
            agg = jax.ops.segment_sum(msg, dst, num_segments=n_nodes)
            cnt = jax.ops.segment_sum(jnp.ones((src.shape[0],), x.dtype), dst, num_segments=n_nodes)
            agg = agg / jnp.maximum(cnt, 1.0)[:, None]
            return agg @ Wl.T + b + x @ Wr.T
        src, dst = (edge_index[0], edge_index[1])
        n = x.shape[0]
        h = _sage_conv(x, src, dst, W1l, b1, W1r, n)
        h = jax.nn.elu(h)
        h = _sage_conv(h, src, dst, W2l, b2, W2r, n)
        return h
    edge_index = jnp.stack([src, dst])
    x = _layernorm(x + _L0_gnn_ref(x, src, dst, L0_gnn_W, L0_gnn_b), axis=-1)
    x = _layernorm(x + _L1_gnn_ref(x, edge_index, edge_attr_4, L1_gnn_W_node, L1_gnn_b_node, L1_gnn_g_node, L1_gnn_beta_node, L1_gnn_W_edge, L1_gnn_b_edge, L1_gnn_g_edge, L1_gnn_beta_edge, L1_gnn_W_msg, L1_gnn_b_msg, L1_gnn_g_msg, L1_gnn_beta_msg), axis=-1)
    x = _layernorm(x + _L2_gnn_ref(x, edge_index, L2_gnn_Wl1, L2_gnn_bl1, L2_gnn_Wr1, L2_gnn_Wl2, L2_gnn_bl2, L2_gnn_Wr2), axis=-1)
    x = _layernorm(x + _L3_gnn_ref(x, edge_index, L3_gnn_W1l, L3_gnn_b1, L3_gnn_W1r, L3_gnn_W2l, L3_gnn_b2, L3_gnn_W2r), axis=-1)
    return x

_drawn_inputs = setup_inputs


def setup_inputs(seed=0):
    import zlib

    import numpy as np

    out = dict(_drawn_inputs(seed))
    spreads = {'L0_gnn_b': (0.0, 0.332),
     'L1_gnn_b_node': (0.0, 0.416),
     'L1_gnn_g_node': (1.0, 0.544),
     'L1_gnn_beta_node': (0.0, 0.488),
     'L1_gnn_b_edge': (0.0, 0.1),
     'L1_gnn_g_edge': (1.0, 0.2),
     'L1_gnn_beta_edge': (0.0, 0.353),
     'L1_gnn_b_msg': (0.0, 0.1),
     'L1_gnn_g_msg': (1.0, 0.2),
     'L1_gnn_beta_msg': (0.0, 0.1),
     'L2_gnn_bl1': (0.0, 0.1),
     'L2_gnn_bl2': (0.0, 0.1)}
    factors = {}
    for name, (base, spread) in spreads.items():
        noise = np.random.default_rng([zlib.crc32(name.encode()), seed]).standard_normal(out[name].shape)
        drawn = base * np.exp(spread * noise) if base else spread * noise
        out[name] = jnp.asarray(drawn.astype(out[name].dtype))
    for name, factor in factors.items():
        out[name] = (out[name] * factor).astype(out[name].dtype)
    return out
```

```python
import math
from contextlib import ExitStack

import numpy as np

import concourse.bass as bass
from concourse import mybir

P = 128
F = 96
CH = 4
TE = CH * P
RING = 4
GT = 7
GC = GT * P
EDGE_DIM = 4
MSG_EPS = 1e-7
EPS = 1e-5
BIG = 1e38
HC = 8

MATRICES = ["W0", "W_node", "W_src", "W_dst", "W_ef", "W2l1", "W2r1", "W2l2", "W2r2", "W3l1", "W3r1", "W3l2", "W3r2"]
ROWS = ["b0", "b21", "b22", "b31", "b32"]
COLUMNS = ["b_node", "g_node", "beta_node", "b_edge", "g_edge", "beta_edge", "b_msg", "g_msg", "beta_msg"]

SOFT, MESSAGE, MEAN = range(3)
PASSES = [SOFT, MESSAGE, MEAN, MEAN, MEAN, MEAN]


def edge_tiles(n_edges):
    return RING * math.ceil(n_edges / (TE * RING))


def node_tiles(n_nodes):
    return GT * math.ceil(n_nodes / (P * GT))


def wait(eng, semaphore, value):
    if not (isinstance(value, int) and value <= 0):
        eng.wait_ge(semaphore, value)


class Chain:

    def __init__(self, eng, semaphore):
        self.eng, self.semaphore, self.base, self.n = eng, semaphore, 0, 0

    def do(self, instruction):
        self.n += 1
        instruction.then_inc(self.semaphore, 1)
        self.eng.wait_ge(self.semaphore, self.base + self.n)


def build(nc, n_edges, x_in, src_in, dst_in, dst_cols_in, dst_seq_in, attr_in, w_edge_in, matrices_in, rows_in,
          columns_in, out):
    dt = mybir.dt
    f32, i32, i8, bf16 = dt.float32, dt.int32, dt.int8, dt.bfloat16
    ALU = mybir.AluOpType
    ACT = mybir.ActivationFunctionType
    X = mybir.AxisListType.X

    n_nodes = x_in.shape[0]
    ET = edge_tiles(n_edges)
    EI = ET // RING
    EP = ET * TE
    NT = node_tiles(n_nodes)
    NG = NT // GT
    NP = NT * P
    FULL = n_nodes // P
    REST = n_nodes - FULL * P
    SEQ = EP // P
    HI = SEQ // HC // 2

    ctx = ExitStack()
    with ctx:
        def sb(name, shape, t=f32):
            return ctx.enter_context(nc.sbuf_tensor(name, shape, t))

        def dram(name, shape, t=f32):
            return nc.dram_tensor(name, shape, t, kind="Internal").ap()

        def sem(name):
            return ctx.enter_context(nc.semaphore(name))

        def ring_sems(name):
            return [sem(f"{name}{s}") for s in range(RING)]

        def sems(suffix, names):
            return {n: sem(f"{n}_{suffix}") for n in names.split()}

        relu_table = dram("relu_table", [NP, F])
        src_table = dram("src_table", [NP, F])
        dst_table = dram("dst_table", [NP, F])
        x_table = dram("x_table", [NP, F])
        h_table = dram("h_table", [NP, F])
        flag_dram = dram("flag_dram", [EP], i8)
        sign_dram = dram("sign_dram", [EP], i8)
        soft_sums = dram("soft_sums", [EP, 2 * F])
        sums = dram("sums", [EP, F])
        soft_sums_t = soft_sums.rearrange("(t p c) f -> t p (c f)", p=P, c=CH)
        sums_t = sums.rearrange("(t p c) f -> t p (c f)", p=P, c=CH)
        flag_t = [d.rearrange("(t e) -> t e", e=TE) for d in (sign_dram, flag_dram, flag_dram, flag_dram,
                                                              flag_dram, flag_dram)]

        def node_rows(table, g):
            return table.rearrange("(k p) f -> p k f", p=P)[:, bass.ds(g * GT, GT), :]

        gather_table = [relu_table, src_table, x_table, h_table, x_table, h_table]
        next_table = [None, x_table, h_table, x_table, h_table, None]

        ident = sb("ident", [P, P])
        ones = sb("ones", [P, P])
        W = {n: sb(f"m_{n}", [F, F]) for n in MATRICES}
        row = {n: sb(f"r_{n}", [1, F]) for n in ROWS}
        col = {n: sb(f"c_{n}", [F, 1]) for n in COLUMNS}
        w_edge = sb("w_edge", [EDGE_DIM, F])
        w_ef_scaled = sb("w_ef_scaled", [F, F])

        x_sb = sb("x_sb", [P, NT, F])
        hidden = sb("hidden", [P, NP])
        h_sb = hidden[:, 0:NT * F].rearrange("p (k f) -> p k f", f=F)
        node_feat = hidden[0:F, :]
        end_row = sb("end_row", [P, NT], i32)
        deg, has, rdeg = sb("deg", [P, NT]), sb("has", [P, NT]), sb("rdeg", [P, NT])

        def of_group(t, g):
            return t[:, bass.ds(g * GT, GT)]

        area = sb("area", [P, max(NT * 2 * F, 2 * RING * (TE + CH * F))])
        ends = area[:, 0:NT * 2 * F].rearrange("p (k f) -> p k f", f=2 * F)

        def parts_of(tensor):
            used = [0]

            def part(parts, width):
                used[0] += width
                assert used[0] <= tensor.shape[1], (used[0], tensor.shape)
                return tensor[0:parts, used[0] - width:used[0]]
            return part

        ring = parts_of(area)
        src_rows = ring(P, RING * CH * F).rearrange("p (s c f) -> p s c f", s=RING, c=CH)
        sum_ring = ring(F, RING * TE)
        num_ring = ring(F, RING * TE)
        dst_rows = ring(P, RING * CH * F).rearrange("p (s c f) -> p s c f", s=RING, c=CH)
        out_ring = sb("out_ring", [P, RING, CH, 2 * F])
        idx_src = [sb(f"idx_src{s}", [P, CH], i32) for s in range(RING)]
        idx_dst = [sb(f"idx_dst{s}", [P, CH], i32) for s in range(RING)]
        flags = sb("flags", [F, RING, TE], i8)
        attr = sb("attr", [EDGE_DIM, RING, TE])
        dump = sb("dump", [F, GC])
        relu_dump = sb("relu_dump", [F, TE])

        second = sb("second", [P, 7680])
        soft = parts_of(second)
        max_ring = soft(F, 1 + RING * TE)
        decay = soft(F, 2 * TE).rearrange("p (b e) -> p b e", b=2)
        weight = soft(F, 2 * TE).rearrange("p (b e) -> p b e", b=2)
        weighted = soft(F, 2 * TE).rearrange("p (b e) -> p b e", b=2)
        message = parts_of(second)
        h_ring = message(F, 2 * TE).rearrange("p (b e) -> p b e", b=2)
        msg_ring = message(F, RING * TE).rearrange("p (b e) -> p b e", b=RING)
        nodes = parts_of(second)
        grp, xg, res, sq, ng, dg = [nodes(P, GT * F).rearrange("p (k f) -> p k f", f=F) for _ in range(6)]
        fa, fx = nodes(F, GC), nodes(F, GC)

        first = parts_of(area)
        seq_now, seq_before, seq_int = [first(P, SEQ).bitcast(i32) for _ in range(3)]
        cols_lo, cols_hi = first(P, SEQ), first(P, SEQ)
        iota_lo, iota_hi = first(P, P), first(P, NT)
        tri = first(P, P)
        flag8 = sb("flag8", [P, 2, SEQ], i8)
        hot_lo = sb("hot_lo", [P, 2, HC, P], bf16)
        hot_hi = sb("hot_hi", [P, 2, HC, NT], bf16)
        end_f, end_i, end_j = sb("end_f", [P, NT]), sb("end_i", [P, NT], i32), sb("end_j", [P, NT], i32)
        total, before = sb("total", [P, NT]), sb("before", [P, NT])

        ef_sum, ef_sq = sb("ef_sum", [F, ET]), sb("ef_sq", [F, ET])
        mg_sum, mg_sq = sb("mg_sum", [F, ET]), sb("mg_sq", [F, ET])
        nd_sum, nd_sq = sb("nd_sum", [F, NG]), sb("nd_sq", [F, NG])
        mu, var, tmp = sb("mu", [F, 1]), sb("var", [F, 1]), sb("tmp", [F, 1])
        s_ef, t_ef = sb("s_ef", [F, 1]), sb("t_ef", [F, 1])
        s_nd, t_nd = sb("s_nd", [F, 1]), sb("t_nd", [F, 1])
        s_mg, t_mg = sb("s_mg", [F, 1]), sb("t_mg", [F, 1])
        msg_bias = sb("msg_bias", [F, 1])
        diag_s, diag_t = sb("diag_s", [F, F]), sb("diag_t", [F, F])
        s_row, t_row = sb("s_row", [P, F]), sb("t_row", [P, F])
        eps = sb("eps", [P, 1])
        mean, rstd = sb("mean", [P, GT]), sb("rstd", [P, GT])

        ps = ctx.enter_context(nc.psum_tensor("ps", [P, 8, 512], f32))

        def bank(b, parts=P, width=512):
            return ps[0:parts, b, 0:width]

        def node_major(b):
            return ps[:, b:b + 2, :].rearrange("p b (k n) -> p (b k) n", n=P)

        def feature_major(b):
            return ps[0:F, b:b + 2, :].rearrange("p b n -> p (b n)")[:, 0:GC]

        weights_landed, x_landed = sem("weights_landed"), sem("x_landed")
        cols_landed, seq_landed = sem("cols_landed"), sem("seq_landed")
        pool_step, consts_made = sem("pool_step"), sem("consts_made")
        dve_step = sem("dve_step")
        flag_made, flag_stored = sem("flag_made"), sem("flag_stored")
        hot_made, hot_used, deg_counted, deg_made, prefix_summed = (
            sem("hot_made"), sem("hot_used"), sem("deg_counted"), sem("deg_made"), sem("prefix_summed"))
        index_made, relu_made, relu_stored = sem("index_made"), sem("relu_made"), sem("relu_stored")
        ef_coefs_made, ef_bias_summed, msg_bias_made = sem("ef_coefs_made"), sem("ef_bias_summed"), sem("msg_bias_made")
        diags_made, rows_spread = sem("diags_made"), sem("rows_spread")
        idx_landed, idx_dst_landed, flags_landed = ring_sems("idx_landed"), ring_sems("idx_dst_landed"), ring_sems("flags_landed")
        attr_landed = ring_sems("attr_landed")
        src_gathered, dst_gathered = ring_sems("src_gathered"), ring_sems("dst_gathered")
        sums_stored = ring_sems("sums_stored")
        ends_landed = [sem(f"ends_landed{g}") for g in range(NG)]
        ends_ready = sem("ends_ready")
        var_summed, rooted = sem("var_summed"), sem("rooted")
        coef_var_made, coef_rooted = sem("coef_var_made"), sem("coef_rooted")
        gathers_begun = sem("gathers_begun")
        out_stored = sem("out_stored")
        EDGE = "turned summed back copied"
        edge = [sems(f"e{p}", EDGE + {SOFT: " hid hrelu squared maxed masked scored expd weighed wrapped",
                                      MESSAGE: " hid hrelu squared relued"}.get(kind, ""))
                for p, kind in enumerate(PASSES)]
        node = [sems(f"n{p}", "copied mixed normed stored" + (" kept" if p < len(PASSES) - 1 else "")
                     + {SOFT: " prepared turned turned2 copied2 src_made src_kept dst_made dst_kept dst_stored nh_made"
                              " nh_kept nh_squared",
                        MEAN: " prepared turned xcopied"}.get(kind, "") + (" floored expd" if p == 4 else ""))
                for p, kind in enumerate(PASSES)]

        def over_tiles(eng, lead, lag=None):
            lead(0, 0)
            for s in range(RING):
                lead((s + 1) // RING, (s + 1) % RING)
                if lag:
                    lag(0, s)
            with eng.Fori(1, EI - 1) as u:
                for s in range(RING):
                    lead(u + (s + 1) // RING, (s + 1) % RING)
                    if lag:
                        lag(u, s)
            for s in range(RING):
                if s + 1 < RING:
                    lead(EI - 1, s + 1)
                if lag:
                    lag(EI - 1, s)

        def tile_before(step, u, s):
            if s:
                step(u, s - 1)
            elif not isinstance(u, int) or u:
                step(u - 1, RING - 1)

        def over_groups(eng, lead, lag, chain=None, steps=0):
            lead(0)
            lead(1)
            lag(0)
            start = chain.base + chain.n - steps if chain else 0
            with eng.Fori(1, NG - 1) as g:
                if chain:
                    chain.base, chain.n = g * steps + start, 0
                lead(g + 1)
                lag(g)
                assert not chain or chain.n == steps, chain.n
            if chain:
                chain.base, chain.n = start + steps * (NG - 1), 0
            lag(NG - 1)

        def wait_for_tables(eng, p):
            if p:
                eng.wait_ge(node[p - 1]["stored"], 16 * NG)
            if PASSES[p] == MESSAGE:
                eng.wait_ge(node[p - 1]["dst_stored"], 16 * NG)

        def norms_before(p):
            return NG * {0: 0, 1: 1, 3: 2, 5: 3}[p]

        def nothing(*where):
            pass

        block = ctx.enter_context(nc.Block())

        @block.sync
        def _(sp):
            sp.dma_start(x_sb[:, 0:FULL, :], x_in[0:FULL * P, :].rearrange("(k p) f -> p k f", p=P)).then_inc(x_landed, 16)
            sp.wait_ge(consts_made, 1)
            sp.dma_start(x_sb[0:REST, FULL, :], x_in[FULL * P:n_nodes, :]).then_inc(x_landed, 16)
            sp.dma_start(seq_now, dst_seq_in[1:1 + EP].rearrange("(p j) -> p j", p=P)).then_inc(seq_landed, 16)
            sp.dma_start(seq_before, dst_seq_in[0:EP].rearrange("(p j) -> p j", p=P)).then_inc(seq_landed, 16)
            sp.dma_start(seq_int, dst_cols_in).then_inc(cols_landed, 16)
            sp.dma_start(w_edge[:, :], w_edge_in).then_inc(weights_landed, 16)
            for k, n in enumerate(MATRICES):
                sp.dma_start(W[n][:, :], matrices_in[k, :, :]).then_inc(weights_landed, 16)
            for k, n in enumerate(ROWS):
                sp.dma_start(row[n][:, :], rows_in[k:k + 1, :]).then_inc(weights_landed, 16)
            for k, n in enumerate(COLUMNS):
                sp.dma_start(col[n][:, :], columns_in[k, :, :]).then_inc(weights_landed, 16)
            sp.wait_ge(relu_made, 1)
            sp.dma_start(relu_table.rearrange("(k p) f -> p k f", p=P), hidden[:, 0:NT * F].rearrange(
                "p (k f) -> p k f", f=F)).then_inc(relu_stored, 16)
            sp.wait_ge(flag_made, 2)
            for d, b in ((flag_dram, 0), (sign_dram, 1)):
                sp.dma_start(d.rearrange("(p j) -> p j", p=P), flag8[:, b, :]).then_inc(flag_stored, 16)
            sp.wait_ge(flag_stored, 32)

            for p, kind in enumerate(PASSES):
                e, n = edge[p], node[p]

                def load(u, s):
                    use, t = p * EI + u, u * RING + s
                    one = bass.ds(t, 1)
                    wait(sp, src_gathered[s], use * 16 * CH)
                    sp.dma_start(idx_src[s][:, :], src_in[one, :, :].rearrange("a p c -> (a p) c")).then_inc(idx_landed[s], 16)
                    if kind == MESSAGE:
                        wait(sp, dst_gathered[s], u * 16 * CH)
                        sp.dma_start(idx_dst[s][:, :], dst_in[one, :, :].rearrange("a p c -> (a p) c"))\
                          .then_inc(idx_dst_landed[s], 16)
                    if kind != MEAN:
                        wait(sp, e["hid"], t - RING + 1)
                        sp.dma_start(attr[:, s, :], attr_in[:, bass.ds(t * TE, TE)]).then_inc(attr_landed[s], 16)
                    wait(sp, e["summed"], t - RING + 1)
                    sp.dma_start(flags[:, s, :], flag_t[p][one, :].to_broadcast([F, TE])).then_inc(flags_landed[s], 16)

                over_tiles(sp, load)

                def store(g):
                    if kind == SOFT:
                        sp.wait_ge(n["src_kept"], g + 1)
                        sp.dma_start(node_rows(src_table, g), xg).then_inc(n["stored"], 16)
                        sp.wait_ge(n["dst_kept"], g + 1)
                        sp.dma_start(node_rows(dst_table, g), dg).then_inc(n["dst_stored"], 16)
                    elif p < len(PASSES) - 1:
                        sp.wait_ge(n["normed"], g + 1)
                        sp.dma_start(node_rows(next_table[p], g), ng).then_inc(n["stored"], 16)
                    else:
                        sp.wait_ge(n["normed"], g + 1)
                        if isinstance(g, int) and g == NG - 1:
                            done = g * GT
                            if FULL > done:
                                sp.dma_start(out[done * P:FULL * P, :].rearrange("(k p) f -> p k f", p=P),
                                             ng[:, 0:FULL - done, :]).then_inc(n["stored"], 16)
                            sp.dma_start(out[FULL * P:n_nodes, :], ng[0:REST, FULL - done, :]).then_inc(out_stored, 16)
                        else:
                            sp.dma_start(node_rows_out(g), ng).then_inc(n["stored"], 16)

                def node_rows_out(g):
                    return out[bass.ds(g * GC, GC), :].rearrange("(k p) f -> p k f", p=P)

                over_groups(sp, nothing, store)
            sp.wait_ge(node[-1]["stored"], 16 * (NG - (FULL == (NG - 1) * GT)))
            sp.wait_ge(out_stored, 16)

        @block.gpsimd
        def _(pool):
            chain = Chain(pool, pool_step)
            nc.gpsimd.memset(x_sb[:, FULL:NT, :], 0.0).then_inc(consts_made, 1)
            nc.gpsimd.memset(ones[:, :], 1.0)
            nc.gpsimd.memset(eps[:, :], EPS)
            nc.gpsimd.memset(tri, 1.0)
            chain.do(nc.gpsimd.memset(ident[:, :], 0.0))
            nc.gpsimd.affine_select(out=ident[:, :], in_=ident[:, :], compare_op=ALU.not_equal, fill=1.0, base=0,
                                    pattern=[[-1, P]], channel_multiplier=1)
            nc.gpsimd.affine_select(out=tri, in_=tri, compare_op=ALU.is_ge, fill=0.0, base=0,
                                    pattern=[[1, P]], channel_multiplier=-1)
            nc.gpsimd.iota(iota_lo, pattern=[[1, P]], base=0, channel_multiplier=0, allow_small_or_imprecise_dtypes=True)
            nc.gpsimd.iota(iota_hi, pattern=[[1, NT]], base=0, channel_multiplier=0, allow_small_or_imprecise_dtypes=True)\
              .then_inc(consts_made, 1)

            for p, kind in enumerate(PASSES):
                e, n = edge[p], node[p]
                if p == 0:
                    pool.wait_ge(relu_stored, 16)
                    pool.wait_ge(index_made, 1)
                wait_for_tables(pool, p)

                def gather(u, s):
                    use, t = p * EI + u, u * RING + s
                    wait(pool, idx_landed[s], (use + 1) * 16)
                    wait(pool, e["turned"], t - RING + 1)
                    pool.sem_inc(gathers_begun, 1)
                    for c in range(CH):
                        pool.indirect_dma_start(out=src_rows[:, s, c, :], out_offset=None, in_=gather_table[p],
                                                in_offset=bass.IndirectOffsetOnAxis(ap=idx_src[s][:, c:c + 1], axis=0))\
                            .then_inc(src_gathered[s], 16)
                    if kind == MESSAGE:
                        wait(pool, idx_dst_landed[s], (u + 1) * 16)
                        pool.sem_inc(gathers_begun, 1)
                        for c in range(CH):
                            pool.indirect_dma_start(out=dst_rows[:, s, c, :], out_offset=None, in_=dst_table,
                                                    in_offset=bass.IndirectOffsetOnAxis(ap=idx_dst[s][:, c:c + 1], axis=0))\
                                .then_inc(dst_gathered[s], 16)

                over_tiles(pool, gather)

                for s in range(RING):
                    pool.wait_ge(sums_stored[s], 16 * EI * (p + 1))
                for g in range(NG):
                    for k in range(g * GT, (g + 1) * GT):
                        wide = 2 * F if kind == SOFT else F
                        pool.indirect_dma_start(out=ends[:, k, 0:wide], out_offset=None,
                                                in_=soft_sums if kind == SOFT else sums,
                                                in_offset=bass.IndirectOffsetOnAxis(ap=end_row[:, k:k + 1], axis=0))\
                            .then_inc(ends_landed[g], 16)
                    if g:
                        pool.wait_ge(ends_landed[g - 1], 16 * GT * (p + 1))
                        pool.sem_inc(ends_ready, 1)
                pool.wait_ge(ends_landed[NG - 1], 16 * GT * (p + 1))
                pool.sem_inc(ends_ready, 1)

        @block.tensor
        def _(pe):
            pe.wait_ge(consts_made, 2)
            pe.wait_ge(weights_landed, 16 * (len(MATRICES) + len(ROWS) + len(COLUMNS) + 1))
            pe.wait_ge(hot_made, 1)
            nc.tensor.matmul(bank(0, P, NT), hot_lo[:, 0, 0, :], hot_hi[:, 0, 0, :], start=True, stop=False)
            for c in range(1, HC):
                last = nc.tensor.matmul(bank(0, P, NT), hot_lo[:, 0, c, :], hot_hi[:, 0, c, :], start=False, stop=False)
            last.then_inc(hot_used, 1)

            def count(number, b):
                pe.wait_ge(hot_made, number + 1)
                for c in range(HC):
                    last = nc.tensor.matmul(bank(0, P, NT), hot_lo[:, b, c, :], hot_hi[:, b, c, :], start=False, stop=False)
                last.then_inc(hot_used, 1)

            count(1, 1)
            with pe.Fori(1, HI - 1) as i:
                count(2 * i, 0)
                count(2 * i + 1, 1)
            count(2 * HI - 2, 0)
            pe.wait_ge(hot_made, 2 * HI)
            for c in range(HC):
                last = nc.tensor.matmul(bank(0, P, NT), hot_lo[:, 1, c, :], hot_hi[:, 1, c, :], start=False, stop=c == HC - 1)
            last.then_inc(deg_counted, 1)
            pe.wait_ge(deg_made, 1)
            nc.tensor.matmul(bank(1, P, NT), tri, deg[:, :], start=True, stop=True)
            nc.tensor.matmul(bank(2, P, NT), ones[:, :], deg[:, :], start=True, stop=True).then_inc(prefix_summed, 1)

            for p, kind in enumerate(PASSES):
                e, n = edge[p], node[p]

                def project(u, s):
                    t = u * RING + s
                    wait(pe, attr_landed[s], (p * EI + u + 1) * 16)
                    wait(pe, e["hrelu"], t - 1)
                    nc.tensor.matmul(bank(6 + s % 2, F), w_edge[:, :], attr[:, s, :], start=True, stop=True)\
                      .then_inc(e["hid"], 1)

                def turn(u, s):
                    t = u * RING + s
                    wait(pe, src_gathered[s], (p * EI + u + 1) * 16 * CH)
                    wait(pe, e["weighed"] if kind == SOFT else e["summed"], t - 1)
                    for c in range(CH):
                        last = nc.tensor.transpose(ps[0:F, s % 2, c * P:(c + 1) * P], src_rows[:, s, c, :], ident[:, :])
                    last.then_inc(e["turned"], 1)

                def score(u, s):
                    t = u * RING + s
                    wait(pe, e["hrelu"], t + 1)
                    wait(pe, e["relued"], t - 1)
                    nc.tensor.matmul(bank(s % 2, F), w_ef_scaled[:, :], h_ring[:, s % 2, :], start=True, stop=False)
                    wait(pe, src_gathered[s], (p * EI + u + 1) * 16 * CH)
                    wait(pe, dst_gathered[s], (u + 1) * 16 * CH)
                    for c in range(CH):
                        for rows in (src_rows, dst_rows):
                            last = nc.tensor.matmul(ps[0:F, s % 2, c * P:(c + 1) * P], rows[:, s, c, :], ident[:, :],
                                                    start=False, stop=c == CH - 1 and rows is dst_rows)
                    last.then_inc(e["turned"], 1)

                def turn_back(u, s):
                    t = u * RING + s
                    wait(pe, e["summed"], t + 1)
                    wait(pe, e["copied"], t - 1)
                    for r, b in ((sum_ring, 2), (num_ring, 4))[0:2 if kind == SOFT else 1]:
                        for c in range(CH):
                            last = nc.tensor.transpose(ps[:, b + s % 2, c * F:(c + 1) * F],
                                                       r[:, (s * CH + c) * P:(s * CH + c + 1) * P], ident[0:F, 0:F])
                    last.then_inc(e["back"], 1)

                def turn_and_project(u, s):
                    turn(u, s)
                    project(u, s)

                def score_and_turn_back(u, s):
                    score(u, s)
                    tile_before(turn_back, u, s)

                if kind == SOFT:
                    over_tiles(pe, turn_and_project, lambda u, s: tile_before(turn_back, u, s))
                    turn_back(EI - 1, RING - 1)
                elif kind == MESSAGE:
                    pe.wait_ge(ef_coefs_made, 1)
                    nc.tensor.matmul(bank(2, F, 1), W["W_ef"][:, :], t_ef[:, :], start=True, stop=True)\
                      .then_inc(ef_bias_summed, 1)
                    over_tiles(pe, project, score_and_turn_back)
                    turn_back(EI - 1, RING - 1)
                    pe.wait_ge(diags_made, 1)
                    pe.wait_ge(e["copied"], ET)
                    nc.tensor.matmul(bank(2, P, F), ones[0:F, :], diag_s[:, :], start=True, stop=True)
                    nc.tensor.matmul(bank(3, P, F), ones[0:F, :], diag_t[:, :], start=True, stop=True)\
                      .then_inc(rows_spread, 1)
                else:
                    over_tiles(pe, turn, turn_back)

                left = {0: "W0", 2: "W2l1", 3: "W2l2", 4: "W3l1", 5: "W3l2"}.get(p)
                right = {2: "W2r1", 3: "W2r2", 4: "W3r1", 5: "W3r2"}.get(p)
                bias = {0: "b0", 2: "b21", 3: "b22", 4: "b31", 5: "b32"}.get(p)

                def turn_nodes(g):
                    wait(pe, n["prepared"], g + 1)
                    wait(pe, n["copied"], g)
                    for k in range(GT):
                        last = nc.tensor.transpose(feature_major(0)[:, k * P:(k + 1) * P], grp[:, k, :], ident[:, :])
                    if right:
                        pe.wait_ge(n["xcopied"], g + 1)
                        for k in range(GT):
                            last = nc.tensor.transpose(feature_major(2)[:, k * P:(k + 1) * P], xg[:, k, :], ident[:, :])
                    last.then_inc(n["turned"], 1)

                def mix(g):
                    pe.wait_ge(n["copied"], g + 1)
                    wait(pe, n["normed"], g)
                    if kind == SOFT:
                        wait(pe, n["nh_kept"], g)
                    for k in range(GT):
                        o = node_major(4)[:, k, 0:F]
                        nc.tensor.matmul(o, fa[:, k * P:(k + 1) * P], W[left][:, :], start=True, stop=False)
                        if right:
                            nc.tensor.matmul(o, fx[:, k * P:(k + 1) * P], W[right][:, :], start=False, stop=False)
                        last = nc.tensor.matmul(o, ones[0:1, :], row[bias][:, :], start=False, stop=True)
                    last.then_inc(n["mixed"], 1)

                def project_nodes(g):
                    mix(g)
                    pe.wait_ge(n["normed"], g + 1)
                    wait(pe, n["copied2"], g)
                    for k in range(GT):
                        last = nc.tensor.transpose(feature_major(2)[:, k * P:(k + 1) * P], ng[:, k, :], ident[:, :])
                    last.then_inc(n["turned2"], 1)
                    pe.wait_ge(n["copied2"], g + 1)
                    wait(pe, n["dst_kept"], g)
                    for k in range(GT):
                        last = nc.tensor.matmul(node_major(6)[:, k, 0:F], fx[:, k * P:(k + 1) * P], W["W_src"][:, :],
                                                start=True, stop=True)
                    last.then_inc(n["src_made"], 1)
                    for c, w in ((0, 512), (512, GC - 512)):
                        last = nc.tensor.matmul(feature_major(4)[:, c:c + w], W["W_node"][:, :], fx[:, c:c + w],
                                                start=True, stop=True)
                    last.then_inc(n["nh_made"], 1)
                    pe.wait_ge(n["src_kept"], g + 1)
                    for k in range(GT):
                        last = nc.tensor.matmul(node_major(6)[:, k, 0:F], fx[:, k * P:(k + 1) * P], W["W_dst"][:, :],
                                                start=True, stop=True)
                    last.then_inc(n["dst_made"], 1)

                def turn_features(g):
                    pe.wait_ge(n["copied"], g + 1)
                    wait(pe, n["normed"], g)
                    for k in range(GT):
                        last = nc.tensor.transpose(node_major(4)[:, k, 0:F], fx[:, k * P:(k + 1) * P], ident[0:F, 0:F])
                    last.then_inc(n["mixed"], 1)

                if kind == SOFT:
                    over_groups(pe, turn_nodes, project_nodes)
                elif kind == MESSAGE:
                    over_groups(pe, nothing, turn_features)
                else:
                    over_groups(pe, turn_nodes, mix)

        @block.scalar
        def _(act):
            act.wait_ge(consts_made, 2)
            act.wait_ge(weights_landed, 16 * (len(MATRICES) + len(ROWS) + len(COLUMNS) + 1))

            def coef_root(number):
                act.wait_ge(coef_var_made, number)
                nc.scalar.activation(var[:, :], var[:, :], ACT.Sqrt, bias=eps[0:F, :]).then_inc(coef_rooted, 1)

            for p, kind in enumerate(PASSES):
                e, n = edge[p], node[p]

                wait_for_tables(act, p)

                def valid_edges(u, s):
                    return max(0, min(TE, n_edges - (u * RING + s) * TE)) if isinstance(u, int) else TE

                def relu_and_stats(o, i, bias, total, squares, t, v, done, squared):
                    wait(act, squared, t)
                    if v < TE:
                        last = nc.scalar.activation(o[:, v:TE], i[:, v:TE], ACT.Relu, bias=bias)
                    if v:
                        last = nc.scalar.activation(o[:, 0:v], i[:, 0:v], ACT.Relu, bias=bias, accum_out=total[:, bass.ds(t, 1)])
                    last.then_inc(done, 1)
                    act.wait_ge(done, t + 1)
                    if v:
                        nc.scalar.activation(dump[:, 0:v], o[:, 0:v], ACT.Square, accum_out=squares[:, bass.ds(t, 1)])\
                          .then_inc(squared, 1)
                    else:
                        act.sem_inc(squared, 1)

                def copy_back(u, s):
                    use, t = p * EI + u, u * RING + s
                    wait(act, e["back"], t + 1)
                    wait(act, sums_stored[s], use * 16)
                    if kind == SOFT:
                        for half, b in ((0, 2), (1, 4)):
                            last = nc.scalar.activation(out_ring[:, s, :, half * F:(half + 1) * F],
                                                        bank(b + s % 2, P, CH * F).rearrange("p (c f) -> p c f", f=F), ACT.Copy)
                        last.then_inc(e["copied"], 1)
                        act.wait_ge(e["copied"], t + 1)
                        act.dma_start(soft_sums_t[bass.ds(t, 1), :, :].rearrange("a p n -> (a p) n"),
                                      out_ring[:, s, :, :].rearrange("p c f -> p (c f)")).then_inc(sums_stored[s], 16)
                    else:
                        o = out_ring[:, s, 0:CH // 2, :].rearrange("p c f -> p (c f)")
                        nc.scalar.activation(o, bank(2 + s % 2, P, CH * F), ACT.Copy).then_inc(e["copied"], 1)
                        act.wait_ge(e["copied"], t + 1)
                        act.dma_start(sums_t[bass.ds(t, 1), :, :].rearrange("a p n -> (a p) n"), o).then_inc(sums_stored[s], 16)

                def soften(u, s):
                    t = u * RING + s
                    wait(act, e["hid"], t + 1)
                    relu_and_stats(relu_dump, bank(6 + s % 2, F), col["b_edge"][:, :], ef_sum, ef_sq, t, valid_edges(u, s),
                                   e["hrelu"], e["squared"])
                    wait(act, e["scored"], t + 1)
                    nc.scalar.activation(decay[:, s % 2, :], decay[:, s % 2, :], ACT.Exp)
                    nc.scalar.activation(weight[:, s % 2, :], weight[:, s % 2, :], ACT.Exp).then_inc(e["expd"], 1)

                def relu_features(u, s):
                    t = u * RING + s
                    wait(act, e["hid"], t + 1)
                    wait(act, e["turned"], t - 1)
                    nc.scalar.activation(h_ring[:, s % 2, :], bank(6 + s % 2, F), ACT.Relu, bias=col["b_edge"][:, :])\
                      .then_inc(e["hrelu"], 1)

                def relu_message(u, s):
                    t = u * RING + s
                    wait(act, e["turned"], t + 1)
                    wait(act, e["summed"], t - RING + 1)
                    relu_and_stats(msg_ring[:, s, :], bank(s % 2, F), msg_bias[:, :], mg_sum, mg_sq, t, valid_edges(u, s),
                                   e["relued"], e["squared"])
                    tile_before(copy_back, u, s)

                if kind == SOFT:
                    over_tiles(act, soften, lambda u, s: tile_before(copy_back, u, s))
                    copy_back(EI - 1, RING - 1)
                elif kind == MESSAGE:
                    coef_root(1)
                    coef_root(2)
                    act.wait_ge(msg_bias_made, 1)
                    over_tiles(act, relu_features, relu_message)
                    copy_back(EI - 1, RING - 1)
                    coef_root(3)
                else:
                    over_tiles(act, nothing, copy_back)

                source = {2: x_sb, 3: h_sb, 4: x_sb, 5: h_sb}.get(p)
                kept_in = {0: x_sb, 1: x_sb, 2: h_sb, 3: x_sb, 4: h_sb}[p] if p < len(PASSES) - 1 else None

                def keep(g):
                    if p not in (2, 4):
                        act.wait_ge(var_summed, norms_before(p) + g + 1)
                        nc.scalar.activation(rstd[:, :], rstd[:, :], ACT.Sqrt, bias=eps[:, :], scale=1.0 / F)\
                          .then_inc(rooted, 1)
                    if kept_in is not None:
                        act.wait_ge(n["normed"], g + 1)
                        nc.scalar.activation(of_group(kept_in, g), ng, ACT.Copy).then_inc(n["kept"], 1)

                def copy_turned(g):
                    if source is not None:
                        wait(act, n["turned"], g)
                        nc.scalar.activation(xg, of_group(source, g), ACT.Copy).then_inc(n["xcopied"], 1)
                    act.wait_ge(n["turned"], g + 1)
                    wait(act, n["mixed"], g)
                    if source is not None:
                        nc.scalar.activation(fx, feature_major(2), ACT.Copy)
                    nc.scalar.activation(fa, feature_major(0), ACT.Copy).then_inc(n["copied"], 1)

                def exp_and_keep(g):
                    act.wait_ge(n["floored"], g + 1)
                    nc.scalar.activation(sq, sq, ACT.Exp).then_inc(n["expd"], 1)
                    keep(g)

                def node_features(g):
                    keep(g)
                    act.wait_ge(n["turned2"], g + 1)
                    wait(act, n["dst_made"], g)
                    nc.scalar.activation(fx, feature_major(2), ACT.Copy).then_inc(n["copied2"], 1)
                    act.wait_ge(n["src_made"], g + 1)
                    wait(act, n["stored"], g * 16)
                    nc.scalar.activation(xg, node_major(6)[:, 0:GT, 0:F], ACT.Copy).then_inc(n["src_kept"], 1)
                    act.wait_ge(n["nh_made"], g + 1)
                    v = min(GC, n_nodes - g * GC) if isinstance(g, int) else GC
                    nf = node_feat[:, bass.ds(g * GC, GC)]
                    if v < GC:
                        nc.scalar.activation(nf[:, v:GC], feature_major(4)[:, v:GC], ACT.Relu, bias=col["b_node"][:, :])
                    nc.scalar.activation(nf[:, 0:v], feature_major(4)[:, 0:v], ACT.Relu, bias=col["b_node"][:, :],
                                         accum_out=nd_sum[:, bass.ds(g, 1)]).then_inc(n["nh_kept"], 1)
                    act.wait_ge(n["nh_kept"], g + 1)
                    nc.scalar.activation(dump[:, 0:v], nf[:, 0:v], ACT.Square, accum_out=nd_sq[:, bass.ds(g, 1)])\
                      .then_inc(n["nh_squared"], 1)

                def norm_features(g):
                    wait(act, n["mixed"], g)
                    nc.scalar.activation(fx, node_feat[:, bass.ds(g * GC, GC)], ACT.Identity, bias=t_nd[:, :], scale=s_nd[:, :])\
                      .then_inc(n["copied"], 1)

                if kind == SOFT:
                    over_groups(act, copy_turned, node_features)
                elif kind == MESSAGE:
                    over_groups(act, norm_features, keep)
                elif p == 4:
                    over_groups(act, copy_turned, exp_and_keep)
                else:
                    over_groups(act, copy_turned, keep)

        @block.vector
        def _(dve):
            v = nc.vector
            chain = Chain(dve, dve_step)

            def every(t, g):
                return of_group(t, g).unsqueeze(2).to_broadcast([P, GT, F])

            def by_feature(r):
                return r[:, :].unsqueeze(1).to_broadcast([P, GT, F])

            dve.wait_ge(x_landed, 32)
            v.tensor_scalar(h_sb, x_sb[:, :, :], 0.0, MSG_EPS, ALU.max, ALU.add).then_inc(relu_made, 1)
            dve.wait_ge(seq_landed, 32)
            v.tensor_tensor(flag8[:, 0, :], seq_now, seq_before, ALU.is_equal).then_inc(flag_made, 1)
            dve.wait_ge(flag_made, 1)
            v.tensor_scalar(flag8[:, 1, :], flag8[:, 0, :], 2.0, -1.0, ALU.mult, ALU.add).then_inc(flag_made, 1)
            for t in (ef_sum, ef_sq, mg_sum, mg_sq):
                v.memset(t[:, :], 0.0)
            dve.wait_ge(cols_landed, 16)
            chain.do(v.tensor_scalar(seq_now, seq_int, P - 1, None, ALU.bitwise_and))
            chain.do(v.tensor_copy(cols_lo, seq_now))
            chain.do(v.tensor_scalar(seq_now, seq_int, 7, None, ALU.arith_shift_right))
            chain.do(v.tensor_copy(cols_hi, seq_now))
            dve.wait_ge(consts_made, 2)

            def hot(i, b, number):
                wait(dve, hot_used, number - 1)
                at = bass.ds(i * 2 * HC + b * HC, HC)
                v.tensor_tensor(hot_lo[:, b, :, :], cols_lo[:, at].unsqueeze(2).to_broadcast([P, HC, P]),
                                iota_lo.unsqueeze(1).to_broadcast([P, HC, P]), ALU.is_equal)
                v.tensor_tensor(hot_hi[:, b, :, :], cols_hi[:, at].unsqueeze(2).to_broadcast([P, HC, NT]),
                                iota_hi.unsqueeze(1).to_broadcast([P, HC, NT]), ALU.is_equal).then_inc(hot_made, 1)

            for b in range(2):
                hot(0, b, b)
            with dve.Fori(1, HI) as i:
                for b in range(2):
                    hot(i, b, 2 * i + b)
            dve.wait_ge(deg_counted, 1)
            v.tensor_copy(deg[:, :], bank(0, P, NT)).then_inc(deg_made, 1)
            dve.wait_ge(deg_made, 1)
            chain.do(v.tensor_scalar(has[:, :], deg[:, :], 1.0, None, ALU.min))
            chain.do(v.tensor_scalar(rdeg[:, :], deg[:, :], 1.0, None, ALU.max))
            chain.do(v.reciprocal(rdeg[:, :], rdeg[:, :]))
            chain.do(v.tensor_tensor(rdeg[:, :], rdeg[:, :], has[:, :], ALU.mult))
            dve.wait_ge(prefix_summed, 1)
            chain.do(v.tensor_copy(total[:, :], bank(2, P, NT)))
            chain.do(v.tensor_tensor_scan(out=before[:, :], data0=total[:, :], data1=total[:, :], initial=0.0,
                                          op0=ALU.add, op1=ALU.bypass))
            chain.do(v.tensor_tensor(before[:, :], before[:, :], total[:, :], ALU.subtract))
            chain.do(v.tensor_tensor(end_f[:, :], before[:, :], bank(1, P, NT), ALU.add))
            chain.do(v.tensor_scalar(end_f[:, :], end_f[:, :], -1.0, 0.0, ALU.add, ALU.max))
            chain.do(v.tensor_copy(end_i[:, :], end_f[:, :]))
            chain.do(v.tensor_scalar(end_j[:, :], end_i[:, :], P - 1, CH // 2, ALU.bitwise_and, ALU.logical_shift_left))
            chain.do(v.tensor_scalar(end_row[:, :], end_i[:, :], 7, CH - 1, ALU.logical_shift_right, ALU.bitwise_and))
            chain.do(v.tensor_tensor(end_j[:, :], end_j[:, :], end_row[:, :], ALU.bitwise_or))
            chain.do(v.tensor_scalar(end_i[:, :], end_i[:, :], 9, 9, ALU.logical_shift_right, ALU.logical_shift_left))
            v.tensor_tensor(end_row[:, :], end_i[:, :], end_j[:, :], ALU.bitwise_or).then_inc(index_made, 1)
            dve.wait_ge(index_made, 1)

            def norm_coefs(number, total, squares, count, g, beta, s, t):
                chain.do(v.reduce_sum(mu[:, :], total, axis=X))
                chain.do(v.reduce_sum(var[:, :], squares, axis=X))
                chain.do(v.tensor_scalar(mu[:, :], mu[:, :], 1.0 / count, None, ALU.mult))
                chain.do(v.tensor_tensor(tmp[:, :], mu[:, :], mu[:, :], ALU.mult))
                chain.do(v.scalar_tensor_tensor(var[:, :], var[:, :], 1.0 / count, tmp[:, :], ALU.mult, ALU.subtract))
                v.tensor_scalar(var[:, :], var[:, :], 0.0, None, ALU.max).then_inc(coef_var_made, 1)
                dve.wait_ge(coef_rooted, number)
                chain.do(v.reciprocal(var[:, :], var[:, :]))
                chain.do(v.tensor_tensor(s[:, :], g[:, :], var[:, :], ALU.mult))
                chain.do(v.tensor_tensor(tmp[:, :], s[:, :], mu[:, :], ALU.mult))
                chain.do(v.tensor_tensor(t[:, :], beta[:, :], tmp[:, :], ALU.subtract))

            for p, kind in enumerate(PASSES):
                e, n = edge[p], node[p]

                wait_for_tables(dve, p)

                def start_from_zero():
                    at = RING * TE - 1
                    chain.do(v.memset(sum_ring[:, at:at + 1], 0.0))
                    if kind == SOFT:
                        chain.do(v.memset(num_ring[:, at:at + 1], 0.0))
                        chain.do(v.memset(max_ring[:, 0:1], 0.0))

                def last_of(r, s):
                    at = s * TE - 1 if s else RING * TE - 1
                    return r[:, at:at + 1]

                def slot(r, s):
                    return r[:, s * TE:(s + 1) * TE]

                def scan(u, s):
                    t = u * RING + s
                    wait(dve, e["relued"] if kind == MESSAGE else e["turned"], t + 1)
                    wait(dve, flags_landed[s], (p * EI + u + 1) * 16)
                    wait(dve, e["back"], t - RING + 1)
                    wait(dve, e["summed"], t)
                    v.tensor_tensor_scan(out=slot(sum_ring, s), data0=flags[:, s, :],
                                         data1=msg_ring[:, s, :] if kind == MESSAGE else bank(s % 2, F),
                                         initial=last_of(sum_ring, s), op0=ALU.mult, op1=ALU.add).then_inc(e["summed"], 1)

                def running_max(u, s):
                    t, b = u * RING + s, s % 2
                    wait(dve, e["turned"], t + 1)
                    wait(dve, flags_landed[s], (p * EI + u + 1) * 16)
                    if s == 0 and not (isinstance(u, int) and u == 0):
                        v.tensor_copy(max_ring[:, 0:1], max_ring[:, RING * TE:RING * TE + 1]).then_inc(e["wrapped"], 1)
                        dve.wait_ge(e["wrapped"], u)
                    now = max_ring[:, 1 + s * TE:1 + (s + 1) * TE]
                    v.tensor_tensor_scan(out=now, data0=flags[:, s, :], data1=bank(b, F),
                                         initial=max_ring[:, s * TE:s * TE + 1], op0=ALU.mult, op1=ALU.max)\
                     .then_inc(e["maxed"], 1)
                    dve.wait_ge(e["maxed"], t + 1)
                    v.scalar_tensor_tensor(decay[:, b, :], flags[:, s, :], BIG, max_ring[:, s * TE:(s + 1) * TE],
                                           ALU.mult, ALU.min).then_inc(e["masked"], 1)
                    dve.wait_ge(e["masked"], t + 1)
                    v.tensor_tensor(decay[:, b, :], decay[:, b, :], now, ALU.subtract)
                    v.tensor_tensor(weight[:, b, :], bank(b, F), now, ALU.subtract).then_inc(e["scored"], 1)

                def soft_scan(u, s):
                    t, b = u * RING + s, s % 2
                    dve.wait_ge(e["expd"], t + 1)
                    v.tensor_tensor(weighted[:, b, :], weight[:, b, :], bank(b, F), ALU.mult).then_inc(e["weighed"], 1)
                    wait(dve, e["back"], t - RING + 1)
                    wait(dve, e["summed"], t)
                    v.tensor_tensor_scan(out=slot(sum_ring, s), data0=decay[:, b, :], data1=weight[:, b, :],
                                         initial=last_of(sum_ring, s), op0=ALU.mult, op1=ALU.add)
                    dve.wait_ge(e["weighed"], t + 1)
                    v.tensor_tensor_scan(out=slot(num_ring, s), data0=decay[:, b, :], data1=weighted[:, b, :],
                                         initial=last_of(num_ring, s), op0=ALU.mult, op1=ALU.add).then_inc(e["summed"], 1)

                if kind == MESSAGE:
                    dve.wait_ge(edge[0]["squared"], ET)
                    norm_coefs(1, ef_sum[:, :], ef_sq[:, :], n_edges, col["g_edge"], col["beta_edge"], s_ef, t_ef)
                    v.tensor_scalar(w_ef_scaled[:, :], W["W_ef"][:, :], s_ef[:, :], None, ALU.mult).then_inc(ef_coefs_made, 1)
                    dve.wait_ge(node[0]["nh_squared"], NG)
                    norm_coefs(2, nd_sum[:, :], nd_sq[:, :], n_nodes, col["g_node"], col["beta_node"], s_nd, t_nd)
                    dve.wait_ge(ef_bias_summed, 1)
                    v.tensor_tensor(msg_bias[:, :], bank(2, F, 1), col["b_msg"][:, :], ALU.add).then_inc(msg_bias_made, 1)

                start_from_zero()
                if kind == SOFT:
                    over_tiles(dve, running_max, soft_scan)
                else:
                    over_tiles(dve, nothing, scan)

                if kind == MESSAGE:
                    dve.wait_ge(e["squared"], ET)
                    norm_coefs(3, mg_sum[:, :], mg_sq[:, :], n_edges, col["g_msg"], col["beta_msg"], s_mg, t_mg)
                    v.tensor_scalar(diag_s[:, :], ident[0:F, 0:F], s_mg[:, :], None, ALU.mult)
                    v.tensor_scalar(diag_t[:, :], ident[0:F, 0:F], t_mg[:, :], None, ALU.mult).then_inc(diags_made, 1)
                    dve.wait_ge(rows_spread, 1)
                    chain.do(v.tensor_copy(s_row[:, :], bank(2, P, F)))
                    chain.do(v.tensor_copy(t_row[:, :], bank(3, P, F)))

                mixed = node_major(4)[:, 0:GT, 0:F]

                def result_free(g):
                    if p < len(PASSES) - 1:
                        wait(dve, n["kept"], g)
                    if kind == SOFT:
                        wait(dve, n["turned2"], g)
                    else:
                        wait(dve, n["stored"], g * 16)

                def layer_norm(g):
                    chain.do(v.reduce_sum(mean[:, :], res, axis=X))
                    chain.do(v.tensor_scalar(mean[:, :], mean[:, :], 1.0 / F, None, ALU.mult))
                    chain.do(v.tensor_tensor(res, res, mean[:, :].unsqueeze(2).to_broadcast([P, GT, F]), ALU.subtract))
                    chain.do(v.tensor_tensor(sq, res, res, ALU.mult))
                    v.reduce_sum(rstd[:, :], sq, axis=X).then_inc(var_summed, 1)
                    dve.wait_ge(rooted, norms_before(p) + g + 1)
                    chain.do(v.reciprocal(rstd[:, :], rstd[:, :]))
                    result_free(g)
                    v.tensor_tensor(ng, res, rstd[:, :].unsqueeze(2).to_broadcast([P, GT, F]), ALU.mult)\
                     .then_inc(n["normed"], 1)

                def soft_prepare(g):
                    dve.wait_ge(ends_ready, p * NG + g + 1)
                    e_g = ends[:, bass.ds(g * GT, GT), :]
                    sum_g, num_g = e_g[:, :, 0:F], e_g[:, :, F:2 * F]
                    chain.do(v.reciprocal(sum_g, sum_g))
                    chain.do(v.tensor_tensor(num_g, num_g, sum_g, ALU.mult))
                    chain.do(v.tensor_tensor(num_g, num_g, every(has, g), ALU.mult))
                    wait(dve, n["turned"], g)
                    v.tensor_tensor(grp, num_g, of_group(x_sb, g), ALU.add).then_inc(n["prepared"], 1)

                def prepare(g):
                    dve.wait_ge(ends_ready, p * NG + g + 1)
                    wait(dve, n["turned"], g)
                    v.tensor_tensor(grp, ends[:, bass.ds(g * GT, GT), 0:F], every(rdeg, g), ALU.mult)\
                     .then_inc(n["prepared"], 1)

                def add_and_norm(g):
                    dve.wait_ge(n["mixed"], g + 1)
                    wait(dve, n["normed"], g)
                    chain.do(v.tensor_tensor(res, mixed, of_group(x_sb, g), ALU.add))
                    layer_norm(g)

                def norm_and_keep(g):
                    add_and_norm(g)
                    dve.wait_ge(n["dst_made"], g + 1)
                    wait(dve, n["dst_stored"], g * 16)
                    v.tensor_copy(dg, node_major(6)[:, 0:GT, 0:F]).then_inc(n["dst_kept"], 1)

                def relu(g):
                    dve.wait_ge(n["mixed"], g + 1)
                    result_free(g)
                    v.tensor_scalar(ng, mixed, 0.0, None, ALU.max).then_inc(n["normed"], 1)

                def elu(g):
                    dve.wait_ge(n["mixed"], g + 1)
                    wait(dve, n["normed"], g)
                    v.tensor_scalar(sq, mixed, 0.0, None, ALU.min).then_inc(n["floored"], 1)
                    chain.do(v.tensor_scalar(res, mixed, 0.0, None, ALU.max))
                    dve.wait_ge(n["expd"], g + 1)
                    result_free(g)
                    v.scalar_tensor_tensor(ng, sq, -1.0, res, ALU.add, ALU.add).then_inc(n["normed"], 1)

                def join(g):
                    dve.wait_ge(ends_ready, p * NG + g + 1)
                    wait(dve, n["normed"], g)
                    chain.do(v.tensor_tensor(res, ends[:, bass.ds(g * GT, GT), 0:F], every(has, g), ALU.mult))
                    chain.do(v.tensor_tensor(res, res, by_feature(s_row), ALU.mult))
                    chain.do(v.tensor_tensor(sq, every(deg, g), by_feature(t_row), ALU.mult))
                    chain.do(v.tensor_tensor(res, res, sq, ALU.add))
                    chain.do(v.tensor_tensor(res, res, of_group(x_sb, g), ALU.add))
                    dve.wait_ge(n["mixed"], g + 1)
                    chain.do(v.tensor_tensor(res, res, mixed, ALU.add))
                    layer_norm(g)

                if kind == SOFT:
                    over_groups(dve, soft_prepare, norm_and_keep, chain, 3 + 1 + 5)
                elif kind == MESSAGE:
                    over_groups(dve, nothing, join, chain, 6 + 5)
                elif p == 2:
                    over_groups(dve, prepare, relu, chain, 0)
                elif p == 4:
                    over_groups(dve, prepare, elu, chain, 1)
                else:
                    over_groups(dve, prepare, add_and_norm, chain, 1 + 5)


def kernel(**inputs):
    import concourse.bacc as bacc
    from concourse.bass_utils import run_bass_kernel_spmd

    a = {k: np.asarray(v) for k, v in inputs.items()}
    n_edges, ep = a["src"].shape[0], edge_tiles(a["src"].shape[0]) * TE

    def padded(v, fill):
        return np.concatenate([v, np.full((ep - n_edges,), fill, v.dtype)])

    def by_tile(v):
        return np.ascontiguousarray(v.reshape(-1, CH, P).transpose(0, 2, 1))

    w_msg = a["L1_gnn_W_msg"]
    matrices = [a["L0_gnn_W"], a["L1_gnn_W_node"], w_msg[0:F], w_msg[F:2 * F], w_msg[2 * F:3 * F]]
    matrices += [a[n].T for n in ("L2_gnn_Wl1", "L2_gnn_Wr1", "L2_gnn_Wl2", "L2_gnn_Wr2",
                                  "L3_gnn_W1l", "L3_gnn_W1r", "L3_gnn_W2l", "L3_gnn_W2r")]
    rows = [a[n] for n in ("L0_gnn_b", "L2_gnn_bl1", "L2_gnn_bl2", "L3_gnn_b1", "L3_gnn_b2")]
    columns = [a["L1_gnn_" + n] for n in COLUMNS]
    arrays = {
        "x_dram": a["x"],
        "src_dram": by_tile(padded(a["src"], 0)),
        "dst_dram": by_tile(padded(a["dst"], 0)),
        "dst_columns_dram": np.ascontiguousarray(padded(a["dst"], -1).reshape(-1, P).T),
        "dst_sequence_dram": np.concatenate([np.full((1,), -1, a["dst"].dtype), padded(a["dst"], -1)]),
        "attr_dram": np.ascontiguousarray(np.concatenate(
            [a["edge_attr_4"], np.zeros((ep - n_edges, EDGE_DIM), a["edge_attr_4"].dtype)]).T),
        "w_edge_dram": a["L1_gnn_W_edge"],
        "matrices_dram": np.stack(matrices),
        "rows_dram": np.stack(rows),
        "columns_dram": np.stack(columns)[:, :, None],
    }
    nc = bacc.Bacc("TRN2", target_bir_lowering=False, num_devices=1)
    args = [nc.dram_tensor(n, v.shape, mybir.dt.from_np(v.dtype), kind="ExternalInput").ap() for n, v in arrays.items()]
    out = nc.dram_tensor("out_dram", a["x"].shape, mybir.dt.float32, kind="ExternalOutput").ap()
    build(nc, n_edges, *args, out)
    return run_bass_kernel_spmd(nc, [arrays], core_ids=[0]).results[0]["out_dram"]
```

```python
import math
from contextlib import ExitStack

import numpy as np

import concourse.bass as bass
from concourse import mybir

P = 128
F = 96
CH = 4
TE = CH * P
RING = 4
GT = 7
GC = GT * P
EDGE_DIM = 4
MSG_EPS = 1e-7
EPS = 1e-5
BIG = 1e38
HC = 8
PARTS = 3
AK = PARTS * PARTS * EDGE_DIM

MATRICES = ["W0", "W_node", "W_src", "W_dst", "W_ef", "W2l1", "W2r1", "W2l2", "W2r2", "W3l1", "W3r1", "W3l2", "W3r2"]
ROWS = ["b0", "b21", "b22", "b31", "b32"]
COLUMNS = ["b_node", "g_node", "beta_node", "b_edge", "g_edge", "beta_edge", "b_msg", "g_msg", "beta_msg"]

SOFT, MESSAGE, MEAN = range(3)
PASSES = [SOFT, MESSAGE, MEAN, MEAN, MEAN, MEAN]


def edge_tiles(n_edges):
    return RING * math.ceil(n_edges / (TE * RING))


def node_tiles(n_nodes):
    return GT * math.ceil(n_nodes / (P * GT))


def wait(eng, semaphore, value):
    if not (isinstance(value, int) and value <= 0):
        eng.wait_ge(semaphore, value)


class Chain:

    def __init__(self, eng, semaphore):
        self.eng, self.semaphore, self.base, self.n = eng, semaphore, 0, 0

    def do(self, instruction):
        self.n += 1
        instruction.then_inc(self.semaphore, 1)
        self.eng.wait_ge(self.semaphore, self.base + self.n)


def build(nc, n_edges, x_in, src_in, dst_cols_in, dst_before_in, dst_seq_in, attr_in, w_edge_in, matrices_in, rows_in,
          columns_in, out):
    dt = mybir.dt
    f32, i32, i8, bf16 = dt.float32, dt.int32, dt.int8, dt.bfloat16
    ALU = mybir.AluOpType
    ACT = mybir.ActivationFunctionType
    X = mybir.AxisListType.X

    n_nodes = x_in.shape[0]
    ET = edge_tiles(n_edges)
    EI = ET // RING
    EP = ET * TE
    NT = node_tiles(n_nodes)
    NG = NT // GT
    NP = NT * P
    FULL = n_nodes // P
    REST = n_nodes - FULL * P
    SEQ = EP // P
    CN = EP // P
    CB = math.ceil(CN / P)
    HI = CN // HC // 2

    ctx = ExitStack()
    with ctx:
        def sb(name, shape, t=f32):
            return ctx.enter_context(nc.sbuf_tensor(name, shape, t))

        def dram(name, shape, t=f32):
            return nc.dram_tensor(name, shape, t, kind="Internal").ap()

        def sem(name):
            return ctx.enter_context(nc.semaphore(name))

        def ring_sems(name):
            return [sem(f"{name}{s}") for s in range(RING)]

        def sems(suffix, names):
            return {n: sem(f"{n}_{suffix}") for n in names.split()}

        relu_table = dram("relu_table", [NP, F])
        src_table = dram("src_table", [NP, F])
        dst_table = dram("dst_table", [NP + P, F])
        rank_dram = dram("rank_dram", [EP], i8)
        attr_parts = dram("attr_parts", [AK, EP], bf16)
        x_table = dram("x_table", [NP, F])
        h_table = dram("h_table", [NP, F])
        flag_dram = dram("flag_dram", [EP], i8)
        sign_dram = dram("sign_dram", [EP], i8)
        soft_sums = dram("soft_sums", [EP, 2 * F])
        sums = dram("sums", [EP, F])
        soft_sums_t = soft_sums.rearrange("(t p c) f -> t p (c f)", p=P, c=CH)
        sums_t = sums.rearrange("(t p c) f -> t p (c f)", p=P, c=CH)
        flag_t = [d.rearrange("(t e) -> t e", e=TE) for d in (sign_dram, flag_dram, flag_dram, flag_dram,
                                                              flag_dram, flag_dram)]

        def node_rows(table, g):
            return table.rearrange("(k p) f -> p k f", p=P)[:, bass.ds(g * GT, GT), :]

        gather_table = [relu_table, src_table, x_table, h_table, x_table, h_table]
        next_table = [None, x_table, h_table, x_table, h_table, None]

        ident = sb("ident", [P, P])
        ones = sb("ones", [P, P])
        W = {n: sb(f"m_{n}", [F, F]) for n in MATRICES}
        row = {n: sb(f"r_{n}", [1, F]) for n in ROWS}
        col = {n: sb(f"c_{n}", [F, 1]) for n in COLUMNS}
        w_edge = sb("w_edge", [AK, F])
        w_edge_parts = sb("w_edge_parts", [AK, F], bf16)
        w_ef_scaled = sb("w_ef_scaled", [F, F])

        x_sb = sb("x_sb", [P, NT, F])
        hidden = sb("hidden", [P, NP])
        h_sb = hidden[:, 0:NT * F].rearrange("p (k f) -> p k f", f=F)
        node_feat = hidden[0:F, :]
        end_row = sb("end_row", [P, NT], i32)
        dst_row = sb("dst_row", [P, NT], i32)
        first_rank = sb("first_rank", [1, CN], i32)
        deg, has, rdeg = sb("deg", [P, NT]), sb("has", [P, NT]), sb("rdeg", [P, NT])

        def of_group(t, g):
            return t[:, bass.ds(g * GT, GT)]

        area = sb("area", [P, max(NT * 2 * F, 2 * RING * (TE + CH * F))])
        ends = area[:, 0:NT * 2 * F].rearrange("p (k f) -> p k f", f=2 * F)

        def parts_of(tensor):
            used = [0]

            def part(parts, width):
                used[0] += width
                assert used[0] <= tensor.shape[1], (used[0], tensor.shape)
                return tensor[0:parts, used[0] - width:used[0]]
            return part

        ring = parts_of(area)
        src_rows = ring(P, RING * CH * F).rearrange("p (s c f) -> p s c f", s=RING, c=CH)
        sum_ring = ring(F, RING * TE)
        num_ring = ring(F, RING * TE)
        dst_rows = ring(P, RING * CH * F).rearrange("p (s c f) -> p s c f", s=RING, c=CH)
        out_ring = sb("out_ring", [P, RING, CH, 2 * F])
        idx_src = [sb(f"idx_src{s}", [P, CH], i32) for s in range(RING)]
        ranks = sb("ranks", [P, RING, TE], i8)
        flags = sb("flags", [F, RING, TE], i8)
        attr = sb("attr", [AK, RING, TE], bf16)
        dump = sb("dump", [F, GC])
        relu_dump = sb("relu_dump", [F, TE])

        second = sb("second", [P, 7680])
        soft = parts_of(second)
        max_ring = soft(F, 1 + RING * TE)
        decay = soft(F, 2 * TE).rearrange("p (b e) -> p b e", b=2)
        weight = soft(F, 2 * TE).rearrange("p (b e) -> p b e", b=2)
        weighted = soft(F, 2 * TE).rearrange("p (b e) -> p b e", b=2)
        message = parts_of(second)
        h_ring = message(F, 2 * TE).rearrange("p (b e) -> p b e", b=2)
        msg_ring = message(F, RING * TE).rearrange("p (b e) -> p b e", b=RING)
        rank_hot = message(P, 2 * TE).rearrange("p (b e) -> p b e", b=2)
        nodes = parts_of(second)
        grp, xg, res, sq, ng, dg = [nodes(P, GT * F).rearrange("p (k f) -> p k f", f=F) for _ in range(6)]
        fa, fx = nodes(F, GC), nodes(F, GC)

        first = parts_of(area)
        seq_now, seq_before, seq_int = [first(P, SEQ).bitcast(i32) for _ in range(3)]
        before_int, started = first(P, CN).bitcast(i32), first(1, CN)
        running = sb("running", [1, CN])
        tri = sb("tri", [P, P])
        attr_bf = [first(P, EP * EDGE_DIM // P // 2).bitcast(bf16) for _ in range(PARTS)]
        split = parts_of(second)
        attr_f, attr_rest = split(P, EP * EDGE_DIM // P), split(P, EP * EDGE_DIM // P)
        w_rest = sb("w_rest", [AK, F])
        w_part = [sb(f"w_part{i}", [AK, F], bf16) for i in range(PARTS)]
        cols_lo, cols_hi = sb("cols_lo", [P, CN], bf16), sb("cols_hi", [P, CN], bf16)
        starts = sb("starts", [P, CN], bf16)
        tri_bf, ones_bf = sb("tri_bf", [P, P], bf16), sb("ones_bf", [P, 1], bf16)
        iota_lo, iota_hi = sb("iota_lo", [P, P, HC], bf16), sb("iota_hi", [P, NT, HC], bf16)
        iota_p, node_number = sb("iota_p", [P, 1]), sb("node_number", [P, NT])
        rank8 = sb("rank8", [P, CB, P], i8)
        others, all_with = sb("others", [P, NT]), sb("all_with", [P, 1])
        flag8 = sb("flag8", [P, 2, SEQ], i8)
        hot_lo = sb("hot_lo", [P, 2, P, HC], bf16)
        hot_hi = sb("hot_hi", [P, 2, NT, HC], bf16)
        end_f, end_i, end_j = sb("end_f", [P, NT]), sb("end_i", [P, NT], i32), sb("end_j", [P, NT], i32)
        total, before = sb("total", [P, NT]), sb("before", [P, NT])

        ef_sum, ef_sq = sb("ef_sum", [F, ET]), sb("ef_sq", [F, ET])
        mg_sum, mg_sq = sb("mg_sum", [F, ET]), sb("mg_sq", [F, ET])
        nd_sum, nd_sq = sb("nd_sum", [F, NG]), sb("nd_sq", [F, NG])
        mu, var, tmp = sb("mu", [F, 1]), sb("var", [F, 1]), sb("tmp", [F, 1])
        s_ef, t_ef = sb("s_ef", [F, 1]), sb("t_ef", [F, 1])
        s_nd, t_nd = sb("s_nd", [F, 1]), sb("t_nd", [F, 1])
        s_mg, t_mg = sb("s_mg", [F, 1]), sb("t_mg", [F, 1])
        msg_bias = sb("msg_bias", [F, 1])
        diag_s, diag_t = sb("diag_s", [F, F]), sb("diag_t", [F, F])
        s_row, t_row = sb("s_row", [P, F]), sb("t_row", [P, F])
        eps = sb("eps", [P, 1])
        mean, rstd = sb("mean", [P, GT]), sb("rstd", [P, GT])

        ps = ctx.enter_context(nc.psum_tensor("ps", [P, 8, 512], f32))

        def bank(b, parts=P, width=512):
            return ps[0:parts, b, 0:width]

        def node_major(b):
            return ps[:, b:b + 2, :].rearrange("p b (k n) -> p (b k) n", n=P)

        def feature_major(b):
            return ps[0:F, b:b + 2, :].rearrange("p b n -> p (b n)")[:, 0:GC]

        weights_landed, x_landed = sem("weights_landed"), sem("x_landed")
        cols_landed, seq_landed = sem("cols_landed"), sem("seq_landed")
        pool_step, consts_made = sem("pool_step"), sem("consts_made")
        dve_step = sem("dve_step")
        flag_made = sem("flag_made")
        attr_in_landed, parts_split = sem("attr_in_landed"), sem("parts_split")
        setup_stored = sem("setup_stored")
        SETUP_STORES = 2 + 2 + 2 * PARTS * PARTS + CB
        ranks_summed, ranks_made = sem("ranks_summed"), sem("ranks_made")
        starts_made = sem("starts_made")
        hot_made, hot_used, deg_counted, deg_made, prefix_summed = (
            sem("hot_made"), sem("hot_used"), sem("deg_counted"), sem("deg_made"), sem("prefix_summed"))
        index_made, relu_made = sem("index_made"), sem("relu_made")
        ef_coefs_made, ef_bias_summed, msg_bias_made = sem("ef_coefs_made"), sem("ef_bias_summed"), sem("msg_bias_made")
        diags_made, rows_spread = sem("diags_made"), sem("rows_spread")
        idx_landed, flags_landed = ring_sems("idx_landed"), ring_sems("flags_landed")
        attr_landed = ring_sems("attr_landed")
        src_gathered = ring_sems("src_gathered")
        window_landed, ranks_landed = ring_sems("window_landed"), ring_sems("ranks_landed")
        sums_stored = ring_sems("sums_stored")
        ends_landed = [sem(f"ends_landed{b}") for b in range(2)]
        ends_ready = sem("ends_ready")
        var_summed, rooted = sem("var_summed"), sem("rooted")
        coef_var_made, coef_rooted = sem("coef_var_made"), sem("coef_rooted")
        gathers_begun = sem("gathers_begun")
        out_stored = sem("out_stored")
        EDGE = "turned summed back copied"
        edge = [sems(f"e{p}", EDGE + {SOFT: " hid hrelu squared maxed scored expd weighed wrapped",
                                      MESSAGE: " hid hrelu squared relued placed"}.get(kind, ""))
                for p, kind in enumerate(PASSES)]
        node = [sems(f"n{p}", "copied mixed normed stored" + (" kept" if p < len(PASSES) - 1 else "")
                     + {SOFT: " prepared turned turned2 copied2 src_made src_kept dst_made dst_kept dst_stored nh_made"
                              " nh_kept nh_squared",
                        MEAN: " prepared turned xcopied"}.get(kind, "") + (" floored expd" if p == 4 else ""))
                for p, kind in enumerate(PASSES)]

        def over_tiles(eng, lead, lag=None):
            lead(0, 0)
            for s in range(RING):
                lead((s + 1) // RING, (s + 1) % RING)
                if lag:
                    lag(0, s)
            with eng.Fori(1, EI - 1) as u:
                for s in range(RING):
                    lead(u + (s + 1) // RING, (s + 1) % RING)
                    if lag:
                        lag(u, s)
            for s in range(RING):
                if s + 1 < RING:
                    lead(EI - 1, s + 1)
                if lag:
                    lag(EI - 1, s)

        def tile_before(step, u, s):
            if s:
                step(u, s - 1)
            elif not isinstance(u, int) or u:
                step(u - 1, RING - 1)

        def over_groups(eng, lead, lag, chain=None, steps=0):
            lead(0)
            lead(1)
            lag(0)
            start = chain.base + chain.n - steps if chain else 0
            with eng.Fori(1, NG - 1) as g:
                if chain:
                    chain.base, chain.n = g * steps + start, 0
                lead(g + 1)
                lag(g)
                assert not chain or chain.n == steps, chain.n
            if chain:
                chain.base, chain.n = start + steps * (NG - 1), 0
            lag(NG - 1)

        def wait_for_tables(eng, p):
            if p:
                eng.wait_ge(node[p - 1]["stored"], 16 * NG)
            if PASSES[p] == MESSAGE:
                eng.wait_ge(node[p - 1]["dst_stored"], 16 * NT)

        def norms_before(p):
            return NG * {0: 0, 1: 1, 3: 2, 5: 3}[p]

        def nothing(*where):
            pass

        block = ctx.enter_context(nc.Block())

        @block.sync
        def _(sp):
            sp.dma_start(x_sb[:, 0:FULL, :], x_in[0:FULL * P, :].rearrange("(k p) f -> p k f", p=P)).then_inc(x_landed, 16)
            sp.wait_ge(consts_made, 1)
            sp.dma_start(x_sb[0:REST, FULL, :], x_in[FULL * P:n_nodes, :]).then_inc(x_landed, 16)
            sp.dma_start(seq_now, dst_seq_in[1:1 + EP].rearrange("(p j) -> p j", p=P)).then_inc(seq_landed, 16)
            sp.dma_start(seq_before, dst_seq_in[0:EP].rearrange("(p j) -> p j", p=P)).then_inc(seq_landed, 16)
            sp.dma_start(seq_int, dst_cols_in).then_inc(cols_landed, 16)
            sp.dma_start(before_int, dst_before_in).then_inc(cols_landed, 16)
            sp.dma_start(w_edge[:, :], w_edge_in).then_inc(attr_in_landed, 16)
            sp.dma_start(attr_f, attr_in.rearrange("(p j) -> p j", p=P)).then_inc(attr_in_landed, 16)
            for k, n in enumerate(MATRICES):
                sp.dma_start(W[n][:, :], matrices_in[k, :, :]).then_inc(weights_landed, 16)
            for k, n in enumerate(ROWS):
                sp.dma_start(row[n][:, :], rows_in[k:k + 1, :]).then_inc(weights_landed, 16)
            for k, n in enumerate(COLUMNS):
                sp.dma_start(col[n][:, :], columns_in[k, :, :]).then_inc(weights_landed, 16)
            sp.wait_ge(relu_made, 1)
            sp.dma_start(relu_table.rearrange("(k p) f -> p k f", p=P), hidden[:, 0:NT * F].rearrange(
                "p (k f) -> p k f", f=F)).then_inc(setup_stored, 16)
            sp.wait_ge(consts_made, 2)
            sp.dma_start(dst_table[NP:NP + P, :], s_row[:, :]).then_inc(setup_stored, 16)
            sp.wait_ge(flag_made, 2)
            for d, b in ((flag_dram, 0), (sign_dram, 1)):
                sp.dma_start(d.rearrange("(p j) -> p j", p=P), flag8[:, b, :]).then_inc(setup_stored, 16)
            sp.wait_ge(ranks_made, 1)
            for b in range(CB):
                m = min(P, CN - b * P)
                sp.dma_start(rank_dram[b * P * P:(b * P + m) * P].rearrange("(c e) -> c e", e=P), rank8[0:m, b, :])\
                  .then_inc(setup_stored, 16)
            sp.wait_ge(parts_split, 2)
            for i in range(PARTS):
                for j in range(PARTS):
                    at = (i * PARTS + j) * EDGE_DIM
                    sp.dma_start(attr_parts[at:at + EDGE_DIM, :].rearrange("a e -> (a e)").rearrange("(p j) -> p j", p=P),
                                 attr_bf[i]).then_inc(setup_stored, 16)
                    sp.dma_start(w_edge_parts[at:at + EDGE_DIM, :], w_part[j][at:at + EDGE_DIM, :]).then_inc(setup_stored, 16)
            sp.wait_ge(setup_stored, 16 * SETUP_STORES)
            ranks_t = rank_dram.rearrange("(t e) -> t e", e=TE)

            for p, kind in enumerate(PASSES):
                e, n = edge[p], node[p]
                if kind == MESSAGE:
                    wait_for_tables(sp, p)

                def load(u, s):
                    use, t = p * EI + u, u * RING + s
                    one = bass.ds(t, 1)
                    if kind == MESSAGE:
                        _, firsts = nc.values_load_multi_w_load_instructions(
                            first_rank[0:1, bass.ds(t * CH, CH)], engines=[mybir.EngineType.SP], min_val=0, max_val=NP,
                            skip_runtime_bounds_check_because="a count of runs, of which there are NP at most")
                    if kind != MEAN:
                        wait(sp, e["hid"], t - RING + 1)
                    wait(sp, src_gathered[s], use * 16 * CH)
                    sp.dma_start(idx_src[s][:, :], src_in[one, :, :].rearrange("a p c -> (a p) c")).then_inc(idx_landed[s], 16)
                    if kind == MESSAGE:
                        wait(sp, e["turned"], t - RING + 1)
                        sp.dma_start(ranks[:, s, :], ranks_t[one, :].to_broadcast([P, TE])).then_inc(ranks_landed[s], 16)
                        for c in range(CH):
                            sp.dma_start(dst_rows[:, s, c, :], dst_table[bass.ds(firsts[c], P), :]).then_inc(window_landed[s], 16)
                    if kind != MEAN:
                        sp.dma_start(attr[:, s, :], attr_parts[:, bass.ds(t * TE, TE)]).then_inc(attr_landed[s], 16)
                    wait(sp, e["summed"], t - RING + 1)
                    sp.dma_start(flags[:, s, :], flag_t[p][one, :].to_broadcast([F, TE])).then_inc(flags_landed[s], 16)

                over_tiles(sp, load)

                def store(g):
                    if kind == SOFT:
                        sp.wait_ge(n["src_kept"], g + 1)
                        sp.dma_start(node_rows(src_table, g), xg).then_inc(n["stored"], 16)
                    elif p < len(PASSES) - 1:
                        sp.wait_ge(n["normed"], g + 1)
                        sp.dma_start(node_rows(next_table[p], g), ng).then_inc(n["stored"], 16)
                    else:
                        sp.wait_ge(n["normed"], g + 1)
                        if isinstance(g, int) and g == NG - 1:
                            done = g * GT
                            if FULL > done:
                                sp.dma_start(out[done * P:FULL * P, :].rearrange("(k p) f -> p k f", p=P),
                                             ng[:, 0:FULL - done, :]).then_inc(n["stored"], 16)
                            sp.dma_start(out[FULL * P:n_nodes, :], ng[0:REST, FULL - done, :]).then_inc(out_stored, 16)
                        else:
                            sp.dma_start(node_rows_out(g), ng).then_inc(n["stored"], 16)

                def node_rows_out(g):
                    return out[bass.ds(g * GC, GC), :].rearrange("(k p) f -> p k f", p=P)

                over_groups(sp, nothing, store)
            sp.wait_ge(node[-1]["stored"], 16 * (NG - (FULL == (NG - 1) * GT)))
            sp.wait_ge(out_stored, 16)

        @block.gpsimd
        def _(pool):
            chain = Chain(pool, pool_step)
            nc.gpsimd.memset(x_sb[:, FULL:NT, :], 0.0).then_inc(consts_made, 1)
            nc.gpsimd.memset(ones[:, :], 1.0)
            nc.gpsimd.memset(eps[:, :], EPS)
            nc.gpsimd.memset(tri[:, :], 1.0)
            chain.do(nc.gpsimd.memset(ident[:, :], 0.0))
            nc.gpsimd.affine_select(out=ident[:, :], in_=ident[:, :], compare_op=ALU.not_equal, fill=1.0, base=0,
                                    pattern=[[-1, P]], channel_multiplier=1)
            nc.gpsimd.affine_select(out=tri[:, :], in_=tri[:, :], compare_op=ALU.is_ge, fill=0.0, base=0,
                                    pattern=[[1, P]], channel_multiplier=-1)
            def iota(t, pattern, step):
                return nc.gpsimd.iota(t, pattern=pattern, base=0, channel_multiplier=step,
                                      allow_small_or_imprecise_dtypes=True)

            iota(iota_lo[:, :, :], [[1, P], [0, HC]], 0)
            iota(iota_p[:, :], [[0, 1]], 1)
            iota(node_number[:, :], [[P, NT]], 1)
            nc.gpsimd.memset(ones_bf[:, :], 1.0)
            nc.gpsimd.memset(s_row[:, :], 0.0)
            nc.gpsimd.memset(tri_bf[:, :], 1.0)
            chain.do(iota(iota_hi[:, :, :], [[1, NT], [0, HC]], 0))
            chain.do(nc.gpsimd.affine_select(out=tri_bf[:, :], in_=tri_bf[:, :], compare_op=ALU.is_ge, fill=0.0, base=0,
                                             pattern=[[1, P]], channel_multiplier=-1))
            nc.gpsimd.memset(tri_bf[0:1, :], 0.0).then_inc(consts_made, 1)

            pool.wait_ge(attr_in_landed, 32)
            chain.do(nc.gpsimd.tensor_copy(attr_bf[0], attr_f))
            chain.do(nc.gpsimd.tensor_tensor(attr_rest, attr_f, attr_bf[0], ALU.subtract))
            chain.do(nc.gpsimd.tensor_copy(attr_bf[1], attr_rest))
            chain.do(nc.gpsimd.tensor_tensor(attr_rest, attr_rest, attr_bf[1], ALU.subtract))
            nc.gpsimd.tensor_copy(attr_bf[2], attr_rest).then_inc(parts_split, 1)

            for p, kind in enumerate(PASSES):
                e, n = edge[p], node[p]
                if p == 0:
                    pool.wait_ge(setup_stored, 16 * SETUP_STORES)
                    pool.wait_ge(index_made, 1)
                wait_for_tables(pool, p)

                def gather(u, s):
                    use, t = p * EI + u, u * RING + s
                    wait(pool, idx_landed[s], (use + 1) * 16)
                    wait(pool, e["turned"], t - RING + 1)
                    pool.sem_inc(gathers_begun, 1)
                    for c in range(CH):
                        pool.indirect_dma_start(out=src_rows[:, s, c, :], out_offset=None, in_=gather_table[p],
                                                in_offset=bass.IndirectOffsetOnAxis(ap=idx_src[s][:, c:c + 1], axis=0))\
                            .then_inc(src_gathered[s], 16)

                over_tiles(pool, gather)

                def ends_of(g):
                    groups = p * len(range(g % 2, NG, 2)) + g // 2 + 1
                    pool.wait_ge(ends_landed[g % 2], 16 * GT * groups)
                    pool.sem_inc(ends_ready, 1)

                for s in range(RING):
                    pool.wait_ge(sums_stored[s], 16 * EI * (p + 1))
                for g in range(NG):
                    for k in range(g * GT, (g + 1) * GT):
                        wide = 2 * F if kind == SOFT else F
                        pool.indirect_dma_start(out=ends[:, k, 0:wide], out_offset=None,
                                                in_=soft_sums if kind == SOFT else sums,
                                                in_offset=bass.IndirectOffsetOnAxis(ap=end_row[:, k:k + 1], axis=0))\
                            .then_inc(ends_landed[g % 2], 16)
                    if g:
                        ends_of(g - 1)
                ends_of(NG - 1)
                if kind == SOFT:
                    for g in range(NG):
                        pool.wait_ge(n["dst_kept"], g + 1)
                        for k in range(GT):
                            at = dst_row[:, g * GT + k:g * GT + k + 1]
                            pool.indirect_dma_start(out=dst_table, out_offset=bass.IndirectOffsetOnAxis(ap=at, axis=0),
                                                    in_=dg[:, k, :], in_offset=None).then_inc(n["dst_stored"], 16)

        @block.tensor
        def _(pe):
            pe.wait_ge(consts_made, 2)
            pe.wait_ge(weights_landed, 16 * (len(MATRICES) + len(ROWS) + len(COLUMNS)))
            pe.wait_ge(starts_made, 1)
            for b in range(CB):
                m = min(P, CN - b * P)
                nc.tensor.matmul(ps[0:m, 4 + b // 4, (b % 4) * P:(b % 4 + 1) * P], starts[:, b * P:b * P + m], tri_bf[:, :],
                                 start=True, stop=True)
            for h in range(2):
                last = nc.tensor.matmul(bank(2 + h, 1, CN // 2), ones_bf[:, :], starts[:, h * CN // 2:(h + 1) * CN // 2],
                                        start=True, stop=True)
            last.then_inc(ranks_summed, 1)

            def count(number, b, start=False, stop=False):
                pe.wait_ge(hot_made, number + 1)
                for c in range(HC):
                    last = nc.tensor.matmul(bank(0, P, NT), hot_lo[:, b, :, c], hot_hi[:, b, :, c],
                                            start=start and c == 0, stop=stop and c == HC - 1)
                return last

            count(0, 0, start=True).then_inc(hot_used, 1)
            count(1, 1).then_inc(hot_used, 1)
            with pe.Fori(1, HI - 1) as i:
                count(2 * i, 0).then_inc(hot_used, 1)
                count(2 * i + 1, 1).then_inc(hot_used, 1)
            count(2 * HI - 2, 0).then_inc(hot_used, 1)
            last = count(2 * HI - 1, 1, stop=True)
            last.then_inc(deg_counted, 1)
            pe.wait_ge(deg_made, 1)
            pe.wait_ge(ranks_made, 1)
            nc.tensor.matmul(bank(1, P, NT), tri[:, :], deg[:, :], start=True, stop=True)
            nc.tensor.matmul(bank(2, P, NT), ones[:, :], deg[:, :], start=True, stop=True)
            nc.tensor.matmul(bank(3, P, NT), tri[:, :], has[:, :], start=True, stop=True)
            nc.tensor.matmul(bank(4, P, NT), ones[:, :], has[:, :], start=True, stop=True).then_inc(prefix_summed, 1)
            pe.wait_ge(setup_stored, 16 * SETUP_STORES)

            for p, kind in enumerate(PASSES):
                e, n = edge[p], node[p]

                def project(u, s):
                    t = u * RING + s
                    wait(pe, attr_landed[s], (p * EI + u + 1) * 16)
                    wait(pe, e["hrelu"], t - 1)
                    nc.tensor.matmul(bank(6 + s % 2, F), w_edge_parts[:, :], attr[:, s, :], start=True, stop=True)\
                      .then_inc(e["hid"], 1)

                def turn(u, s):
                    t = u * RING + s
                    wait(pe, src_gathered[s], (p * EI + u + 1) * 16 * CH)
                    wait(pe, e["weighed"] if kind == SOFT else e["summed"], t - 1)
                    for c in range(CH):
                        last = nc.tensor.transpose(ps[0:F, s % 2, c * P:(c + 1) * P], src_rows[:, s, c, :], ident[:, :])
                    last.then_inc(e["turned"], 1)

                def score(u, s):
                    t = u * RING + s
                    wait(pe, e["hrelu"], t + 1)
                    wait(pe, e["relued"], t - 1)
                    nc.tensor.matmul(bank(s % 2, F), w_ef_scaled[:, :], h_ring[:, s % 2, :], start=True, stop=False)
                    wait(pe, src_gathered[s], (p * EI + u + 1) * 16 * CH)
                    wait(pe, window_landed[s], (u + 1) * 16 * CH)
                    wait(pe, e["placed"], t + 1)
                    for c in range(CH):
                        at = slice(c * P, (c + 1) * P)
                        nc.tensor.matmul(ps[0:F, s % 2, at], src_rows[:, s, c, :], ident[:, :], start=False, stop=False)
                        last = nc.tensor.matmul(ps[0:F, s % 2, at], dst_rows[:, s, c, :], rank_hot[:, s % 2, at],
                                                start=False, stop=c == CH - 1)
                    last.then_inc(e["turned"], 1)

                def turn_back(u, s):
                    t = u * RING + s
                    wait(pe, e["summed"], t + 1)
                    wait(pe, e["copied"], t - 1)
                    for r, b in ((sum_ring, 2), (num_ring, 4))[0:2 if kind == SOFT else 1]:
                        for c in range(CH):
                            last = nc.tensor.transpose(ps[:, b + s % 2, c * F:(c + 1) * F],
                                                       r[:, (s * CH + c) * P:(s * CH + c + 1) * P], ident[0:F, 0:F])
                    last.then_inc(e["back"], 1)

                def turn_and_project(u, s):
                    turn(u, s)
                    project(u, s)

                def score_and_turn_back(u, s):
                    score(u, s)
                    tile_before(turn_back, u, s)

                if kind == SOFT:
                    over_tiles(pe, turn_and_project, lambda u, s: tile_before(turn_back, u, s))
                    turn_back(EI - 1, RING - 1)
                elif kind == MESSAGE:
                    pe.wait_ge(ef_coefs_made, 1)
                    nc.tensor.matmul(bank(2, F, 1), W["W_ef"][:, :], t_ef[:, :], start=True, stop=True)\
                      .then_inc(ef_bias_summed, 1)
                    over_tiles(pe, project, score_and_turn_back)
                    turn_back(EI - 1, RING - 1)
                    pe.wait_ge(diags_made, 1)
                    pe.wait_ge(e["copied"], ET)
                    nc.tensor.matmul(bank(2, P, F), ones[0:F, :], diag_s[:, :], start=True, stop=True)
                    nc.tensor.matmul(bank(3, P, F), ones[0:F, :], diag_t[:, :], start=True, stop=True)\
                      .then_inc(rows_spread, 1)
                else:
                    over_tiles(pe, turn, turn_back)

                left = {0: "W0", 2: "W2l1", 3: "W2l2", 4: "W3l1", 5: "W3l2"}.get(p)
                right = {2: "W2r1", 3: "W2r2", 4: "W3r1", 5: "W3r2"}.get(p)
                bias = {0: "b0", 2: "b21", 3: "b22", 4: "b31", 5: "b32"}.get(p)

                def turn_nodes(g):
                    wait(pe, n["prepared"], g + 1)
                    wait(pe, n["copied"], g)
                    for k in range(GT):
                        last = nc.tensor.transpose(feature_major(0)[:, k * P:(k + 1) * P], grp[:, k, :], ident[:, :])
                    if right:
                        pe.wait_ge(n["xcopied"], g + 1)
                        for k in range(GT):
                            last = nc.tensor.transpose(feature_major(2)[:, k * P:(k + 1) * P], xg[:, k, :], ident[:, :])
                    last.then_inc(n["turned"], 1)

                def mix(g):
                    pe.wait_ge(n["copied"], g + 1)
                    wait(pe, n["normed"], g)
                    if kind == SOFT:
                        wait(pe, n["nh_kept"], g)
                    for k in range(GT):
                        o = node_major(4)[:, k, 0:F]
                        nc.tensor.matmul(o, fa[:, k * P:(k + 1) * P], W[left][:, :], start=True, stop=False)
                        if right:
                            nc.tensor.matmul(o, fx[:, k * P:(k + 1) * P], W[right][:, :], start=False, stop=False)
                        last = nc.tensor.matmul(o, ones[0:1, :], row[bias][:, :], start=False, stop=True)
                    last.then_inc(n["mixed"], 1)

                def project_nodes(g):
                    mix(g)
                    pe.wait_ge(n["normed"], g + 1)
                    wait(pe, n["copied2"], g)
                    for k in range(GT):
                        last = nc.tensor.transpose(feature_major(2)[:, k * P:(k + 1) * P], ng[:, k, :], ident[:, :])
                    last.then_inc(n["turned2"], 1)
                    pe.wait_ge(n["copied2"], g + 1)
                    wait(pe, n["dst_kept"], g)
                    for k in range(GT):
                        last = nc.tensor.matmul(node_major(6)[:, k, 0:F], fx[:, k * P:(k + 1) * P], W["W_src"][:, :],
                                                start=True, stop=True)
                    last.then_inc(n["src_made"], 1)
                    for c, w in ((0, 512), (512, GC - 512)):
                        last = nc.tensor.matmul(feature_major(4)[:, c:c + w], W["W_node"][:, :], fx[:, c:c + w],
                                                start=True, stop=True)
                    last.then_inc(n["nh_made"], 1)
                    pe.wait_ge(n["src_kept"], g + 1)
                    for k in range(GT):
                        last = nc.tensor.matmul(node_major(6)[:, k, 0:F], fx[:, k * P:(k + 1) * P], W["W_dst"][:, :],
                                                start=True, stop=True)
                    last.then_inc(n["dst_made"], 1)

                def turn_features(g):
                    pe.wait_ge(n["copied"], g + 1)
                    wait(pe, n["normed"], g)
                    for k in range(GT):
                        last = nc.tensor.transpose(node_major(4)[:, k, 0:F], fx[:, k * P:(k + 1) * P], ident[0:F, 0:F])
                    last.then_inc(n["mixed"], 1)

                if kind == SOFT:
                    over_groups(pe, turn_nodes, project_nodes)
                elif kind == MESSAGE:
                    over_groups(pe, nothing, turn_features)
                else:
                    over_groups(pe, turn_nodes, mix)

        @block.scalar
        def _(act):
            act.wait_ge(consts_made, 2)
            act.wait_ge(weights_landed, 16 * (len(MATRICES) + len(ROWS) + len(COLUMNS)))

            def coef_root(number):
                act.wait_ge(coef_var_made, number)
                nc.scalar.activation(var[:, :], var[:, :], ACT.Sqrt, bias=eps[0:F, :]).then_inc(coef_rooted, 1)

            for p, kind in enumerate(PASSES):
                e, n = edge[p], node[p]

                wait_for_tables(act, p)

                def valid_edges(u, s):
                    return max(0, min(TE, n_edges - (u * RING + s) * TE)) if isinstance(u, int) else TE

                def relu_and_stats(o, i, bias, total, squares, t, v, done, squared):
                    wait(act, squared, t)
                    if v < TE:
                        last = nc.scalar.activation(o[:, v:TE], i[:, v:TE], ACT.Relu, bias=bias)
                    if v:
                        last = nc.scalar.activation(o[:, 0:v], i[:, 0:v], ACT.Relu, bias=bias, accum_out=total[:, bass.ds(t, 1)])
                    last.then_inc(done, 1)
                    act.wait_ge(done, t + 1)
                    if v:
                        nc.scalar.activation(dump[:, 0:v], o[:, 0:v], ACT.Square, accum_out=squares[:, bass.ds(t, 1)])\
                          .then_inc(squared, 1)
                    else:
                        act.sem_inc(squared, 1)

                def copy_back(u, s):
                    use, t = p * EI + u, u * RING + s
                    wait(act, e["back"], t + 1)
                    wait(act, sums_stored[s], use * 16)
                    if kind == SOFT:
                        for half, b in ((0, 2), (1, 4)):
                            last = nc.scalar.activation(out_ring[:, s, :, half * F:(half + 1) * F],
                                                        bank(b + s % 2, P, CH * F).rearrange("p (c f) -> p c f", f=F), ACT.Copy)
                        last.then_inc(e["copied"], 1)
                        act.wait_ge(e["copied"], t + 1)
                        act.dma_start(soft_sums_t[bass.ds(t, 1), :, :].rearrange("a p n -> (a p) n"),
                                      out_ring[:, s, :, :].rearrange("p c f -> p (c f)")).then_inc(sums_stored[s], 16)
                    else:
                        o = out_ring[:, s, 0:CH // 2, :].rearrange("p c f -> p (c f)")
                        nc.scalar.activation(o, bank(2 + s % 2, P, CH * F), ACT.Copy).then_inc(e["copied"], 1)
                        act.wait_ge(e["copied"], t + 1)
                        act.dma_start(sums_t[bass.ds(t, 1), :, :].rearrange("a p n -> (a p) n"), o).then_inc(sums_stored[s], 16)

                def soften(u, s):
                    t = u * RING + s
                    wait(act, e["hid"], t + 1)
                    relu_and_stats(relu_dump, bank(6 + s % 2, F), col["b_edge"][:, :], ef_sum, ef_sq, t, valid_edges(u, s),
                                   e["hrelu"], e["squared"])
                    wait(act, e["scored"], t + 1)
                    nc.scalar.activation(decay[:, s % 2, :], decay[:, s % 2, :], ACT.Exp)
                    nc.scalar.activation(weight[:, s % 2, :], weight[:, s % 2, :], ACT.Exp).then_inc(e["expd"], 1)

                def relu_features(u, s):
                    t = u * RING + s
                    wait(act, e["hid"], t + 1)
                    wait(act, e["turned"], t - 1)
                    nc.scalar.activation(h_ring[:, s % 2, :], bank(6 + s % 2, F), ACT.Relu, bias=col["b_edge"][:, :])\
                      .then_inc(e["hrelu"], 1)

                def relu_message(u, s):
                    t = u * RING + s
                    wait(act, e["turned"], t + 1)
                    wait(act, e["summed"], t - RING + 1)
                    relu_and_stats(msg_ring[:, s, :], bank(s % 2, F), msg_bias[:, :], mg_sum, mg_sq, t, valid_edges(u, s),
                                   e["relued"], e["squared"])
                    tile_before(copy_back, u, s)

                if kind == SOFT:
                    over_tiles(act, soften, lambda u, s: tile_before(copy_back, u, s))
                    copy_back(EI - 1, RING - 1)
                elif kind == MESSAGE:
                    coef_root(1)
                    coef_root(2)
                    act.wait_ge(msg_bias_made, 1)
                    over_tiles(act, relu_features, relu_message)
                    copy_back(EI - 1, RING - 1)
                    coef_root(3)
                else:
                    over_tiles(act, nothing, copy_back)

                source = {2: x_sb, 3: h_sb, 4: x_sb, 5: h_sb}.get(p)
                kept_in = {0: x_sb, 1: x_sb, 2: h_sb, 3: x_sb, 4: h_sb}[p] if p < len(PASSES) - 1 else None

                def keep(g):
                    if p not in (2, 4):
                        act.wait_ge(var_summed, norms_before(p) + g + 1)
                        nc.scalar.activation(rstd[:, :], rstd[:, :], ACT.Sqrt, bias=eps[:, :], scale=1.0 / F)\
                          .then_inc(rooted, 1)
                    if kept_in is not None:
                        act.wait_ge(n["normed"], g + 1)
                        nc.scalar.activation(of_group(kept_in, g), ng, ACT.Copy).then_inc(n["kept"], 1)

                def copy_turned(g):
                    if source is not None:
                        wait(act, n["turned"], g)
                        nc.scalar.activation(xg, of_group(source, g), ACT.Copy).then_inc(n["xcopied"], 1)
                    act.wait_ge(n["turned"], g + 1)
                    wait(act, n["mixed"], g)
                    if source is not None:
                        nc.scalar.activation(fx, feature_major(2), ACT.Copy)
                    nc.scalar.activation(fa, feature_major(0), ACT.Copy).then_inc(n["copied"], 1)

                def exp_and_keep(g):
                    act.wait_ge(n["floored"], g + 1)
                    nc.scalar.activation(sq, sq, ACT.Exp).then_inc(n["expd"], 1)
                    keep(g)

                def node_features(g):
                    keep(g)
                    act.wait_ge(n["turned2"], g + 1)
                    wait(act, n["dst_made"], g)
                    nc.scalar.activation(fx, feature_major(2), ACT.Copy).then_inc(n["copied2"], 1)
                    act.wait_ge(n["src_made"], g + 1)
                    wait(act, n["stored"], g * 16)
                    nc.scalar.activation(xg, node_major(6)[:, 0:GT, 0:F], ACT.Copy).then_inc(n["src_kept"], 1)
                    act.wait_ge(n["nh_made"], g + 1)
                    v = min(GC, n_nodes - g * GC) if isinstance(g, int) else GC
                    nf = node_feat[:, bass.ds(g * GC, GC)]
                    if v < GC:
                        nc.scalar.activation(nf[:, v:GC], feature_major(4)[:, v:GC], ACT.Relu, bias=col["b_node"][:, :])
                    nc.scalar.activation(nf[:, 0:v], feature_major(4)[:, 0:v], ACT.Relu, bias=col["b_node"][:, :],
                                         accum_out=nd_sum[:, bass.ds(g, 1)]).then_inc(n["nh_kept"], 1)
                    act.wait_ge(n["nh_kept"], g + 1)
                    nc.scalar.activation(dump[:, 0:v], nf[:, 0:v], ACT.Square, accum_out=nd_sq[:, bass.ds(g, 1)])\
                      .then_inc(n["nh_squared"], 1)

                def norm_features(g):
                    wait(act, n["mixed"], g)
                    nc.scalar.activation(fx, node_feat[:, bass.ds(g * GC, GC)], ACT.Identity, bias=t_nd[:, :], scale=s_nd[:, :])\
                      .then_inc(n["copied"], 1)

                if kind == SOFT:
                    over_groups(act, copy_turned, node_features)
                elif kind == MESSAGE:
                    over_groups(act, norm_features, keep)
                elif p == 4:
                    over_groups(act, copy_turned, exp_and_keep)
                else:
                    over_groups(act, copy_turned, keep)

        @block.vector
        def _(dve):
            v = nc.vector
            chain = Chain(dve, dve_step)

            def every(t, g):
                return of_group(t, g).unsqueeze(2).to_broadcast([P, GT, F])

            def by_feature(r):
                return r[:, :].unsqueeze(1).to_broadcast([P, GT, F])

            dve.wait_ge(x_landed, 32)
            v.tensor_scalar(h_sb, x_sb[:, :, :], 0.0, MSG_EPS, ALU.max, ALU.add).then_inc(relu_made, 1)
            dve.wait_ge(seq_landed, 32)
            v.tensor_tensor(flag8[:, 0, :], seq_now, seq_before, ALU.is_equal).then_inc(flag_made, 1)
            dve.wait_ge(flag_made, 1)
            v.tensor_scalar(flag8[:, 1, :], flag8[:, 0, :], 2.0, -1.0, ALU.mult, ALU.add).then_inc(flag_made, 1)
            for t in (ef_sum, ef_sq, mg_sum, mg_sq):
                v.memset(t[:, :], 0.0)
            dve.wait_ge(cols_landed, 32)
            v.tensor_tensor(starts[:, :], seq_int, before_int, ALU.not_equal).then_inc(starts_made, 1)
            chain.do(v.tensor_scalar(seq_before, seq_int, 7, None, ALU.arith_shift_right))
            chain.do(v.tensor_copy(cols_hi[:, :], seq_before))
            chain.do(v.tensor_scalar(seq_before, seq_int, P - 1, None, ALU.bitwise_and))
            chain.do(v.tensor_copy(cols_lo[:, :], seq_before))
            dve.wait_ge(consts_made, 2)

            def hot(i, b, number):
                wait(dve, hot_used, number - 1)
                at = bass.ds(i * 2 * HC + b * HC, HC)
                v.tensor_tensor(hot_hi[:, b, :, :], cols_hi[:, at].unsqueeze(1).to_broadcast([P, NT, HC]),
                                iota_hi[:, :, :], ALU.is_equal)
                v.tensor_tensor(hot_lo[:, b, :, :], cols_lo[:, at].unsqueeze(1).to_broadcast([P, P, HC]),
                                iota_lo[:, :, :], ALU.is_equal).then_inc(hot_made, 1)

            for b in range(2):
                hot(0, b, b)
            with dve.Fori(1, HI) as i:
                for b in range(2):
                    hot(i, b, 2 * i + b)
            dve.wait_ge(attr_in_landed, 32)
            chain.do(v.tensor_copy(w_part[0][:, :], w_edge[:, :]))
            chain.do(v.tensor_tensor(w_rest[:, :], w_edge[:, :], w_part[0][:, :], ALU.subtract))
            chain.do(v.tensor_copy(w_part[1][:, :], w_rest[:, :]))
            chain.do(v.tensor_tensor(w_rest[:, :], w_rest[:, :], w_part[1][:, :], ALU.subtract))
            v.tensor_copy(w_part[2][:, :], w_rest[:, :]).then_inc(parts_split, 1)
            dve.wait_ge(ranks_summed, 1)
            for b in range(CB):
                m = min(P, CN - b * P)
                v.tensor_copy(rank8[0:m, b, :], ps[0:m, 4 + b // 4, (b % 4) * P:(b % 4 + 1) * P])
            for h in range(2):
                chain.do(v.tensor_copy(started[:, h * CN // 2:(h + 1) * CN // 2], bank(2 + h, 1, CN // 2)))
            now = running[:, :]
            chain.do(v.tensor_tensor_scan(out=now, data0=started, data1=started, initial=0.0, op0=ALU.add, op1=ALU.bypass))
            chain.do(v.tensor_tensor(now, now, started, ALU.subtract))
            chain.do(v.tensor_tensor(now, now, starts[0:1, :], ALU.add))
            chain.do(v.tensor_scalar(now, now, -1.0, None, ALU.add))
            v.tensor_copy(first_rank[:, :], now).then_inc(ranks_made, 1)
            dve.wait_ge(deg_counted, 1)
            chain.do(v.tensor_copy(deg[:, :], bank(0, P, NT)))
            v.tensor_scalar(has[:, :], deg[:, :], 1.0, None, ALU.min).then_inc(deg_made, 1)
            dve.wait_ge(deg_made, 1)
            chain.do(v.tensor_scalar(rdeg[:, :], deg[:, :], 1.0, None, ALU.max))
            chain.do(v.reciprocal(rdeg[:, :], rdeg[:, :]))
            chain.do(v.tensor_tensor(rdeg[:, :], rdeg[:, :], has[:, :], ALU.mult))
            dve.wait_ge(prefix_summed, 1)
            chain.do(v.tensor_copy(total[:, :], bank(2, P, NT)))
            chain.do(v.tensor_tensor_scan(out=before[:, :], data0=total[:, :], data1=total[:, :], initial=0.0,
                                          op0=ALU.add, op1=ALU.bypass))
            chain.do(v.tensor_tensor(before[:, :], before[:, :], total[:, :], ALU.subtract))
            chain.do(v.tensor_tensor(end_f[:, :], before[:, :], bank(1, P, NT), ALU.add))
            chain.do(v.tensor_scalar(end_f[:, :], end_f[:, :], -1.0, 0.0, ALU.add, ALU.max))
            chain.do(v.tensor_copy(end_i[:, :], end_f[:, :]))
            chain.do(v.tensor_scalar(end_j[:, :], end_i[:, :], P - 1, CH // 2, ALU.bitwise_and, ALU.logical_shift_left))
            chain.do(v.tensor_scalar(end_row[:, :], end_i[:, :], 7, CH - 1, ALU.logical_shift_right, ALU.bitwise_and))
            chain.do(v.tensor_tensor(end_j[:, :], end_j[:, :], end_row[:, :], ALU.bitwise_or))
            chain.do(v.tensor_scalar(end_i[:, :], end_i[:, :], 9, 9, ALU.logical_shift_right, ALU.logical_shift_left))
            chain.do(v.tensor_tensor(end_row[:, :], end_i[:, :], end_j[:, :], ALU.bitwise_or))
            chain.do(v.tensor_copy(total[:, :], bank(4, P, NT)))
            chain.do(v.tensor_tensor_scan(out=before[:, :], data0=total[:, :], data1=total[:, :], initial=0.0,
                                          op0=ALU.add, op1=ALU.bypass))
            chain.do(v.tensor_copy(all_with[:, :], before[:, NT - 1:NT]))
            chain.do(v.tensor_tensor(before[:, :], before[:, :], total[:, :], ALU.subtract))
            chain.do(v.tensor_tensor(end_f[:, :], before[:, :], bank(3, P, NT), ALU.add))
            chain.do(v.tensor_tensor(end_f[:, :], end_f[:, :], has[:, :], ALU.subtract))
            chain.do(v.tensor_tensor(others[:, :], node_number[:, :], end_f[:, :], ALU.subtract))
            chain.do(v.tensor_scalar(others[:, :], others[:, :], all_with[:, :], None, ALU.add))
            chain.do(v.tensor_tensor(end_f[:, :], end_f[:, :], others[:, :], ALU.subtract))
            chain.do(v.tensor_tensor(end_f[:, :], end_f[:, :], has[:, :], ALU.mult))
            chain.do(v.tensor_tensor(end_f[:, :], end_f[:, :], others[:, :], ALU.add))
            v.tensor_copy(dst_row[:, :], end_f[:, :]).then_inc(index_made, 1)
            dve.wait_ge(index_made, 1)
            dve.wait_ge(setup_stored, 16 * SETUP_STORES)

            def norm_coefs(number, total, squares, count, g, beta, s, t):
                chain.do(v.reduce_sum(mu[:, :], total, axis=X))
                chain.do(v.reduce_sum(var[:, :], squares, axis=X))
                chain.do(v.tensor_scalar(mu[:, :], mu[:, :], 1.0 / count, None, ALU.mult))
                chain.do(v.tensor_tensor(tmp[:, :], mu[:, :], mu[:, :], ALU.mult))
                chain.do(v.scalar_tensor_tensor(var[:, :], var[:, :], 1.0 / count, tmp[:, :], ALU.mult, ALU.subtract))
                v.tensor_scalar(var[:, :], var[:, :], 0.0, None, ALU.max).then_inc(coef_var_made, 1)
                dve.wait_ge(coef_rooted, number)
                chain.do(v.reciprocal(var[:, :], var[:, :]))
                chain.do(v.tensor_tensor(s[:, :], g[:, :], var[:, :], ALU.mult))
                chain.do(v.tensor_tensor(tmp[:, :], s[:, :], mu[:, :], ALU.mult))
                chain.do(v.tensor_tensor(t[:, :], beta[:, :], tmp[:, :], ALU.subtract))

            for p, kind in enumerate(PASSES):
                e, n = edge[p], node[p]

                wait_for_tables(dve, p)

                def start_from_zero():
                    at = RING * TE - 1
                    chain.do(v.memset(sum_ring[:, at:at + 1], 0.0))
                    if kind == SOFT:
                        chain.do(v.memset(num_ring[:, at:at + 1], 0.0))
                        chain.do(v.memset(max_ring[:, 0:1], 0.0))

                def last_of(r, s):
                    at = s * TE - 1 if s else RING * TE - 1
                    return r[:, at:at + 1]

                def slot(r, s):
                    return r[:, s * TE:(s + 1) * TE]

                def place(u, s):
                    t = u * RING + s
                    wait(dve, ranks_landed[s], (u + 1) * 16)
                    wait(dve, e["turned"], t - 1)
                    v.tensor_scalar(rank_hot[:, s % 2, :], ranks[:, s, :], iota_p[:, :], None, ALU.is_equal)\
                     .then_inc(e["placed"], 1)

                def scan(u, s):
                    t = u * RING + s
                    wait(dve, e["relued"] if kind == MESSAGE else e["turned"], t + 1)
                    wait(dve, flags_landed[s], (p * EI + u + 1) * 16)
                    wait(dve, e["back"], t - RING + 1)
                    wait(dve, e["summed"], t)
                    v.tensor_tensor_scan(out=slot(sum_ring, s), data0=flags[:, s, :],
                                         data1=msg_ring[:, s, :] if kind == MESSAGE else bank(s % 2, F),
                                         initial=last_of(sum_ring, s), op0=ALU.mult, op1=ALU.add).then_inc(e["summed"], 1)

                def running_max(u, s):
                    t, b = u * RING + s, s % 2
                    wait(dve, e["turned"], t + 1)
                    wait(dve, flags_landed[s], (p * EI + u + 1) * 16)
                    if s == 0 and not (isinstance(u, int) and u == 0):
                        v.tensor_copy(max_ring[:, 0:1], max_ring[:, RING * TE:RING * TE + 1]).then_inc(e["wrapped"], 1)
                        dve.wait_ge(e["wrapped"], u)
                    now = max_ring[:, 1 + s * TE:1 + (s + 1) * TE]
                    v.tensor_tensor_scan(out=now, data0=flags[:, s, :], data1=bank(b, F),
                                         initial=max_ring[:, s * TE:s * TE + 1], op0=ALU.mult, op1=ALU.max)\
                     .then_inc(e["maxed"], 1)
                    dve.wait_ge(e["maxed"], 2 * t + 1)
                    v.scalar_tensor_tensor(decay[:, b, :], flags[:, s, :], BIG, max_ring[:, s * TE:(s + 1) * TE],
                                           ALU.mult, ALU.min).then_inc(e["maxed"], 1)
                    dve.wait_ge(e["maxed"], 2 * t + 2)
                    v.tensor_tensor(decay[:, b, :], decay[:, b, :], now, ALU.subtract)
                    v.tensor_tensor(weight[:, b, :], bank(b, F), now, ALU.subtract).then_inc(e["scored"], 1)

                def soft_scan(u, s):
                    t, b = u * RING + s, s % 2
                    dve.wait_ge(e["expd"], t + 1)
                    v.tensor_tensor(weighted[:, b, :], weight[:, b, :], bank(b, F), ALU.mult).then_inc(e["weighed"], 1)
                    wait(dve, e["back"], t - RING + 1)
                    wait(dve, e["summed"], t)
                    v.tensor_tensor_scan(out=slot(sum_ring, s), data0=decay[:, b, :], data1=weight[:, b, :],
                                         initial=last_of(sum_ring, s), op0=ALU.mult, op1=ALU.add)
                    dve.wait_ge(e["weighed"], t + 1)
                    v.tensor_tensor_scan(out=slot(num_ring, s), data0=decay[:, b, :], data1=weighted[:, b, :],
                                         initial=last_of(num_ring, s), op0=ALU.mult, op1=ALU.add).then_inc(e["summed"], 1)

                if kind == MESSAGE:
                    dve.wait_ge(edge[0]["squared"], ET)
                    norm_coefs(1, ef_sum[:, :], ef_sq[:, :], n_edges, col["g_edge"], col["beta_edge"], s_ef, t_ef)
                    v.tensor_scalar(w_ef_scaled[:, :], W["W_ef"][:, :], s_ef[:, :], None, ALU.mult).then_inc(ef_coefs_made, 1)
                    dve.wait_ge(node[0]["nh_squared"], NG)
                    norm_coefs(2, nd_sum[:, :], nd_sq[:, :], n_nodes, col["g_node"], col["beta_node"], s_nd, t_nd)
                    dve.wait_ge(ef_bias_summed, 1)
                    v.tensor_tensor(msg_bias[:, :], bank(2, F, 1), col["b_msg"][:, :], ALU.add).then_inc(msg_bias_made, 1)

                start_from_zero()
                if kind == SOFT:
                    over_tiles(dve, running_max, soft_scan)
                elif kind == MESSAGE:
                    over_tiles(dve, place, scan)
                else:
                    over_tiles(dve, nothing, scan)

                if kind == MESSAGE:
                    dve.wait_ge(e["squared"], ET)
                    norm_coefs(3, mg_sum[:, :], mg_sq[:, :], n_edges, col["g_msg"], col["beta_msg"], s_mg, t_mg)
                    v.tensor_scalar(diag_s[:, :], ident[0:F, 0:F], s_mg[:, :], None, ALU.mult)
                    v.tensor_scalar(diag_t[:, :], ident[0:F, 0:F], t_mg[:, :], None, ALU.mult).then_inc(diags_made, 1)
                    dve.wait_ge(rows_spread, 1)
                    chain.do(v.tensor_copy(s_row[:, :], bank(2, P, F)))
                    chain.do(v.tensor_copy(t_row[:, :], bank(3, P, F)))

                mixed = node_major(4)[:, 0:GT, 0:F]

                def result_free(g):
                    if p < len(PASSES) - 1:
                        wait(dve, n["kept"], g)
                    if kind == SOFT:
                        wait(dve, n["turned2"], g)
                    else:
                        wait(dve, n["stored"], g * 16)

                def layer_norm(g):
                    chain.do(v.reduce_sum(mean[:, :], res, axis=X))
                    chain.do(v.tensor_scalar(mean[:, :], mean[:, :], 1.0 / F, None, ALU.mult))
                    chain.do(v.tensor_tensor(res, res, mean[:, :].unsqueeze(2).to_broadcast([P, GT, F]), ALU.subtract))
                    chain.do(v.tensor_tensor(sq, res, res, ALU.mult))
                    v.reduce_sum(rstd[:, :], sq, axis=X).then_inc(var_summed, 1)
                    dve.wait_ge(rooted, norms_before(p) + g + 1)
                    chain.do(v.reciprocal(rstd[:, :], rstd[:, :]))
                    result_free(g)
                    v.tensor_tensor(ng, res, rstd[:, :].unsqueeze(2).to_broadcast([P, GT, F]), ALU.mult)\
                     .then_inc(n["normed"], 1)

                def soft_prepare(g):
                    dve.wait_ge(ends_ready, p * NG + g + 1)
                    e_g = ends[:, bass.ds(g * GT, GT), :]
                    sum_g, num_g = e_g[:, :, 0:F], e_g[:, :, F:2 * F]
                    chain.do(v.reciprocal(sum_g, sum_g))
                    chain.do(v.tensor_tensor(num_g, num_g, sum_g, ALU.mult))
                    chain.do(v.tensor_tensor(num_g, num_g, every(has, g), ALU.mult))
                    wait(dve, n["turned"], g)
                    v.tensor_tensor(grp, num_g, of_group(x_sb, g), ALU.add).then_inc(n["prepared"], 1)

                def prepare(g):
                    dve.wait_ge(ends_ready, p * NG + g + 1)
                    wait(dve, n["turned"], g)
                    v.tensor_tensor(grp, ends[:, bass.ds(g * GT, GT), 0:F], every(rdeg, g), ALU.mult)\
                     .then_inc(n["prepared"], 1)

                def add_and_norm(g):
                    dve.wait_ge(n["mixed"], g + 1)
                    wait(dve, n["normed"], g)
                    chain.do(v.tensor_tensor(res, mixed, of_group(x_sb, g), ALU.add))
                    layer_norm(g)

                def norm_and_keep(g):
                    add_and_norm(g)
                    dve.wait_ge(n["dst_made"], g + 1)
                    wait(dve, n["dst_stored"], g * 16 * GT)
                    v.tensor_copy(dg, node_major(6)[:, 0:GT, 0:F]).then_inc(n["dst_kept"], 1)

                def relu(g):
                    dve.wait_ge(n["mixed"], g + 1)
                    result_free(g)
                    v.tensor_scalar(ng, mixed, 0.0, None, ALU.max).then_inc(n["normed"], 1)

                def elu(g):
                    dve.wait_ge(n["mixed"], g + 1)
                    wait(dve, n["normed"], g)
                    v.tensor_scalar(sq, mixed, 0.0, None, ALU.min).then_inc(n["floored"], 1)
                    chain.do(v.tensor_scalar(res, mixed, 0.0, None, ALU.max))
                    dve.wait_ge(n["expd"], g + 1)
                    result_free(g)
                    v.scalar_tensor_tensor(ng, sq, -1.0, res, ALU.add, ALU.add).then_inc(n["normed"], 1)

                def join(g):
                    dve.wait_ge(ends_ready, p * NG + g + 1)
                    wait(dve, n["normed"], g)
                    chain.do(v.tensor_tensor(res, ends[:, bass.ds(g * GT, GT), 0:F], every(has, g), ALU.mult))
                    chain.do(v.tensor_tensor(res, res, by_feature(s_row), ALU.mult))
                    chain.do(v.tensor_tensor(sq, every(deg, g), by_feature(t_row), ALU.mult))
                    chain.do(v.tensor_tensor(res, res, sq, ALU.add))
                    chain.do(v.tensor_tensor(res, res, of_group(x_sb, g), ALU.add))
                    dve.wait_ge(n["mixed"], g + 1)
                    chain.do(v.tensor_tensor(res, res, mixed, ALU.add))
                    layer_norm(g)

                if kind == SOFT:
                    over_groups(dve, soft_prepare, norm_and_keep, chain, 3 + 1 + 5)
                elif kind == MESSAGE:
                    over_groups(dve, nothing, join, chain, 6 + 5)
                elif p == 2:
                    over_groups(dve, prepare, relu, chain, 0)
                elif p == 4:
                    over_groups(dve, prepare, elu, chain, 1)
                else:
                    over_groups(dve, prepare, add_and_norm, chain, 1 + 5)


def kernel(**inputs):
    import concourse.bacc as bacc
    from concourse.bass_utils import run_bass_kernel_spmd

    a = {k: np.asarray(v) for k, v in inputs.items()}
    n_edges, ep = a["src"].shape[0], edge_tiles(a["src"].shape[0]) * TE

    def padded(v, fill):
        return np.concatenate([v, np.full((ep - n_edges,), fill, v.dtype)])

    def by_tile(v):
        return np.ascontiguousarray(v.reshape(-1, CH, P).transpose(0, 2, 1))

    w_msg = a["L1_gnn_W_msg"]
    matrices = [a["L0_gnn_W"], a["L1_gnn_W_node"], w_msg[0:F], w_msg[F:2 * F], w_msg[2 * F:3 * F]]
    matrices += [a[n].T for n in ("L2_gnn_Wl1", "L2_gnn_Wr1", "L2_gnn_Wl2", "L2_gnn_Wr2",
                                  "L3_gnn_W1l", "L3_gnn_W1r", "L3_gnn_W2l", "L3_gnn_W2r")]
    rows = [a[n] for n in ("L0_gnn_b", "L2_gnn_bl1", "L2_gnn_bl2", "L3_gnn_b1", "L3_gnn_b2")]
    columns = [a["L1_gnn_" + n] for n in COLUMNS]
    dst_sequence = np.concatenate([np.full((1,), -1, a["dst"].dtype), padded(a["dst"], -1)])
    arrays = {
        "x_dram": a["x"],
        "src_dram": by_tile(padded(a["src"], 0)),
        "dst_columns_dram": np.ascontiguousarray(dst_sequence[1:].reshape(-1, P).T),
        "dst_before_dram": np.ascontiguousarray(dst_sequence[:-1].reshape(-1, P).T),
        "dst_sequence_dram": dst_sequence,
        "attr_dram": np.ascontiguousarray(np.concatenate(
            [a["edge_attr_4"], np.zeros((ep - n_edges, EDGE_DIM), a["edge_attr_4"].dtype)]).T).reshape(-1),
        "w_edge_dram": np.tile(a["L1_gnn_W_edge"], (PARTS * PARTS, 1)),
        "matrices_dram": np.stack(matrices),
        "rows_dram": np.stack(rows),
        "columns_dram": np.stack(columns)[:, :, None],
    }
    nc = bacc.Bacc("TRN2", target_bir_lowering=False, num_devices=1)
    args = [nc.dram_tensor(n, v.shape, mybir.dt.from_np(v.dtype), kind="ExternalInput").ap() for n, v in arrays.items()]
    out = nc.dram_tensor("out_dram", a["x"].shape, mybir.dt.float32, kind="ExternalOutput").ap()
    build(nc, n_edges, *args, out)
    return run_bass_kernel_spmd(nc, [arrays], core_ids=[0]).results[0]["out_dram"]
```

```python
import math
from contextlib import ExitStack

import numpy as np

import concourse.bass as bass
from concourse import mybir

P = 128
F = 96
CH = 4
TE = CH * P
RING = 4
GT = 7
GC = GT * P
EDGE_DIM = 4
MSG_EPS = 1e-7
EPS = 1e-5
BIG = 1e38
HC = 8
PARTS = 3
AK = PARTS * PARTS * EDGE_DIM

MATRICES = ["W0", "W_node", "W_src", "W_dst", "W_ef", "W2l1", "W2r1", "W2l2", "W2r2", "W3l1", "W3r1", "W3l2", "W3r2"]
BIAS = {"W0": 0, "W2l1": 1, "W2l2": 2, "W3l1": 3, "W3l2": 4}
COLUMNS = ["b_node", "g_node", "beta_node", "b_edge", "g_edge", "beta_edge", "b_msg", "g_msg", "beta_msg"]

SOFT, MESSAGE, MEAN = range(3)
PASSES = [SOFT, MESSAGE, MEAN, MEAN, MEAN, MEAN]


def edge_tiles(n_edges):
    return RING * math.ceil(n_edges / (TE * RING))


def node_tiles(n_nodes):
    return GT * math.ceil(n_nodes / (P * GT))


def wait(eng, semaphore, value, before=0):
    if not (isinstance(value, int) and value <= 0):
        eng.wait_ge(semaphore, value + before)


class Chain:

    def __init__(self, eng, semaphore):
        self.eng, self.semaphore, self.base, self.n = eng, semaphore, 0, 0

    def do(self, instruction):
        self.n += 1
        instruction.then_inc(self.semaphore, 1)
        self.eng.wait_ge(self.semaphore, self.base + self.n)


def build(nc, n_edges, x_in, src_in, dst_cols_in, dst_before_in, dst_seq_in, attr_in, w_edge_in, matrices_in, rows_in,
          columns_in, out):
    dt = mybir.dt
    f32, i32, i8, bf16 = dt.float32, dt.int32, dt.int8, dt.bfloat16
    ALU = mybir.AluOpType
    ACT = mybir.ActivationFunctionType
    X = mybir.AxisListType.X

    n_nodes = x_in.shape[0]
    ET = edge_tiles(n_edges)
    EI = ET // RING
    EP = ET * TE
    NT = node_tiles(n_nodes)
    NG = NT // GT
    NP = NT * P
    FULL = n_nodes // P
    REST = n_nodes - FULL * P
    SEQ = EP // P
    CN = EP // P
    CB = math.ceil(CN / P)
    HI = CN // HC // 2

    ctx = ExitStack()
    with ctx:
        def sb(name, shape, t=f32):
            return ctx.enter_context(nc.sbuf_tensor(name, shape, t))

        def dram(name, shape, t=f32):
            return nc.dram_tensor(name, shape, t, kind="Internal").ap()

        def sem(name):
            return ctx.enter_context(nc.semaphore(name))

        def ring_sems(name):
            return [sem(f"{name}{s}") for s in range(RING)]

        def sems(suffix, names):
            return {n: sem(f"{n}_{suffix}") for n in names.split()}

        relu_table = dram("relu_table", [NP, F])
        src_table = dram("src_table", [NP, F])
        dst_table = dram("dst_table", [NP + P, F])
        rank_dram = dram("rank_dram", [EP], i8)
        attr_parts = dram("attr_parts", [AK, EP], bf16)
        x_table = dram("x_table", [NP, F])
        h_table = dram("h_table", [NP, F])
        flag_dram = dram("flag_dram", [EP], i8)
        sign_dram = dram("sign_dram", [EP], i8)
        soft_sums = dram("soft_sums", [EP, 2 * F])
        sums = dram("sums", [EP, F])
        soft_sums_t = soft_sums.rearrange("(t p c) f -> t p (c f)", p=P, c=CH)
        sums_t = sums.rearrange("(t p c) f -> t p (c f)", p=P, c=CH)
        flag_t = [d.rearrange("(t e) -> t e", e=2 * TE) for d in (sign_dram, flag_dram, flag_dram, flag_dram,
                                                              flag_dram, flag_dram)]

        def node_rows(table, g):
            return table.rearrange("(k p) f -> p k f", p=P)[:, bass.ds(g * GT, GT), :]

        gather_table = [relu_table, src_table, x_table, h_table, x_table, h_table]
        next_table = [None, x_table, h_table, x_table, h_table, None]

        ident = sb("ident", [P, P])
        ones = sb("ones", [P, P])
        W = {n: sb(f"m_{n}", [F, F]) for n in MATRICES if n not in BIAS}
        W.update({n: sb(f"m_{n}", [F + 1, F]) for n in BIAS})
        col = {n: sb(f"c_{n}", [F, 1]) for n in COLUMNS}
        w_edge = sb("w_edge", [AK, F])
        w_edge_parts = sb("w_edge_parts", [AK, F], bf16)
        w_ef_scaled = sb("w_ef_scaled", [F, F])

        x_sb = sb("x_sb", [P, NT, F])
        hidden = sb("hidden", [P, NP])
        h_sb = hidden[:, 0:NT * F].rearrange("p (k f) -> p k f", f=F)
        node_feat = hidden[0:F, :]
        end_row = sb("end_row", [P, NT], i32)
        dst_row = sb("dst_row", [P, NT], i32)
        first_rank = sb("first_rank", [1, CN], i32)
        deg, has, rdeg = sb("deg", [P, NT]), sb("has", [P, NT]), sb("rdeg", [P, NT])

        def of_group(t, g):
            return t[:, bass.ds(g * GT, GT)]

        area = sb("area", [P, max(NT * 2 * F, 2 * RING * (TE + CH * F))])
        ends = area[:, 0:NT * 2 * F].rearrange("p (k f) -> p k f", f=2 * F)

        def parts_of(tensor):
            used = [0]

            def part(parts, width):
                used[0] += width
                assert used[0] <= tensor.shape[1], (used[0], tensor.shape)
                return tensor[0:parts, used[0] - width:used[0]]
            return part

        ring = parts_of(area)
        src_rows = ring(P, RING * CH * F).rearrange("p (s c f) -> p s c f", s=RING, c=CH)
        sum_ring = ring(F, RING * TE)
        num_ring = ring(F, RING * TE)
        dst_rows = ring(P, RING * CH * F).rearrange("p (s c f) -> p s c f", s=RING, c=CH)
        out_ring = sb("out_ring", [P, RING, CH, 2 * F])
        idx_src = [sb(f"idx_src{h}", [P, 2 * CH], i32) for h in range(RING // 2)]
        ranks = sb("ranks", [P, RING, TE], i8)
        flags = sb("flags", [F, RING, TE], i8)
        attr = sb("attr", [AK, RING, TE], bf16)
        dump = sb("dump", [F, GC])
        relu_dump = sb("relu_dump", [F, TE])

        second = sb("second", [P, 7680])
        soft = parts_of(second)
        max_ring = soft(F, 1 + RING * TE)
        decay = soft(F, 2 * TE).rearrange("p (b e) -> p b e", b=2)
        weight = soft(F, 2 * TE).rearrange("p (b e) -> p b e", b=2)
        weighted = soft(F, 2 * TE).rearrange("p (b e) -> p b e", b=2)
        message = parts_of(second)
        h_ring = message(F, 2 * TE).rearrange("p (b e) -> p b e", b=2)
        msg_ring = message(F, RING * TE).rearrange("p (b e) -> p b e", b=RING)
        rank_hot = message(P, 2 * TE).rearrange("p (b e) -> p b e", b=2)
        nodes = parts_of(second)
        grp, xg, res, sq, ng, dg = [nodes(P, GT * F).rearrange("p (k f) -> p k f", f=F) for _ in range(6)]
        fa, fx = nodes(F + 1, GC), nodes(F, GC)

        first = parts_of(area)
        seq_now, seq_before, seq_int, bits = [first(P, SEQ).bitcast(i32) for _ in range(4)]
        before_int, started = first(P, CN).bitcast(i32), first(1, CN)
        running = sb("running", [1, CN])
        tri = sb("tri", [P, P])
        attr_bf = [first(P, EP * EDGE_DIM // P // 2).bitcast(bf16) for _ in range(PARTS)]
        split = parts_of(second)
        attr_f, attr_rest = split(P, EP * EDGE_DIM // P), split(P, EP * EDGE_DIM // P)
        w_rest = sb("w_rest", [AK, F])
        w_part = [sb(f"w_part{i}", [AK, F], bf16) for i in range(PARTS)]
        cols_lo, cols_hi = sb("cols_lo", [P, CN], bf16), sb("cols_hi", [P, CN], bf16)
        starts = sb("starts", [P, CN], bf16)
        tri_bf, ones_bf = sb("tri_bf", [P, P], bf16), sb("ones_bf", [P, 1], bf16)
        iota_lo, iota_hi = sb("iota_lo", [P, P, HC], bf16), sb("iota_hi", [P, NT, HC], bf16)
        iota_p, node_number = sb("iota_p", [P, 1]), sb("node_number", [P, NT])
        rank8 = sb("rank8", [P, CB, P], i8)
        others, all_with = sb("others", [P, NT]), sb("all_with", [P, 1])
        flag8 = sb("flag8", [P, 2, SEQ], i8)
        hot_lo = sb("hot_lo", [P, 2, P, HC], bf16)
        hot_hi = sb("hot_hi", [P, 2, NT, HC], bf16)
        end_f, end_i, end_j = sb("end_f", [P, NT]), sb("end_i", [P, NT], i32), sb("end_j", [P, NT], i32)
        total, below = sb("total", [P, NT]), sb("below", [P, NT])

        ef_sum, ef_sq = sb("ef_sum", [F, ET]), sb("ef_sq", [F, ET])
        mg_sum, mg_sq = sb("mg_sum", [F, ET]), sb("mg_sq", [F, ET])
        nd_sum, nd_sq = sb("nd_sum", [F, NG]), sb("nd_sq", [F, NG])
        mu, var, tmp = sb("mu", [F, 1]), sb("var", [F, 1]), sb("tmp", [F, 1])
        s_ef, t_ef = sb("s_ef", [F, 1]), sb("t_ef", [F, 1])
        s_nd, t_nd = sb("s_nd", [F, 1]), sb("t_nd", [F, 1])
        s_mg, t_mg = sb("s_mg", [F, 1]), sb("t_mg", [F, 1])
        msg_bias = sb("msg_bias", [F, 1])
        diag_s, diag_t = sb("diag_s", [F, F]), sb("diag_t", [F, F])
        s_row, t_row = sb("s_row", [P, F]), sb("t_row", [P, F])
        eps = sb("eps", [P, 1])
        mean, rstd = sb("mean", [P, GT]), sb("rstd", [P, GT])

        ps = ctx.enter_context(nc.psum_tensor("ps", [P, 8, 512], f32))

        def bank(b, parts=P, width=512):
            return ps[0:parts, b, 0:width]

        def node_major(b):
            return ps[:, b:b + 2, :].rearrange("p b (k n) -> p (b k) n", n=P)

        def feature_major(b):
            return ps[0:F, b:b + 2, :].rearrange("p b n -> p (b n)")[:, 0:GC]

        weights_landed, x_landed = sem("weights_landed"), sem("x_landed")
        cols_landed, seq_landed = sem("cols_landed"), sem("seq_landed")
        pool_step, consts_made = sem("pool_step"), sem("consts_made")
        dve_step = sem("dve_step")
        flag_made = sem("flag_made")
        attr_in_landed, attr_split, w_split = sem("attr_in_landed"), sem("attr_split"), sem("w_split")
        setup_stored = sem("setup_stored")
        SETUP_STORES = 2 + 2 + 2 * PARTS * PARTS + CB
        ranks_summed, ranks_made = sem("ranks_summed"), sem("ranks_made")
        starts_made = sem("starts_made")
        hot_made, hot_used, deg_counted, deg_made, prefix_summed = (
            sem("hot_made"), sem("hot_used"), sem("deg_counted"), sem("deg_made"), sem("prefix_summed"))
        index_made, relu_made = sem("index_made"), sem("relu_made")
        ef_coefs_made, ef_bias_summed, msg_bias_made = sem("ef_coefs_made"), sem("ef_bias_summed"), sem("msg_bias_made")
        diags_made, rows_spread = sem("diags_made"), sem("rows_spread")
        idx_landed, flags_landed, attr_landed, ranks_landed = [
            [sem(f"{name}{h}") for h in range(RING // 2)]
            for name in ("idx_landed", "flags_landed", "attr_landed", "ranks_landed")]
        src_gathered = ring_sems("src_gathered")
        window_landed = ring_sems("window_landed")
        sums_stored = ring_sems("sums_stored")
        ends_landed = [sem(f"ends_landed{b}") for b in range(2)]
        ends_ready = sem("ends_ready")
        var_summed, rooted = sem("var_summed"), sem("rooted")
        coef_var_made, coef_rooted = sem("coef_var_made"), sem("coef_rooted")
        gathers_begun = sem("gathers_begun")
        out_stored = sem("out_stored")
        EDGE = "turned summed back copied"
        edge = [None if kind in PASSES[:p] else sems(f"e{p}", EDGE + {SOFT: " hid hrelu squared maxed scored expd weighed wrapped",
                                      MESSAGE: " hid hrelu squared relued placed"}.get(kind, ""))
                for p, kind in enumerate(PASSES)]
        first_mean = PASSES.index(MEAN) if MEAN in PASSES else 0
        edge = [edge[first_mean] if kind == MEAN else e for e, kind in zip(edge, PASSES)]

        def tiles_before(p):
            return (p - first_mean) * ET if PASSES[p] == MEAN else 0

        node = [sems(f"n{p}", "copied mixed normed stored" + (" taken" if p != 2 else "") + (" kept" if p < len(PASSES) - 1 else "")
                     + {SOFT: " prepared turned turned2 copied2 src_made src_kept dst_made dst_kept dst_stored nh_made"
                              " nh_kept nh_squared",
                        MEAN: " prepared turned xcopied"}.get(kind, "") + (" floored expd" if p == 4 else ""))
                for p, kind in enumerate(PASSES)]

        def over_tiles(eng, lead, lag=None):
            lead(0, 0)
            for s in range(RING):
                lead((s + 1) // RING, (s + 1) % RING)
                if lag:
                    lag(0, s)
            with eng.Fori(1, EI - 1) as u:
                for s in range(RING):
                    lead(u + (s + 1) // RING, (s + 1) % RING)
                    if lag:
                        lag(u, s)
            for s in range(RING):
                if s + 1 < RING:
                    lead(EI - 1, s + 1)
                if lag:
                    lag(EI - 1, s)

        def tile_before(step, u, s):
            if s:
                step(u, s - 1)
            elif not isinstance(u, int) or u:
                step(u - 1, RING - 1)

        def over_groups(eng, lead, lag, last=None, chain=None, steps=0, late=False):
            last = last or nothing
            lead(0)
            for step in (lag, lead) if late else (lead, lag):
                step(0 if step is lag else 1)
            start = chain.base + chain.n - steps if chain else 0
            with eng.Fori(1, NG - 1) as g:
                if chain:
                    chain.base, chain.n = g * steps + start, 0
                if not late:
                    lead(g + 1)
                lag(g)
                last(g - 1)
                if late:
                    lead(g + 1)
                assert not chain or chain.n == steps, chain.n
            if chain:
                chain.base, chain.n = start + steps * (NG - 1), 0
            lag(NG - 1)
            last(NG - 2)
            last(NG - 1)

        def group_before(step, g):
            if not isinstance(g, int) or g:
                step(g - 1)

        def wait_for_tables(eng, p):
            if p:
                eng.wait_ge(node[p - 1]["stored"], 16 * NG)
            if PASSES[p] == MESSAGE:
                eng.wait_ge(node[p - 1]["dst_stored"], 16 * NT)

        def norms_before(p):
            return NG * {0: 0, 1: 1, 3: 2, 5: 3}[p]

        def nothing(*where):
            pass

        block = ctx.enter_context(nc.Block())

        @block.sync
        def _(sp):
            sp.dma_start(seq_int, dst_cols_in).then_inc(cols_landed, 16)
            sp.dma_start(before_int, dst_before_in).then_inc(cols_landed, 16)
            sp.dma_start(w_edge[:, :], w_edge_in).then_inc(attr_in_landed, 16)
            sp.dma_start(attr_f, attr_in.rearrange("(p j) -> p j", p=P)).then_inc(attr_in_landed, 16)
            sp.dma_start(x_sb[:, 0:FULL, :], x_in[0:FULL * P, :].rearrange("(k p) f -> p k f", p=P)).then_inc(x_landed, 16)
            sp.wait_ge(consts_made, 1)
            sp.dma_start(x_sb[0:REST, FULL, :], x_in[FULL * P:n_nodes, :]).then_inc(x_landed, 16)
            sp.dma_start(seq_now, dst_seq_in[1:1 + EP].rearrange("(p j) -> p j", p=P)).then_inc(seq_landed, 16)
            sp.dma_start(seq_before, dst_seq_in[0:EP].rearrange("(p j) -> p j", p=P)).then_inc(seq_landed, 16)
            for k, n in enumerate(MATRICES):
                sp.dma_start(W[n][0:F, :], matrices_in[k, :, :]).then_inc(weights_landed, 16)
            for n, k in BIAS.items():
                sp.dma_start(W[n][F:F + 1, :], rows_in[k:k + 1, :]).then_inc(weights_landed, 16)
            for k, n in enumerate(COLUMNS):
                sp.dma_start(col[n][:, :], columns_in[k, :, :]).then_inc(weights_landed, 16)
            sp.wait_ge(attr_split, 1)
            for i in range(PARTS):
                for j in range(PARTS):
                    at = (i * PARTS + j) * EDGE_DIM
                    sp.dma_start(attr_parts[at:at + EDGE_DIM, :].rearrange("a e -> (a e)").rearrange("(p j) -> p j", p=P),
                                 attr_bf[i]).then_inc(setup_stored, 16)
            sp.wait_ge(relu_made, 1)
            sp.dma_start(relu_table.rearrange("(k p) f -> p k f", p=P), hidden[:, 0:NT * F].rearrange(
                "p (k f) -> p k f", f=F)).then_inc(setup_stored, 16)
            sp.wait_ge(consts_made, 2)
            sp.dma_start(dst_table[NP:NP + P, :], s_row[:, :]).then_inc(setup_stored, 16)
            sp.wait_ge(flag_made, 2)
            for d, b in ((flag_dram, 0), (sign_dram, 1)):
                sp.dma_start(d.rearrange("(p j) -> p j", p=P), flag8[:, b, :]).then_inc(setup_stored, 16)
            sp.wait_ge(w_split, 1)
            for i in range(PARTS):
                for j in range(PARTS):
                    at = (i * PARTS + j) * EDGE_DIM
                    sp.dma_start(w_edge_parts[at:at + EDGE_DIM, :], w_part[j][at:at + EDGE_DIM, :]).then_inc(setup_stored, 16)
            sp.wait_ge(ranks_made, 1)
            for b in range(CB):
                m = min(P, CN - b * P)
                sp.dma_start(rank_dram[b * P * P:(b * P + m) * P].rearrange("(c e) -> c e", e=P), rank8[0:m, b, :])\
                  .then_inc(setup_stored, 16)
            sp.wait_ge(setup_stored, 16 * SETUP_STORES)
            ranks_t = rank_dram.rearrange("(t e) -> t e", e=2 * TE)

            for p, kind in enumerate(PASSES):
                e, n, before = edge[p], node[p], tiles_before(p)
                if kind == MESSAGE:
                    wait_for_tables(sp, p)

                def load(u, h):
                    s = 2 * h
                    use, t, pair = p * EI + u, u * RING + s, u * (RING // 2) + h
                    one = bass.ds(pair, 1)
                    if kind == MESSAGE:
                        _, firsts = nc.values_load_multi_w_load_instructions(
                            first_rank[0:1, bass.ds(t * CH, 2 * CH)], engines=[mybir.EngineType.SP], min_val=0, max_val=NP,
                            skip_runtime_bounds_check_because="a count of runs, of which there are NP at most")
                    if kind != MEAN:
                        wait(sp, e["hid"], t + 2 - RING)
                    wait(sp, src_gathered[s], use * 16 * CH)
                    wait(sp, src_gathered[s + 1], use * 16 * CH)
                    sp.dma_start(idx_src[h][:, :], src_in[one, :, :].rearrange("a p c -> (a p) c")).then_inc(idx_landed[h], 16)
                    if kind != MEAN:
                        sp.dma_start(attr[:, s:s + 2, :].rearrange("p s e -> p (s e)"),
                                     attr_parts[:, bass.ds(t * TE, 2 * TE)]).then_inc(attr_landed[h], 16)
                    wait(sp, e["summed"], t + 2 - RING, before)
                    sp.dma_start(flags[:, s:s + 2, :].rearrange("p s e -> p (s e)"),
                                 flag_t[p][one, :].to_broadcast([F, 2 * TE])).then_inc(flags_landed[h], 16)
                    if kind == MESSAGE:
                        wait(sp, e["turned"], t + 2 - RING)
                        sp.dma_start(ranks[:, s:s + 2, :].rearrange("p s e -> p (s e)"),
                                     ranks_t[one, :].to_broadcast([P, 2 * TE])).then_inc(ranks_landed[h], 16)
                        for c in range(2 * CH):
                            sp.dma_start(dst_rows[:, s + c // CH, c % CH, :], dst_table[bass.ds(firsts[c], P), :])\
                              .then_inc(window_landed[s + c // CH], 16)

                for h in range(RING // 2):
                    load(0, h)
                with sp.Fori(1, EI) as u:
                    for h in range(RING // 2):
                        load(u, h)

                def store(g):
                    if kind == SOFT:
                        sp.wait_ge(n["src_kept"], g + 1)
                        sp.dma_start(node_rows(src_table, g), xg).then_inc(n["stored"], 16)
                    elif p < len(PASSES) - 1:
                        sp.wait_ge(n["normed"], g + 1)
                        sp.dma_start(node_rows(next_table[p], g), ng).then_inc(n["stored"], 16)
                    else:
                        sp.wait_ge(n["normed"], g + 1)
                        if isinstance(g, int) and g == NG - 1:
                            done = g * GT
                            if FULL > done:
                                sp.dma_start(out[done * P:FULL * P, :].rearrange("(k p) f -> p k f", p=P),
                                             ng[:, 0:FULL - done, :]).then_inc(n["stored"], 16)
                            sp.dma_start(out[FULL * P:n_nodes, :], ng[0:REST, FULL - done, :]).then_inc(out_stored, 16)
                        else:
                            sp.dma_start(node_rows_out(g), ng).then_inc(n["stored"], 16)

                def node_rows_out(g):
                    return out[bass.ds(g * GC, GC), :].rearrange("(k p) f -> p k f", p=P)

                over_groups(sp, nothing, store)
            sp.wait_ge(node[-1]["stored"], 16 * (NG - (FULL == (NG - 1) * GT)))
            sp.wait_ge(out_stored, 16)

        @block.gpsimd
        def _(pool):
            chain = Chain(pool, pool_step)
            nc.gpsimd.memset(x_sb[:, FULL:NT, :], 0.0).then_inc(consts_made, 1)
            nc.gpsimd.memset(ones[:, :], 1.0)
            nc.gpsimd.memset(eps[:, :], EPS)
            nc.gpsimd.memset(tri[:, :], 1.0)
            chain.do(nc.gpsimd.memset(ident[:, :], 0.0))
            nc.gpsimd.affine_select(out=ident[:, :], in_=ident[:, :], compare_op=ALU.not_equal, fill=1.0, base=0,
                                    pattern=[[-1, P]], channel_multiplier=1)
            nc.gpsimd.affine_select(out=tri[:, :], in_=tri[:, :], compare_op=ALU.is_ge, fill=0.0, base=0,
                                    pattern=[[1, P]], channel_multiplier=-1)
            def iota(t, pattern, step):
                return nc.gpsimd.iota(t, pattern=pattern, base=0, channel_multiplier=step,
                                      allow_small_or_imprecise_dtypes=True)

            iota(iota_lo[:, :, :], [[1, P], [0, HC]], 0)
            iota(iota_p[:, :], [[0, 1]], 1)
            iota(node_number[:, :], [[P, NT]], 1)
            nc.gpsimd.memset(ones_bf[:, :], 1.0)
            nc.gpsimd.memset(s_row[:, :], 0.0)
            nc.gpsimd.memset(tri_bf[:, :], 1.0)
            chain.do(iota(iota_hi[:, :, :], [[1, NT], [0, HC]], 0))
            chain.do(nc.gpsimd.affine_select(out=tri_bf[:, :], in_=tri_bf[:, :], compare_op=ALU.is_ge, fill=0.0, base=0,
                                             pattern=[[1, P]], channel_multiplier=-1))
            nc.gpsimd.memset(tri_bf[0:1, :], 0.0).then_inc(consts_made, 1)

            pool.wait_ge(attr_in_landed, 32)
            chain.do(nc.gpsimd.tensor_copy(attr_bf[0], attr_f))
            chain.do(nc.gpsimd.tensor_tensor(attr_rest, attr_f, attr_bf[0], ALU.subtract))
            chain.do(nc.gpsimd.tensor_copy(attr_bf[1], attr_rest))
            chain.do(nc.gpsimd.tensor_tensor(attr_rest, attr_rest, attr_bf[1], ALU.subtract))
            nc.gpsimd.tensor_copy(attr_bf[2], attr_rest).then_inc(attr_split, 1)

            for p, kind in enumerate(PASSES):
                e, n, before = edge[p], node[p], tiles_before(p)
                if p == 0:
                    pool.wait_ge(setup_stored, 16 * SETUP_STORES)
                    pool.wait_ge(index_made, 1)
                wait_for_tables(pool, p)

                def gather(u, s):
                    use, t = p * EI + u, u * RING + s
                    wait(pool, idx_landed[s // 2], (use + 1) * 16)
                    wait(pool, e["turned"], t - RING + 1, before)
                    pool.sem_inc(gathers_begun, 1)
                    for c in range(CH):
                        pool.indirect_dma_start(out=src_rows[:, s, c, :], out_offset=None, in_=gather_table[p],
                                                in_offset=bass.IndirectOffsetOnAxis(ap=idx_src[s // 2][:, s % 2 * CH + c:s % 2 * CH + c + 1], axis=0))\
                            .then_inc(src_gathered[s], 16)

                over_tiles(pool, gather)

                def ends_of(g):
                    groups = p * len(range(g % 2, NG, 2)) + g // 2 + 1
                    pool.wait_ge(ends_landed[g % 2], 16 * GT * groups)
                    pool.sem_inc(ends_ready, 1)

                for s in range(RING):
                    pool.wait_ge(sums_stored[s], 16 * EI * (p + 1))
                for g in range(NG):
                    for k in range(g * GT, (g + 1) * GT):
                        wide = 2 * F if kind == SOFT else F
                        pool.indirect_dma_start(out=ends[:, k, 0:wide], out_offset=None,
                                                in_=soft_sums if kind == SOFT else sums,
                                                in_offset=bass.IndirectOffsetOnAxis(ap=end_row[:, k:k + 1], axis=0))\
                            .then_inc(ends_landed[g % 2], 16)
                    if g:
                        ends_of(g - 1)
                ends_of(NG - 1)
                if kind == SOFT:
                    for g in range(NG):
                        pool.wait_ge(n["dst_kept"], g + 1)
                        for k in range(GT):
                            at = dst_row[:, g * GT + k:g * GT + k + 1]
                            pool.indirect_dma_start(out=dst_table, out_offset=bass.IndirectOffsetOnAxis(ap=at, axis=0),
                                                    in_=dg[:, k, :], in_offset=None).then_inc(n["dst_stored"], 16)

        @block.tensor
        def _(pe):
            pe.wait_ge(consts_made, 2)
            pe.wait_ge(starts_made, 1)
            for b in range(CB):
                m = min(P, CN - b * P)
                nc.tensor.matmul(ps[0:m, 4 + b // 4, (b % 4) * P:(b % 4 + 1) * P], starts[:, b * P:b * P + m], tri_bf[:, :],
                                 start=True, stop=True)
            for h in range(2):
                last = nc.tensor.matmul(bank(2 + h, 1, CN // 2), ones_bf[:, :], starts[:, h * CN // 2:(h + 1) * CN // 2],
                                        start=True, stop=True)
            last.then_inc(ranks_summed, 1)

            def count(number, b, start=False, stop=False):
                pe.wait_ge(hot_made, number + 1)
                for c in range(HC):
                    last = nc.tensor.matmul(bank(0, P, NT), hot_lo[:, b, :, c], hot_hi[:, b, :, c],
                                            start=start and c == 0, stop=stop and c == HC - 1)
                return last

            count(0, 0, start=True).then_inc(hot_used, 1)
            count(1, 1).then_inc(hot_used, 1)
            with pe.Fori(1, HI - 1) as i:
                count(2 * i, 0).then_inc(hot_used, 1)
                count(2 * i + 1, 1).then_inc(hot_used, 1)
            count(2 * HI - 2, 0).then_inc(hot_used, 1)
            last = count(2 * HI - 1, 1, stop=True)
            last.then_inc(deg_counted, 1)
            pe.wait_ge(deg_made, 1)
            pe.wait_ge(ranks_made, 1)
            nc.tensor.matmul(bank(1, P, NT), tri[:, :], deg[:, :], start=True, stop=True)
            nc.tensor.matmul(bank(2, P, NT), ones[:, :], deg[:, :], start=True, stop=True)
            nc.tensor.matmul(bank(3, P, NT), tri[:, :], has[:, :], start=True, stop=True)
            nc.tensor.matmul(bank(4, P, NT), ones[:, :], has[:, :], start=True, stop=True).then_inc(prefix_summed, 1)
            pe.wait_ge(setup_stored, 16 * SETUP_STORES)
            pe.wait_ge(weights_landed, 16 * (len(MATRICES) + len(BIAS) + len(COLUMNS)))

            for p, kind in enumerate(PASSES):
                e, n, before = edge[p], node[p], tiles_before(p)

                def project(u, s):
                    t = u * RING + s
                    wait(pe, attr_landed[s // 2], (p * EI + u + 1) * 16)
                    wait(pe, e["hrelu"], t - 1)
                    nc.tensor.matmul(bank(6 + s % 2, F), w_edge_parts[:, :], attr[:, s, :], start=True, stop=True)\
                      .then_inc(e["hid"], 1)

                def turn(u, s):
                    t = u * RING + s
                    wait(pe, src_gathered[s], (p * EI + u + 1) * 16 * CH)
                    wait(pe, e["weighed"] if kind == SOFT else e["summed"], t - 1, before)
                    for c in range(CH):
                        last = nc.tensor.transpose(ps[0:F, s % 2, c * P:(c + 1) * P], src_rows[:, s, c, :], ident[:, :])
                    last.then_inc(e["turned"], 1)

                def score(u, s):
                    t = u * RING + s
                    wait(pe, e["hrelu"], t + 1)
                    wait(pe, e["relued"], t - 1)
                    nc.tensor.matmul(bank(s % 2, F), w_ef_scaled[:, :], h_ring[:, s % 2, :], start=True, stop=False)
                    wait(pe, src_gathered[s], (p * EI + u + 1) * 16 * CH)
                    wait(pe, window_landed[s], (u + 1) * 16 * CH)
                    wait(pe, e["placed"], t + 1)
                    for c in range(CH):
                        at = slice(c * P, (c + 1) * P)
                        nc.tensor.matmul(ps[0:F, s % 2, at], src_rows[:, s, c, :], ident[:, :], start=False, stop=False)
                        last = nc.tensor.matmul(ps[0:F, s % 2, at], dst_rows[:, s, c, :], rank_hot[:, s % 2, at],
                                                start=False, stop=c == CH - 1)
                    last.then_inc(e["turned"], 1)

                def turn_back(u, s):
                    t = u * RING + s
                    wait(pe, e["summed"], t + 1, before)
                    wait(pe, e["copied"], t - 1, before)
                    for r, b in ((sum_ring, 2), (num_ring, 4))[0:2 if kind == SOFT else 1]:
                        for c in range(CH):
                            last = nc.tensor.transpose(ps[:, b + s % 2, c * F:(c + 1) * F],
                                                       r[:, (s * CH + c) * P:(s * CH + c + 1) * P], ident[0:F, 0:F])
                    last.then_inc(e["back"], 1)

                def turn_and_project(u, s):
                    turn(u, s)
                    project(u, s)

                def score_and_turn_back(u, s):
                    score(u, s)
                    tile_before(turn_back, u, s)

                if kind == SOFT:
                    over_tiles(pe, turn_and_project, lambda u, s: tile_before(turn_back, u, s))
                    turn_back(EI - 1, RING - 1)
                elif kind == MESSAGE:
                    pe.wait_ge(ef_coefs_made, 1)
                    nc.tensor.matmul(bank(2, F, 1), W["W_ef"][:, :], t_ef[:, :], start=True, stop=True)\
                      .then_inc(ef_bias_summed, 1)
                    over_tiles(pe, project, score_and_turn_back)
                    turn_back(EI - 1, RING - 1)
                    pe.wait_ge(diags_made, 1)
                    pe.wait_ge(e["copied"], ET)
                    nc.tensor.matmul(bank(2, P, F), ones[0:F, :], diag_s[:, :], start=True, stop=True)
                    nc.tensor.matmul(bank(3, P, F), ones[0:F, :], diag_t[:, :], start=True, stop=True)\
                      .then_inc(rows_spread, 1)
                else:
                    over_tiles(pe, turn, turn_back)

                left = {0: "W0", 2: "W2l1", 3: "W2l2", 4: "W3l1", 5: "W3l2"}.get(p)
                right = {2: "W2r1", 3: "W2r2", 4: "W3r1", 5: "W3r2"}.get(p)
                taken = n["normed" if p == 2 else "taken"]

                def turn_nodes(g):
                    wait(pe, n["copied"], g)
                    if kind == SOFT:
                        wait(pe, n["nh_kept"], g - 1)
                    if right:
                        pe.wait_ge(n["xcopied"], g + 1)
                        for k in range(GT):
                            last = nc.tensor.transpose(feature_major(2)[:, k * P:(k + 1) * P], xg[:, k, :], ident[:, :])
                        last.then_inc(n["turned"], 1)
                    wait(pe, n["prepared"], g + 1)
                    for k in range(GT):
                        last = nc.tensor.transpose(feature_major(0)[:, k * P:(k + 1) * P], grp[:, k, :], ident[:, :])
                    last.then_inc(n["turned"], 1)

                def mix(g):
                    pe.wait_ge(n["copied"], g + 1)
                    wait(pe, taken, g)
                    for k in range(GT):
                        o = node_major(4)[:, k, 0:F]
                        last = nc.tensor.matmul(o, fa[:, k * P:(k + 1) * P], W[left][:, :], start=True, stop=not right)
                        if right:
                            last = nc.tensor.matmul(o, fx[:, k * P:(k + 1) * P], W[right][:, :], start=False, stop=True)
                    last.then_inc(n["mixed"], 1)

                def project_nodes(g):
                    pe.wait_ge(n["normed"], g + 1)
                    wait(pe, n["copied2"], g)
                    for k in range(GT):
                        last = nc.tensor.transpose(feature_major(2)[:, k * P:(k + 1) * P], ng[:, k, :], ident[:, :])
                    last.then_inc(n["turned2"], 1)
                    pe.wait_ge(n["copied2"], g + 1)
                    wait(pe, n["dst_kept"], g)
                    for k in range(GT):
                        last = nc.tensor.matmul(node_major(6)[:, k, 0:F], fx[:, k * P:(k + 1) * P], W["W_src"][:, :],
                                                start=True, stop=True)
                    last.then_inc(n["src_made"], 1)
                    for c, w in ((0, 512), (512, GC - 512)):
                        last = nc.tensor.matmul(feature_major(0)[:, c:c + w], W["W_node"][:, :], fx[:, c:c + w],
                                                start=True, stop=True)
                    last.then_inc(n["nh_made"], 1)
                    pe.wait_ge(n["src_kept"], g + 1)
                    for k in range(GT):
                        last = nc.tensor.matmul(node_major(6)[:, k, 0:F], fx[:, k * P:(k + 1) * P], W["W_dst"][:, :],
                                                start=True, stop=True)
                    last.then_inc(n["dst_made"], 1)

                def turn_features(g):
                    pe.wait_ge(n["copied"], g + 1)
                    wait(pe, taken, g)
                    for k in range(GT):
                        last = nc.tensor.transpose(node_major(4)[:, k, 0:F], fx[:, k * P:(k + 1) * P], ident[0:F, 0:F])
                    last.then_inc(n["mixed"], 1)

                if kind == SOFT:
                    over_groups(pe, turn_nodes, mix, project_nodes, late=True)
                elif kind == MESSAGE:
                    over_groups(pe, nothing, turn_features)
                else:
                    over_groups(pe, turn_nodes, mix, late=True)

        @block.scalar
        def _(act):
            act.wait_ge(consts_made, 2)
            act.wait_ge(weights_landed, 16 * (len(MATRICES) + len(BIAS) + len(COLUMNS)))

            def coef_root(number):
                act.wait_ge(coef_var_made, number)
                nc.scalar.activation(var[:, :], var[:, :], ACT.Sqrt, bias=eps[0:F, :]).then_inc(coef_rooted, 1)

            for p, kind in enumerate(PASSES):
                e, n, before = edge[p], node[p], tiles_before(p)

                wait_for_tables(act, p)

                def valid_edges(u, s):
                    return max(0, min(TE, n_edges - (u * RING + s) * TE)) if isinstance(u, int) else TE

                def relu_and_stats(o, i, bias, total, squares, t, v, done, squared):
                    wait(act, squared, t)
                    if v < TE:
                        last = nc.scalar.activation(o[:, v:TE], i[:, v:TE], ACT.Relu, bias=bias)
                    if v:
                        last = nc.scalar.activation(o[:, 0:v], i[:, 0:v], ACT.Relu, bias=bias, accum_out=total[:, bass.ds(t, 1)])
                    last.then_inc(done, 1)
                    act.wait_ge(done, t + 1)
                    if v:
                        nc.scalar.activation(dump[:, 0:v], o[:, 0:v], ACT.Square, accum_out=squares[:, bass.ds(t, 1)])\
                          .then_inc(squared, 1)
                    else:
                        act.sem_inc(squared, 1)

                def copy_back(u, s):
                    use, t = p * EI + u, u * RING + s
                    wait(act, e["back"], t + 1, before)
                    wait(act, sums_stored[s], use * 16)
                    if kind == SOFT:
                        for half, b in ((0, 2), (1, 4)):
                            last = nc.scalar.activation(out_ring[:, s, :, half * F:(half + 1) * F],
                                                        bank(b + s % 2, P, CH * F).rearrange("p (c f) -> p c f", f=F), ACT.Copy)
                        last.then_inc(e["copied"], 1)
                        act.wait_ge(e["copied"], t + 1)
                        act.dma_start(soft_sums_t[bass.ds(t, 1), :, :].rearrange("a p n -> (a p) n"),
                                      out_ring[:, s, :, :].rearrange("p c f -> p (c f)")).then_inc(sums_stored[s], 16)
                    else:
                        o = out_ring[:, s, 0:CH // 2, :].rearrange("p c f -> p (c f)")
                        nc.scalar.activation(o, bank(2 + s % 2, P, CH * F), ACT.Copy).then_inc(e["copied"], 1)
                        wait(act, e["copied"], t + 1, before)
                        act.dma_start(sums_t[bass.ds(t, 1), :, :].rearrange("a p n -> (a p) n"), o).then_inc(sums_stored[s], 16)

                def soften(u, s):
                    t = u * RING + s
                    wait(act, e["hid"], t + 1)
                    relu_and_stats(relu_dump, bank(6 + s % 2, F), col["b_edge"][:, :], ef_sum, ef_sq, t, valid_edges(u, s),
                                   e["hrelu"], e["squared"])
                    wait(act, e["scored"], t + 1)
                    nc.scalar.activation(decay[:, s % 2, :], decay[:, s % 2, :], ACT.Exp)
                    nc.scalar.activation(weight[:, s % 2, :], weight[:, s % 2, :], ACT.Exp).then_inc(e["expd"], 1)

                def relu_features(u, s):
                    t = u * RING + s
                    wait(act, e["hid"], t + 1)
                    wait(act, e["turned"], t - 1)
                    nc.scalar.activation(h_ring[:, s % 2, :], bank(6 + s % 2, F), ACT.Relu, bias=col["b_edge"][:, :])\
                      .then_inc(e["hrelu"], 1)

                def relu_message(u, s):
                    t = u * RING + s
                    wait(act, e["turned"], t + 1)
                    wait(act, e["summed"], t - RING + 1)
                    relu_and_stats(msg_ring[:, s, :], bank(s % 2, F), msg_bias[:, :], mg_sum, mg_sq, t, valid_edges(u, s),
                                   e["relued"], e["squared"])
                    tile_before(copy_back, u, s)

                if kind == SOFT:
                    over_tiles(act, soften, lambda u, s: tile_before(copy_back, u, s))
                    copy_back(EI - 1, RING - 1)
                elif kind == MESSAGE:
                    coef_root(1)
                    coef_root(2)
                    act.wait_ge(msg_bias_made, 1)
                    over_tiles(act, relu_features, relu_message)
                    copy_back(EI - 1, RING - 1)
                    coef_root(3)
                else:
                    over_tiles(act, nothing, copy_back)

                source = {2: x_sb, 3: h_sb, 4: x_sb, 5: h_sb}.get(p)
                kept_in = {0: x_sb, 1: x_sb, 2: h_sb, 3: x_sb, 4: h_sb}[p] if p < len(PASSES) - 1 else None

                def root(g):
                    if p not in (2, 4):
                        act.wait_ge(var_summed, norms_before(p) + g + 1)
                        nc.scalar.activation(rstd[:, :], rstd[:, :], ACT.Sqrt, bias=eps[:, :], scale=1.0 / F)\
                          .then_inc(rooted, 1)

                def keep(g):
                    if kept_in is not None:
                        act.wait_ge(n["normed"], g + 1)
                        nc.scalar.activation(of_group(kept_in, g), ng, ACT.Copy).then_inc(n["kept"], 1)

                def root_and_keep(g):
                    root(g)
                    keep(g)

                def copy_turned(g):
                    if source is not None:
                        wait(act, n["turned"], 2 * g)
                        nc.scalar.activation(xg, of_group(source, g), ACT.Copy).then_inc(n["xcopied"], 1)
                    wait(act, n["mixed"], g)
                    if source is not None:
                        act.wait_ge(n["turned"], 2 * g + 1)
                        nc.scalar.activation(fx, feature_major(2), ACT.Copy)
                    act.wait_ge(n["turned"], g + 1 if source is None else 2 * g + 2)
                    nc.scalar.activation(fa[0:F, :], feature_major(0), ACT.Copy).then_inc(n["copied"], 1)

                def exp_and_keep(g):
                    act.wait_ge(n["floored"], g + 1)
                    nc.scalar.activation(sq, sq, ACT.Exp).then_inc(n["expd"], 1)
                    root_and_keep(g)

                def copy_result(g):
                    act.wait_ge(n["turned2"], g + 1)
                    wait(act, n["dst_made"], g)
                    nc.scalar.activation(fx, feature_major(2), ACT.Copy).then_inc(n["copied2"], 1)

                def keep_sources(g):
                    act.wait_ge(n["src_made"], g + 1)
                    wait(act, n["stored"], g * 16)
                    nc.scalar.activation(xg, node_major(6)[:, 0:GT, 0:F], ACT.Copy).then_inc(n["src_kept"], 1)

                def node_features(g):
                    act.wait_ge(n["nh_made"], g + 1)
                    v = min(GC, n_nodes - g * GC) if isinstance(g, int) else GC
                    nf = node_feat[:, bass.ds(g * GC, GC)]
                    if v < GC:
                        nc.scalar.activation(nf[:, v:GC], feature_major(0)[:, v:GC], ACT.Relu, bias=col["b_node"][:, :])
                    nc.scalar.activation(nf[:, 0:v], feature_major(0)[:, 0:v], ACT.Relu, bias=col["b_node"][:, :],
                                         accum_out=nd_sum[:, bass.ds(g, 1)]).then_inc(n["nh_kept"], 1)
                    act.wait_ge(n["nh_kept"], g + 1)
                    nc.scalar.activation(dump[:, 0:v], nf[:, 0:v], ACT.Square, accum_out=nd_sq[:, bass.ds(g, 1)])\
                      .then_inc(n["nh_squared"], 1)

                def root_and_features(g):
                    group_before(copy_result, g)
                    root(g)
                    group_before(keep_sources, g)
                    keep(g)
                    group_before(node_features, g)

                def norm_features(g):
                    wait(act, n["mixed"], g)
                    nc.scalar.activation(fx, node_feat[:, bass.ds(g * GC, GC)], ACT.Identity, bias=t_nd[:, :], scale=s_nd[:, :])\
                      .then_inc(n["copied"], 1)

                if kind == SOFT:
                    over_groups(act, copy_turned, root_and_features, late=True)
                    for step in (copy_result, keep_sources, node_features):
                        step(NG - 1)
                elif kind == MESSAGE:
                    over_groups(act, norm_features, root_and_keep)
                elif p == 4:
                    over_groups(act, copy_turned, exp_and_keep)
                else:
                    over_groups(act, copy_turned, root_and_keep)

        @block.vector
        def _(dve):
            v = nc.vector
            chain = Chain(dve, dve_step)

            def every(t, g):
                return of_group(t, g).unsqueeze(2).to_broadcast([P, GT, F])

            def by_feature(r):
                return r[:, :].unsqueeze(1).to_broadcast([P, GT, F])

            dve.wait_ge(cols_landed, 32)
            v.tensor_tensor(starts[:, :], seq_int, before_int, ALU.not_equal).then_inc(starts_made, 1)
            chain.do(v.tensor_scalar(bits, seq_int, 7, None, ALU.arith_shift_right))
            chain.do(v.tensor_copy(cols_hi[:, :], bits))
            chain.do(v.tensor_scalar(bits, seq_int, P - 1, None, ALU.bitwise_and))
            chain.do(v.tensor_copy(cols_lo[:, :], bits))
            dve.wait_ge(consts_made, 2)

            def hot(i, b, number):
                wait(dve, hot_used, number - 1)
                at = bass.ds(i * 2 * HC + b * HC, HC)
                v.tensor_tensor(hot_hi[:, b, :, :], cols_hi[:, at].unsqueeze(1).to_broadcast([P, NT, HC]),
                                iota_hi[:, :, :], ALU.is_equal)
                v.tensor_tensor(hot_lo[:, b, :, :], cols_lo[:, at].unsqueeze(1).to_broadcast([P, P, HC]),
                                iota_lo[:, :, :], ALU.is_equal).then_inc(hot_made, 1)

            for b in range(2):
                hot(0, b, b)
            with dve.Fori(1, HI) as i:
                for b in range(2):
                    hot(i, b, 2 * i + b)
            dve.wait_ge(x_landed, 32)
            v.tensor_scalar(h_sb, x_sb[:, :, :], 0.0, MSG_EPS, ALU.max, ALU.add).then_inc(relu_made, 1)
            dve.wait_ge(seq_landed, 32)
            v.tensor_tensor(flag8[:, 0, :], seq_now, seq_before, ALU.is_equal).then_inc(flag_made, 1)
            dve.wait_ge(flag_made, 1)
            v.tensor_scalar(flag8[:, 1, :], flag8[:, 0, :], 2.0, -1.0, ALU.mult, ALU.add).then_inc(flag_made, 1)
            for t in (ef_sum, ef_sq, mg_sum, mg_sq):
                v.memset(t[:, :], 0.0)
            dve.wait_ge(attr_in_landed, 32)
            chain.do(v.tensor_copy(w_part[0][:, :], w_edge[:, :]))
            chain.do(v.tensor_tensor(w_rest[:, :], w_edge[:, :], w_part[0][:, :], ALU.subtract))
            chain.do(v.tensor_copy(w_part[1][:, :], w_rest[:, :]))
            chain.do(v.tensor_tensor(w_rest[:, :], w_rest[:, :], w_part[1][:, :], ALU.subtract))
            v.tensor_copy(w_part[2][:, :], w_rest[:, :]).then_inc(w_split, 1)
            dve.wait_ge(ranks_summed, 1)
            for b in range(CB):
                m = min(P, CN - b * P)
                v.tensor_copy(rank8[0:m, b, :], ps[0:m, 4 + b // 4, (b % 4) * P:(b % 4 + 1) * P])
            for h in range(2):
                chain.do(v.tensor_copy(started[:, h * CN // 2:(h + 1) * CN // 2], bank(2 + h, 1, CN // 2)))
            now = running[:, :]
            chain.do(v.tensor_tensor_scan(out=now, data0=started, data1=started, initial=0.0, op0=ALU.add, op1=ALU.bypass))
            chain.do(v.tensor_tensor(now, now, started, ALU.subtract))
            chain.do(v.tensor_tensor(now, now, starts[0:1, :], ALU.add))
            chain.do(v.tensor_scalar(now, now, -1.0, None, ALU.add))
            v.tensor_copy(first_rank[:, :], now).then_inc(ranks_made, 1)
            dve.wait_ge(deg_counted, 1)
            chain.do(v.tensor_copy(deg[:, :], bank(0, P, NT)))
            v.tensor_scalar(has[:, :], deg[:, :], 1.0, None, ALU.min).then_inc(deg_made, 1)
            dve.wait_ge(deg_made, 1)
            chain.do(v.tensor_scalar(rdeg[:, :], deg[:, :], 1.0, None, ALU.max))
            chain.do(v.reciprocal(rdeg[:, :], rdeg[:, :]))
            chain.do(v.tensor_tensor(rdeg[:, :], rdeg[:, :], has[:, :], ALU.mult))
            dve.wait_ge(prefix_summed, 1)
            chain.do(v.tensor_copy(total[:, :], bank(2, P, NT)))
            chain.do(v.tensor_tensor_scan(out=below[:, :], data0=total[:, :], data1=total[:, :], initial=0.0,
                                          op0=ALU.add, op1=ALU.bypass))
            chain.do(v.tensor_tensor(below[:, :], below[:, :], total[:, :], ALU.subtract))
            chain.do(v.tensor_tensor(end_f[:, :], below[:, :], bank(1, P, NT), ALU.add))
            chain.do(v.tensor_scalar(end_f[:, :], end_f[:, :], -1.0, 0.0, ALU.add, ALU.max))
            chain.do(v.tensor_copy(end_i[:, :], end_f[:, :]))
            chain.do(v.tensor_scalar(end_j[:, :], end_i[:, :], P - 1, CH // 2, ALU.bitwise_and, ALU.logical_shift_left))
            chain.do(v.tensor_scalar(end_row[:, :], end_i[:, :], 7, CH - 1, ALU.logical_shift_right, ALU.bitwise_and))
            chain.do(v.tensor_tensor(end_j[:, :], end_j[:, :], end_row[:, :], ALU.bitwise_or))
            chain.do(v.tensor_scalar(end_i[:, :], end_i[:, :], 9, 9, ALU.logical_shift_right, ALU.logical_shift_left))
            chain.do(v.tensor_tensor(end_row[:, :], end_i[:, :], end_j[:, :], ALU.bitwise_or))
            chain.do(v.tensor_copy(total[:, :], bank(4, P, NT)))
            chain.do(v.tensor_tensor_scan(out=below[:, :], data0=total[:, :], data1=total[:, :], initial=0.0,
                                          op0=ALU.add, op1=ALU.bypass))
            chain.do(v.tensor_copy(all_with[:, :], below[:, NT - 1:NT]))
            chain.do(v.tensor_tensor(below[:, :], below[:, :], total[:, :], ALU.subtract))
            chain.do(v.tensor_tensor(end_f[:, :], below[:, :], bank(3, P, NT), ALU.add))
            chain.do(v.tensor_tensor(end_f[:, :], end_f[:, :], has[:, :], ALU.subtract))
            chain.do(v.tensor_tensor(others[:, :], node_number[:, :], end_f[:, :], ALU.subtract))
            chain.do(v.tensor_scalar(others[:, :], others[:, :], all_with[:, :], None, ALU.add))
            chain.do(v.tensor_tensor(end_f[:, :], end_f[:, :], others[:, :], ALU.subtract))
            chain.do(v.tensor_tensor(end_f[:, :], end_f[:, :], has[:, :], ALU.mult))
            chain.do(v.tensor_tensor(end_f[:, :], end_f[:, :], others[:, :], ALU.add))
            v.tensor_copy(dst_row[:, :], end_f[:, :]).then_inc(index_made, 1)
            dve.wait_ge(index_made, 1)
            dve.wait_ge(setup_stored, 16 * SETUP_STORES)

            def norm_coefs(number, total, squares, count, g, beta, s, t):
                chain.do(v.reduce_sum(mu[:, :], total, axis=X))
                chain.do(v.reduce_sum(var[:, :], squares, axis=X))
                chain.do(v.tensor_scalar(mu[:, :], mu[:, :], 1.0 / count, None, ALU.mult))
                chain.do(v.tensor_tensor(tmp[:, :], mu[:, :], mu[:, :], ALU.mult))
                chain.do(v.scalar_tensor_tensor(var[:, :], var[:, :], 1.0 / count, tmp[:, :], ALU.mult, ALU.subtract))
                v.tensor_scalar(var[:, :], var[:, :], 0.0, None, ALU.max).then_inc(coef_var_made, 1)
                dve.wait_ge(coef_rooted, number)
                chain.do(v.reciprocal(var[:, :], var[:, :]))
                chain.do(v.tensor_tensor(s[:, :], g[:, :], var[:, :], ALU.mult))
                chain.do(v.tensor_tensor(tmp[:, :], s[:, :], mu[:, :], ALU.mult))
                chain.do(v.tensor_tensor(t[:, :], beta[:, :], tmp[:, :], ALU.subtract))

            for p, kind in enumerate(PASSES):
                e, n, before = edge[p], node[p], tiles_before(p)

                wait_for_tables(dve, p)

                def start_from_zero():
                    at = RING * TE - 1
                    chain.do(v.memset(sum_ring[:, at:at + 1], 0.0))
                    if kind == SOFT:
                        chain.do(v.memset(num_ring[:, at:at + 1], 0.0))
                        chain.do(v.memset(max_ring[:, 0:1], 0.0))

                def last_of(r, s):
                    at = s * TE - 1 if s else RING * TE - 1
                    return r[:, at:at + 1]

                def slot(r, s):
                    return r[:, s * TE:(s + 1) * TE]

                def place(u, s):
                    t = u * RING + s
                    wait(dve, ranks_landed[s // 2], (u + 1) * 16)
                    wait(dve, e["turned"], t - 1)
                    v.tensor_scalar(rank_hot[:, s % 2, :], ranks[:, s, :], iota_p[:, :], None, ALU.is_equal)\
                     .then_inc(e["placed"], 1)

                def scan(u, s):
                    t = u * RING + s
                    wait(dve, e["relued"] if kind == MESSAGE else e["turned"], t + 1, before)
                    wait(dve, flags_landed[s // 2], (p * EI + u + 1) * 16)
                    wait(dve, e["back"], t - RING + 1, before)
                    wait(dve, e["summed"], t, before)
                    v.tensor_tensor_scan(out=slot(sum_ring, s), data0=flags[:, s, :],
                                         data1=msg_ring[:, s, :] if kind == MESSAGE else bank(s % 2, F),
                                         initial=last_of(sum_ring, s), op0=ALU.mult, op1=ALU.add).then_inc(e["summed"], 1)

                def running_max(u, s):
                    t, b = u * RING + s, s % 2
                    wait(dve, e["turned"], t + 1)
                    wait(dve, flags_landed[s // 2], (p * EI + u + 1) * 16)
                    if s == 0 and not (isinstance(u, int) and u == 0):
                        v.tensor_copy(max_ring[:, 0:1], max_ring[:, RING * TE:RING * TE + 1]).then_inc(e["wrapped"], 1)
                        dve.wait_ge(e["wrapped"], u)
                    now = max_ring[:, 1 + s * TE:1 + (s + 1) * TE]
                    v.tensor_tensor_scan(out=now, data0=flags[:, s, :], data1=bank(b, F),
                                         initial=max_ring[:, s * TE:s * TE + 1], op0=ALU.mult, op1=ALU.max)\
                     .then_inc(e["maxed"], 1)
                    dve.wait_ge(e["maxed"], 2 * t + 1)
                    v.scalar_tensor_tensor(decay[:, b, :], flags[:, s, :], BIG, max_ring[:, s * TE:(s + 1) * TE],
                                           ALU.mult, ALU.min).then_inc(e["maxed"], 1)
                    dve.wait_ge(e["maxed"], 2 * t + 2)
                    v.tensor_tensor(decay[:, b, :], decay[:, b, :], now, ALU.subtract)
                    v.tensor_tensor(weight[:, b, :], bank(b, F), now, ALU.subtract).then_inc(e["scored"], 1)

                def soft_scan(u, s):
                    t, b = u * RING + s, s % 2
                    dve.wait_ge(e["expd"], t + 1)
                    v.tensor_tensor(weighted[:, b, :], weight[:, b, :], bank(b, F), ALU.mult).then_inc(e["weighed"], 1)
                    wait(dve, e["back"], t - RING + 1, before)
                    wait(dve, e["summed"], t, before)
                    v.tensor_tensor_scan(out=slot(sum_ring, s), data0=decay[:, b, :], data1=weight[:, b, :],
                                         initial=last_of(sum_ring, s), op0=ALU.mult, op1=ALU.add)
                    dve.wait_ge(e["weighed"], t + 1)
                    v.tensor_tensor_scan(out=slot(num_ring, s), data0=decay[:, b, :], data1=weighted[:, b, :],
                                         initial=last_of(num_ring, s), op0=ALU.mult, op1=ALU.add).then_inc(e["summed"], 1)

                if kind == MESSAGE:
                    dve.wait_ge(edge[0]["squared"], ET)
                    norm_coefs(1, ef_sum[:, :], ef_sq[:, :], n_edges, col["g_edge"], col["beta_edge"], s_ef, t_ef)
                    v.tensor_scalar(w_ef_scaled[:, :], W["W_ef"][:, :], s_ef[:, :], None, ALU.mult).then_inc(ef_coefs_made, 1)
                    dve.wait_ge(node[0]["nh_squared"], NG)
                    norm_coefs(2, nd_sum[:, :], nd_sq[:, :], n_nodes, col["g_node"], col["beta_node"], s_nd, t_nd)
                    dve.wait_ge(ef_bias_summed, 1)
                    v.tensor_tensor(msg_bias[:, :], bank(2, F, 1), col["b_msg"][:, :], ALU.add).then_inc(msg_bias_made, 1)

                start_from_zero()
                if kind == SOFT:
                    over_tiles(dve, running_max, soft_scan)
                elif kind == MESSAGE:
                    over_tiles(dve, place, scan)
                else:
                    over_tiles(dve, nothing, scan)

                if kind == MESSAGE:
                    dve.wait_ge(e["squared"], ET)
                    norm_coefs(3, mg_sum[:, :], mg_sq[:, :], n_edges, col["g_msg"], col["beta_msg"], s_mg, t_mg)
                    v.tensor_scalar(diag_s[:, :], ident[0:F, 0:F], s_mg[:, :], None, ALU.mult)
                    v.tensor_scalar(diag_t[:, :], ident[0:F, 0:F], t_mg[:, :], None, ALU.mult).then_inc(diags_made, 1)
                    dve.wait_ge(rows_spread, 1)
                    chain.do(v.tensor_copy(s_row[:, :], bank(2, P, F)))
                    chain.do(v.tensor_copy(t_row[:, :], bank(3, P, F)))

                mixed = node_major(4)[:, 0:GT, 0:F]
                if kind != MESSAGE:
                    chain.do(v.memset(fa[F:F + 1, :], 1.0))

                def result_free(g):
                    if p < len(PASSES) - 1:
                        wait(dve, n["kept"], g)
                    if kind == SOFT:
                        wait(dve, n["turned2"], g)
                    else:
                        wait(dve, n["stored"], g * 16)

                def layer_norm(g):
                    chain.do(v.reduce_sum(mean[:, :], res, axis=X))
                    chain.do(v.tensor_scalar(mean[:, :], mean[:, :], 1.0 / F, None, ALU.mult))
                    chain.do(v.tensor_tensor(res, res, mean[:, :].unsqueeze(2).to_broadcast([P, GT, F]), ALU.subtract))
                    chain.do(v.tensor_tensor(sq, res, res, ALU.mult))
                    v.reduce_sum(rstd[:, :], sq, axis=X).then_inc(var_summed, 1)
                    dve.wait_ge(rooted, norms_before(p) + g + 1)
                    chain.do(v.reciprocal(rstd[:, :], rstd[:, :]))
                    result_free(g)
                    v.tensor_tensor(ng, res, rstd[:, :].unsqueeze(2).to_broadcast([P, GT, F]), ALU.mult)\
                     .then_inc(n["normed"], 1)

                def soft_prepare(g):
                    dve.wait_ge(ends_ready, p * NG + g + 1)
                    e_g = ends[:, bass.ds(g * GT, GT), :]
                    sum_g, num_g = e_g[:, :, 0:F], e_g[:, :, F:2 * F]
                    chain.do(v.reciprocal(sum_g, sum_g))
                    chain.do(v.tensor_tensor(num_g, num_g, sum_g, ALU.mult))
                    chain.do(v.tensor_tensor(num_g, num_g, every(has, g), ALU.mult))
                    wait(dve, n["turned"], g)
                    v.tensor_tensor(grp, num_g, of_group(x_sb, g), ALU.add).then_inc(n["prepared"], 1)

                def prepare(g):
                    dve.wait_ge(ends_ready, p * NG + g + 1)
                    wait(dve, n["turned"], 2 * g)
                    v.tensor_tensor(grp, ends[:, bass.ds(g * GT, GT), 0:F], every(rdeg, g), ALU.mult)\
                     .then_inc(n["prepared"], 1)

                def add_and_norm(g):
                    dve.wait_ge(n["mixed"], g + 1)
                    wait(dve, n["normed"], g)
                    v.tensor_tensor(res, mixed, of_group(x_sb, g), ALU.add).then_inc(n["taken"], 1)
                    dve.wait_ge(n["taken"], g + 1)
                    layer_norm(g)

                def keep_destinations(g):
                    dve.wait_ge(n["dst_made"], g + 1)
                    wait(dve, n["dst_stored"], g * 16 * GT)
                    v.tensor_copy(dg, node_major(6)[:, 0:GT, 0:F]).then_inc(n["dst_kept"], 1)

                def relu(g):
                    dve.wait_ge(n["mixed"], g + 1)
                    result_free(g)
                    v.tensor_scalar(ng, mixed, 0.0, None, ALU.max).then_inc(n["normed"], 1)

                def elu(g):
                    dve.wait_ge(n["mixed"], g + 1)
                    wait(dve, n["normed"], g)
                    v.tensor_scalar(sq, mixed, 0.0, None, ALU.min).then_inc(n["floored"], 1)
                    v.tensor_scalar(res, mixed, 0.0, None, ALU.max).then_inc(n["taken"], 1)
                    dve.wait_ge(n["taken"], g + 1)
                    dve.wait_ge(n["expd"], g + 1)
                    result_free(g)
                    v.scalar_tensor_tensor(ng, sq, -1.0, res, ALU.add, ALU.add).then_inc(n["normed"], 1)

                def join(g):
                    dve.wait_ge(ends_ready, p * NG + g + 1)
                    wait(dve, n["normed"], g)
                    chain.do(v.tensor_tensor(res, ends[:, bass.ds(g * GT, GT), 0:F], every(has, g), ALU.mult))
                    chain.do(v.tensor_tensor(res, res, by_feature(s_row), ALU.mult))
                    chain.do(v.tensor_tensor(sq, every(deg, g), by_feature(t_row), ALU.mult))
                    chain.do(v.tensor_tensor(res, res, sq, ALU.add))
                    chain.do(v.tensor_tensor(res, res, of_group(x_sb, g), ALU.add))
                    dve.wait_ge(n["mixed"], g + 1)
                    v.tensor_tensor(res, res, mixed, ALU.add).then_inc(n["taken"], 1)
                    dve.wait_ge(n["taken"], g + 1)
                    layer_norm(g)

                if kind == SOFT:
                    over_groups(dve, soft_prepare, add_and_norm, keep_destinations, chain, 3 + 5)
                elif kind == MESSAGE:
                    over_groups(dve, nothing, join, None, chain, 5 + 5)
                elif p == 2:
                    over_groups(dve, prepare, relu, None, chain, 0)
                elif p == 4:
                    over_groups(dve, prepare, elu, None, chain, 0)
                else:
                    over_groups(dve, prepare, add_and_norm, None, chain, 5)


def kernel(**inputs):
    import concourse.bacc as bacc
    from concourse.bass_utils import run_bass_kernel_spmd

    a = {k: np.asarray(v) for k, v in inputs.items()}
    n_edges, ep = a["src"].shape[0], edge_tiles(a["src"].shape[0]) * TE

    def padded(v, fill):
        return np.concatenate([v, np.full((ep - n_edges,), fill, v.dtype)])

    def by_pair(v):
        return np.ascontiguousarray(v.reshape(-1, 2 * CH, P).transpose(0, 2, 1))

    w_msg = a["L1_gnn_W_msg"]
    matrices = [a["L0_gnn_W"], a["L1_gnn_W_node"], w_msg[0:F], w_msg[F:2 * F], w_msg[2 * F:3 * F]]
    matrices += [a[n].T for n in ("L2_gnn_Wl1", "L2_gnn_Wr1", "L2_gnn_Wl2", "L2_gnn_Wr2",
                                  "L3_gnn_W1l", "L3_gnn_W1r", "L3_gnn_W2l", "L3_gnn_W2r")]
    rows = [a[n] for n in ("L0_gnn_b", "L2_gnn_bl1", "L2_gnn_bl2", "L3_gnn_b1", "L3_gnn_b2")]
    columns = [a["L1_gnn_" + n] for n in COLUMNS]
    dst_sequence = np.concatenate([np.full((1,), -1, a["dst"].dtype), padded(a["dst"], -1)])
    arrays = {
        "x_dram": a["x"],
        "src_dram": by_pair(padded(a["src"], 0)),
        "dst_columns_dram": np.ascontiguousarray(dst_sequence[1:].reshape(-1, P).T),
        "dst_before_dram": np.ascontiguousarray(dst_sequence[:-1].reshape(-1, P).T),
        "dst_sequence_dram": dst_sequence,
        "attr_dram": np.ascontiguousarray(np.concatenate(
            [a["edge_attr_4"], np.zeros((ep - n_edges, EDGE_DIM), a["edge_attr_4"].dtype)]).T).reshape(-1),
        "w_edge_dram": np.tile(a["L1_gnn_W_edge"], (PARTS * PARTS, 1)),
        "matrices_dram": np.stack(matrices),
        "rows_dram": np.stack(rows),
        "columns_dram": np.stack(columns)[:, :, None],
    }
    nc = bacc.Bacc("TRN2", target_bir_lowering=False, num_devices=1)
    args = [nc.dram_tensor(n, v.shape, mybir.dt.from_np(v.dtype), kind="ExternalInput").ap() for n, v in arrays.items()]
    out = nc.dram_tensor("out_dram", a["x"].shape, mybir.dt.float32, kind="ExternalOutput").ap()
    build(nc, n_edges, *args, out)
    return run_bass_kernel_spmd(nc, [arrays], core_ids=[0]).results[0]["out_dram"]
```
